# Optimizing a Trainium2 kernel written in Bass

```python
import numpy as np
import jax
import jax.numpy as jnp

def _softmax(x, axis=-1):
    return jax.nn.softmax(x, axis=axis)

def _gelu(x):
    return jax.nn.gelu(x, approximate=True)

def _silu(x):
    return jax.nn.silu(x)

def _sigmoid(x):
    return jax.nn.sigmoid(x)

def _layernorm(x, axis=-1, eps=1e-05):
    m = jnp.mean(x, axis=axis, keepdims=True)
    v = jnp.var(x, axis=axis, keepdims=True)
    return (x - m) / jnp.sqrt(v + eps)

def _scatter_add(tgt, idx, src, axis=0):
    return tgt.at[idx].add(src)

def _segment_sum(src, seg, n):
    return jax.ops.segment_sum(src, seg, n)
kernel_name = 'mk_recurrent_d4_jaxref_r8_9314bc'

def setup_inputs(seed: int=0):
    np.random.seed(seed)
    _w = jnp.asarray

    def _L0_attn_setup():
        import jax, jax.numpy as jnp
        import numpy as np
        D_MODEL = 128
        N_HEADS = 16
        ORDER = 6
        P2 = 2 * ORDER - 1
        EPS_CLAMP = 1e-06
        EPS_DEN = 1e-07

        def _beta_np():
            j = np.arange(ORDER, dtype=np.float32)
            alpha = (j + 1.0) ** (-1.5)
            tail = np.flip(np.cumsum(np.flip(alpha)))
            beta = np.concatenate([np.zeros(1, np.float32), tail[1:].astype(np.float32), np.zeros(ORDER - 1, np.float32)])
            return beta / beta.sum()

        def _cheb(x):
            T = [jnp.ones_like(x), x]
            for _ in range(2, P2):
                T.append(2.0 * x * T[-1] - T[-2])
            return jnp.stack(T, axis=3)
        key = jax.random.key(seed)
        k1, k2, k3 = jax.random.split(key, 3)
        B, S, D = (2, 128, D_MODEL)
        x = jax.random.normal(k1, (B, S, D), dtype=jnp.float32)
        W_in = jax.random.normal(k2, (3 * D, D), dtype=jnp.float32) * 0.02
        W_out = jax.random.normal(k3, (D, D), dtype=jnp.float32) * 0.02
        return {'x': x, 'W_in': W_in, 'W_out': W_out}
    _L0_attn_in = _L0_attn_setup()

    def _L0_ffn_setup():
        import jax, jax.numpy as jnp
        import numpy as np
        B, S, D, F, E = (4, 256, 128, 512, 8)
        key = jax.random.key(seed)
        ks = jax.random.split(key, 7)
        s1 = 1.0 / np.sqrt(D)
        s2 = 1.0 / np.sqrt(F)
        x = jax.random.normal(ks[0], (B, S, D), dtype=jnp.float32)
        W1 = jax.random.uniform(ks[1], (E, D, F), jnp.float32, -s1, s1)
        b1 = jax.random.uniform(ks[2], (E, F), jnp.float32, -s1, s1)
        W2 = jax.random.uniform(ks[3], (E, F, D), jnp.float32, -s2, s2)
        b2 = jax.random.uniform(ks[4], (E, D), jnp.float32, -s2, s2)
        Wr = jax.random.uniform(ks[5], (D, E), jnp.float32, -s1, s1)
        br = jax.random.uniform(ks[6], (E,), jnp.float32, -s1, s1)
        return {'x': x, 'W1': W1, 'b1': b1, 'W2': W2, 'b2': b2, 'Wr': Wr, 'br': br}
    _L0_ffn_in = _L0_ffn_setup()

    def _L1_attn_setup():
        import jax, jax.numpy as jnp
        import numpy as np
        DIM = 128
        EXPAND = 2
        INNER = DIM * EXPAND
        B = 4
        S = 256
        EPS = 1e-06

        def _linear_params(key, fan_in, fan_out):
            kw, kb = jax.random.split(key)
            bound = 1.0 / np.sqrt(fan_in)
            w = jax.random.uniform(kw, (fan_out, fan_in), jnp.float32, -bound, bound)
            b = jax.random.uniform(kb, (fan_out,), jnp.float32, -bound, bound)
            return (w, b)
        key = jax.random.key(seed)
        ks = jax.random.split(key, 8)
        x = jax.random.normal(ks[0], (B, S, DIM), jnp.float32)
        in_w, in_b = _linear_params(ks[1], DIM, INNER)
        gate_w, gate_b = _linear_params(ks[2], DIM, INNER)
        b_w, b_b = _linear_params(ks[3], INNER, INNER)
        c_w, c_b = _linear_params(ks[4], INNER, INNER)
        d_w, d_b = _linear_params(ks[5], INNER, INNER)
        out_w, out_b = _linear_params(ks[6], INNER, DIM)
        a_log = jnp.zeros((INNER,), jnp.float32)
        norm_w = jnp.ones((DIM,), jnp.float32)
        return {'x': x, 'norm_w': norm_w, 'in_w': in_w, 'in_b': in_b, 'gate_w': gate_w, 'gate_b': gate_b, 'b_w': b_w, 'b_b': b_b, 'c_w': c_w, 'c_b': c_b, 'd_w': d_w, 'd_b': d_b, 'out_w': out_w, 'out_b': out_b, 'a_log': a_log}
    _L1_attn_in = _L1_attn_setup()

    def _L1_ffn_setup():
        import jax, jax.numpy as jnp
        import numpy as np
        B, T, DIM = (4, 128, 128)
        H, E, DH, K = (8, 5, 64, 3)

        def _topk_mask(s, k):
            idx = jax.lax.top_k(s, k)[1]
            return jnp.sum(jax.nn.one_hot(idx, s.shape[-1], dtype=s.dtype), axis=-2)
        key = jax.random.key(seed)
        ks = jax.random.split(key, 6)
        w = lambda k, shape: jax.random.normal(k, shape, jnp.float32) * 0.02
        return {'x': jax.random.normal(ks[0], (B, T, DIM), jnp.float32), 'Wq': w(ks[1], (DIM, H * E * DH)), 'Wkv': w(ks[2], (DIM, 2 * H * E * DH)), 'Ws': w(ks[3], (DIM, H * E)), 'Wd': w(ks[4], (DIM, H * E)), 'Wo': w(ks[5], (DH, E * DIM))}
    _L1_ffn_in = _L1_ffn_setup()

    def _L2_attn_setup():
        import jax, jax.numpy as jnp
        import numpy as np
        N_HEAD = 16
        D_K = 64
        D_V = 64
        EMBED = 128
        BATCH = 4
        SEQ = 256
        key = jax.random.key(seed)
        ks = jax.random.split(key, 12)
        s = lambda d: 1.0 / np.sqrt(d)
        u = lambda k, shape, d: jax.random.uniform(k, shape, jnp.float32, -s(d), s(d))
        return {'z': jax.random.normal(ks[0], (BATCH, SEQ, EMBED), jnp.float32), 'wq': u(ks[1], (EMBED, D_K), D_K), 'wk': u(ks[2], (EMBED, D_K), D_K), 'wv': u(ks[3], (EMBED, D_V), D_V), 'fcq_w': u(ks[4], (D_K, N_HEAD * D_K), D_K), 'fcq_b': u(ks[5], (N_HEAD * D_K,), N_HEAD * D_K), 'fck_w': u(ks[6], (D_K, N_HEAD * D_K), D_K), 'fck_b': u(ks[7], (N_HEAD * D_K,), N_HEAD * D_K), 'fcv_w': u(ks[8], (D_V, N_HEAD * D_V), D_V), 'fcv_b': u(ks[9], (N_HEAD * D_V,), N_HEAD * D_V), 'fco_w': u(ks[10], (N_HEAD * D_V, EMBED), EMBED), 'fco_b': u(ks[11], (EMBED,), EMBED)}
    _L2_attn_in = _L2_attn_setup()

    def _L2_ffn_setup():
        import jax, jax.numpy as jnp
        import numpy as np
        E = 8
        D = 128
        H = 256
        TOP_K = 2
        key = jax.random.key(seed)
        k_x, k_g, k_w1, k_w2 = jax.random.split(key, 4)
        B, S = (4, 256)
        inp = {'input': jax.random.normal(k_x, (B, S, D), dtype=jnp.float32), 'Wg': jax.random.normal(k_g, (D, E), dtype=jnp.float32) * 0.02, 'W1': jax.random.normal(k_w1, (E, D, H), dtype=jnp.float32) * 0.02, 'b1': jnp.zeros((E, H), dtype=jnp.float32), 'W2': jax.random.normal(k_w2, (E, H, D), dtype=jnp.float32) * 0.02, 'b2': jnp.zeros((E, D), dtype=jnp.float32)}
        return inp
    _L2_ffn_in = _L2_ffn_setup()

    def _L3_attn_setup():
        import jax, jax.numpy as jnp
        import numpy as np
        from jax.scipy.linalg import solve_triangular
        B, L, D, H = (1, 256, 128, 4)
        DK = DV = D // H
        CONV = 4
        FIR_S, FIR_M, FIR_L = (3, 15, 63)
        CHUNK = 32

        def _l2norm(x):
            return x * jax.lax.rsqrt(jnp.sum(x * x, -1, keepdims=True) + 1e-06)

        def _short_conv(x, w):
            K = w.shape[-1]
            l = x.shape[1]
            xp = jnp.pad(x, ((0, 0), (K - 1, 0), (0, 0)))
            y = sum((xp[:, j:j + l, :] * w[:, j] for j in range(K)))
            return jax.nn.silu(y)

        def _fir(x, filt):
            b, l, h, d = x.shape
            K = filt.shape[-1]
            xf = jnp.transpose(x.reshape(b, l, h * d), (0, 2, 1))
            y = jax.lax.conv_general_dilated(xf, filt.reshape(h * d, 1, K), (1,), [(K - 1, 0)], feature_group_count=h * d)
            return jnp.transpose(y, (0, 2, 1)).reshape(b, l, h, d)

        def _delta_rule_chunkwise(q, k, v, beta):
            b, h, Lq, dk = q.shape
            c = CHUNK
            n = Lq // c
            q = _l2norm(q)
            k = _l2norm(k)
            v = v * beta[..., None]
            kb = k * beta[..., None]
            rs = lambda t: t.reshape(b, h, n, c, t.shape[-1])
            qc, kc, vc, kbc = (rs(q), rs(k), rs(v), rs(kb))
            tri_strict = jnp.tril(jnp.ones((c, c), bool), -1)
            A = jnp.where(tri_strict, -(kbc @ jnp.swapaxes(kc, -1, -2)), 0.0)
            eye = jnp.eye(c, dtype=q.dtype)
            M = eye - A
            T = solve_triangular(M, jnp.broadcast_to(eye, M.shape), lower=True)
            u = T @ vc
            w = T @ kbc
            causal = jnp.tril(jnp.ones((c, c), bool))

            def step(S, inp):
                q_i, k_i, u_i, w_i = inp
                attn = jnp.where(causal, q_i @ jnp.swapaxes(k_i, -1, -2), 0.0)
                u_adj = u_i - w_i @ S
                o_i = q_i @ S + attn @ u_adj
                return (S + jnp.swapaxes(k_i, -1, -2) @ u_adj, o_i)
            S0 = jnp.zeros((b, h, dk, v.shape[-1]), q.dtype)
            mv = lambda t: jnp.moveaxis(t, 2, 0)
            _, o = jax.lax.scan(step, S0, (mv(qc), mv(kc), mv(u), mv(w)))
            return jnp.moveaxis(o, 0, 2).reshape(b, h, Lq, -1)

        def _rmsnorm(x, w, eps=1e-05):
            return x * jax.lax.rsqrt(jnp.mean(x * x, -1, keepdims=True) + eps) * w
        key = jax.random.key(seed)
        ks = jax.random.split(key, 16)
        wn = lambda k, shape, s: jax.random.normal(k, shape, jnp.float32) * s

        def fir_init(k, K):
            f = jnp.zeros((H, DV, K), jnp.float32).at[..., -1].set(1.0)
            return f + wn(k, (H, DV, K), 0.01)
        return {'hidden_states': jax.random.normal(ks[0], (B, L, D), jnp.float32), 'Wq': wn(ks[1], (D, D), 0.02), 'Wk': wn(ks[2], (D, D), 0.02), 'Wv': wn(ks[3], (D, D), 0.02), 'Wb': wn(ks[4], (H, D), 0.02), 'conv_q': wn(ks[5], (D, CONV), 0.1), 'conv_k': wn(ks[6], (D, CONV), 0.1), 'conv_v': wn(ks[7], (D, CONV), 0.1), 'fir_s': fir_init(ks[8], FIR_S), 'fir_m': fir_init(ks[9], FIR_M), 'fir_l': fir_init(ks[10], FIR_L), 'gate_w': wn(ks[11], (H, 5, D), 1.0 / np.sqrt(D)), 'gate_b': jnp.zeros((H, 5), jnp.float32), 'log_temp': jnp.zeros((H, 1), jnp.float32), 'eps_param': jnp.full((H, 1), 0.02, jnp.float32), 'norm_w': jnp.ones((DV,), jnp.float32), 'Wo': wn(ks[12], (D, D), 0.02)}
    _L3_attn_in = _L3_attn_setup()

    def _L3_ffn_setup():
        import math
        import jax, jax.numpy as jnp
        import numpy as np
        B, T, H = (4, 256, 128)
        E, K, F = (8, 2, 256)
        CAP_FACTOR = 1.25

        def _moe_forward(x, Wg, W_in, W_out):
            b, t, h = x.shape
            xf = x.reshape(-1, h)
            S = xf.shape[0]
            C = int(math.ceil(K * S / E * CAP_FACTOR))
            logits = xf @ Wg
            probs = jax.nn.softmax(logits, axis=-1)
            top_vals, top_idx = jax.lax.top_k(probs, K)
            flat_idx = top_idx.T.reshape(-1)
            onehot = jax.nn.one_hot(flat_idx, E, dtype=jnp.int32)
            cum = jnp.cumsum(onehot, axis=0) - 1
            loc = jnp.take_along_axis(cum, flat_idx[:, None], axis=1)[:, 0]
            loc = loc.reshape(K, S).T
            keep = loc < C
            gates = top_vals * keep.astype(top_vals.dtype)
            denom = jnp.maximum(gates.sum(-1, keepdims=True), 1e-09)
            gates = gates / denom
            loc_c = jnp.where(keep, loc, C)
            e_flat = top_idx.reshape(-1)
            l_flat = loc_c.reshape(-1)
            xk = jnp.broadcast_to(xf[:, None, :], (S, K, h)).reshape(-1, h)
            xk = jnp.where(keep.reshape(-1, 1), xk, 0.0)
            buf = jnp.zeros((E, C + 1, h), x.dtype).at[e_flat, l_flat].set(xk)
            inp = buf[:, :C]
            hid = jnp.einsum('ech,ehf->ecf', inp, W_in)
            a, g = jnp.split(hid, 2, axis=-1)
            hid = jax.nn.gelu(a, approximate=False) * g
            out_e = jnp.einsum('ecf,efh->ech', hid, W_out)
            out_pad = jnp.concatenate([out_e, jnp.zeros((E, 1, h), out_e.dtype)], axis=1)
            gathered = out_pad[e_flat, l_flat].reshape(S, K, h)
            y = (gathered * gates[..., None]).sum(axis=1)
            return y.reshape(b, t, h)
        key = jax.random.key(seed)
        k1, k2, k3, k4 = jax.random.split(key, 4)
        x = jax.random.normal(k1, (B, T, H), dtype=jnp.float32)
        Wg = jax.random.normal(k2, (H, E), dtype=jnp.float32) * 0.02
        W_in = jax.random.normal(k3, (E, H, 2 * F), dtype=jnp.float32) * (1.0 / math.sqrt(H))
        W_out = jax.random.normal(k4, (E, F, H), dtype=jnp.float32) * (1.0 / math.sqrt(F))
        return {'x': x, 'Wg': Wg, 'W_in': W_in, 'W_out': W_out}
    _L3_ffn_in = _L3_ffn_setup()
    _d = {'L0_attn_x': _L0_attn_in['x'], 'L0_attn_W_in': _L0_attn_in['W_in'], 'L0_attn_W_out': _L0_attn_in['W_out'], 'L0_ffn_W1': _L0_ffn_in['W1'], 'L0_ffn_b1': _L0_ffn_in['b1'], 'L0_ffn_W2': _L0_ffn_in['W2'], 'L0_ffn_b2': _L0_ffn_in['b2'], 'L0_ffn_Wr': _L0_ffn_in['Wr'], 'L0_ffn_br': _L0_ffn_in['br'], 'L1_attn_norm_w': _L1_attn_in['norm_w'], 'L1_attn_in_w': _L1_attn_in['in_w'], 'L1_attn_in_b': _L1_attn_in['in_b'], 'L1_attn_gate_w': _L1_attn_in['gate_w'], 'L1_attn_gate_b': _L1_attn_in['gate_b'], 'L1_attn_b_w': _L1_attn_in['b_w'], 'L1_attn_b_b': _L1_attn_in['b_b'], 'L1_attn_c_w': _L1_attn_in['c_w'], 'L1_attn_c_b': _L1_attn_in['c_b'], 'L1_attn_d_w': _L1_attn_in['d_w'], 'L1_attn_d_b': _L1_attn_in['d_b'], 'L1_attn_out_w': _L1_attn_in['out_w'], 'L1_attn_out_b': _L1_attn_in['out_b'], 'L1_attn_a_log': _L1_attn_in['a_log'], 'L1_ffn_Wq': _L1_ffn_in['Wq'], 'L1_ffn_Wkv': _L1_ffn_in['Wkv'], 'L1_ffn_Ws': _L1_ffn_in['Ws'], 'L1_ffn_Wd': _L1_ffn_in['Wd'], 'L1_ffn_Wo': _L1_ffn_in['Wo'], 'L2_attn_wq': _L2_attn_in['wq'], 'L2_attn_wk': _L2_attn_in['wk'], 'L2_attn_wv': _L2_attn_in['wv'], 'L2_attn_fcq_w': _L2_attn_in['fcq_w'], 'L2_attn_fcq_b': _L2_attn_in['fcq_b'], 'L2_attn_fck_w': _L2_attn_in['fck_w'], 'L2_attn_fck_b': _L2_attn_in['fck_b'], 'L2_attn_fcv_w': _L2_attn_in['fcv_w'], 'L2_attn_fcv_b': _L2_attn_in['fcv_b'], 'L2_attn_fco_w': _L2_attn_in['fco_w'], 'L2_attn_fco_b': _L2_attn_in['fco_b'], 'L2_ffn_Wg': _L2_ffn_in['Wg'], 'L2_ffn_W1': _L2_ffn_in['W1'], 'L2_ffn_b1': _L2_ffn_in['b1'], 'L2_ffn_W2': _L2_ffn_in['W2'], 'L2_ffn_b2': _L2_ffn_in['b2'], 'L3_attn_Wq': _L3_attn_in['Wq'], 'L3_attn_Wk': _L3_attn_in['Wk'], 'L3_attn_Wv': _L3_attn_in['Wv'], 'L3_attn_Wb': _L3_attn_in['Wb'], 'L3_attn_conv_q': _L3_attn_in['conv_q'], 'L3_attn_conv_k': _L3_attn_in['conv_k'], 'L3_attn_conv_v': _L3_attn_in['conv_v'], 'L3_attn_fir_s': _L3_attn_in['fir_s'], 'L3_attn_fir_m': _L3_attn_in['fir_m'], 'L3_attn_fir_l': _L3_attn_in['fir_l'], 'L3_attn_gate_w': _L3_attn_in['gate_w'], 'L3_attn_gate_b': _L3_attn_in['gate_b'], 'L3_attn_log_temp': _L3_attn_in['log_temp'], 'L3_attn_eps_param': _L3_attn_in['eps_param'], 'L3_attn_norm_w': _L3_attn_in['norm_w'], 'L3_attn_Wo': _L3_attn_in['Wo'], 'L3_ffn_Wg': _L3_ffn_in['Wg'], 'L3_ffn_W_in': _L3_ffn_in['W_in'], 'L3_ffn_W_out': _L3_ffn_in['W_out']}
    _x0 = _d['L0_attn_x']
    _d['L0_attn_x'] = jax.random.normal(jax.random.fold_in(jax.random.key(seed), 1), (16, 256, 128), dtype=_x0.dtype)
    del _x0
    return _d

def reference(L0_attn_x, L0_attn_W_in, L0_attn_W_out, L0_ffn_W1, L0_ffn_b1, L0_ffn_W2, L0_ffn_b2, L0_ffn_Wr, L0_ffn_br, L1_attn_norm_w, L1_attn_in_w, L1_attn_in_b, L1_attn_gate_w, L1_attn_gate_b, L1_attn_b_w, L1_attn_b_b, L1_attn_c_w, L1_attn_c_b, L1_attn_d_w, L1_attn_d_b, L1_attn_out_w, L1_attn_out_b, L1_attn_a_log, L1_ffn_Wq, L1_ffn_Wkv, L1_ffn_Ws, L1_ffn_Wd, L1_ffn_Wo, L2_attn_wq, L2_attn_wk, L2_attn_wv, L2_attn_fcq_w, L2_attn_fcq_b, L2_attn_fck_w, L2_attn_fck_b, L2_attn_fcv_w, L2_attn_fcv_b, L2_attn_fco_w, L2_attn_fco_b, L2_ffn_Wg, L2_ffn_W1, L2_ffn_b1, L2_ffn_W2, L2_ffn_b2, L3_attn_Wq, L3_attn_Wk, L3_attn_Wv, L3_attn_Wb, L3_attn_conv_q, L3_attn_conv_k, L3_attn_conv_v, L3_attn_fir_s, L3_attn_fir_m, L3_attn_fir_l, L3_attn_gate_w, L3_attn_gate_b, L3_attn_log_temp, L3_attn_eps_param, L3_attn_norm_w, L3_attn_Wo, L3_ffn_Wg, L3_ffn_W_in, L3_ffn_W_out):

    def _L0_attn_ref(x, W_in, W_out):
        import jax, jax.numpy as jnp
        import numpy as np
        D_MODEL = 128
        N_HEADS = 16
        ORDER = 6
        P2 = 2 * ORDER - 1
        EPS_CLAMP = 1e-06
        EPS_DEN = 1e-07

        def _beta_np():
            j = np.arange(ORDER, dtype=np.float32)
            alpha = (j + 1.0) ** (-1.5)
            tail = np.flip(np.cumsum(np.flip(alpha)))
            beta = np.concatenate([np.zeros(1, np.float32), tail[1:].astype(np.float32), np.zeros(ORDER - 1, np.float32)])
            return beta / beta.sum()

        def _cheb(x):
            T = [jnp.ones_like(x), x]
            for _ in range(2, P2):
                T.append(2.0 * x * T[-1] - T[-2])
            return jnp.stack(T, axis=3)
        B, S, D = x.shape
        H, Dh = (N_HEADS, D // N_HEADS)
        qkv = jnp.einsum('bsd,ed->bse', x, W_in)
        q, k, v = jnp.split(qkv, 3, axis=-1)
        q = q.reshape(B, S, H, Dh).transpose(0, 2, 1, 3)
        k = k.reshape(B, S, H, Dh).transpose(0, 2, 1, 3)
        v = v.reshape(B, S, H, Dh).transpose(0, 2, 1, 3)
        inv_sqrt_d = 1.0 / jnp.sqrt(jnp.float32(Dh))
        xq = jnp.clip(q * inv_sqrt_d, -1.0 + EPS_CLAMP, 1.0 - EPS_CLAMP)
        xk = jnp.clip(k * inv_sqrt_d, -1.0 + EPS_CLAMP, 1.0 - EPS_CLAMP)
        Tq = _cheb(xq)
        Tk = _cheb(xk)
        beta = jnp.asarray(_beta_np())
        Tv = Tk * v[:, :, :, None, :]
        kv_prefix = jnp.cumsum(Tv, axis=2)
        ks_prefix = jnp.cumsum(Tk.sum(axis=-1), axis=2)
        kv_beta = kv_prefix * beta[None, None, None, :, None]
        k_beta = ks_prefix * beta[None, None, None, :]
        num = (Tq * kv_beta).sum(axis=3)
        den = (Tq.sum(axis=-1) * k_beta).sum(axis=3)
        out_h = num / (den[..., None] + EPS_DEN)
        out = out_h.transpose(0, 2, 1, 3).reshape(B, S, H * Dh)
        return jnp.einsum('bsd,ed->bse', out, W_out)

    def _L0_ffn_ref(x, W1, b1, W2, b2, Wr, br):
        import jax, jax.numpy as jnp
        import numpy as np
        B, S, D, F, E = (4, 256, 128, 512, 8)
        b, s, d = x.shape
        e = Wr.shape[1]
        logits = x @ Wr + br
        idx = jnp.argmax(logits, axis=-1)
        probs = jax.nn.softmax(logits, axis=-1)
        gates = jnp.take_along_axis(probs, idx[..., None], axis=-1)[..., 0]
        xf = x.reshape(-1, d)
        idxf = idx.reshape(-1)
        gf = gates.reshape(-1)
        out = jnp.zeros_like(xf)
        for ei in range(e):
            h = jax.nn.gelu(xf @ W1[ei] + b1[ei], approximate=False)
            y = h @ W2[ei] + b2[ei]
            mask = (idxf == ei).astype(xf.dtype)
            out = out + y * (gf * mask)[:, None]
        return out.reshape(b, s, d)

    def _L1_attn_ref(x, norm_w, in_w, in_b, gate_w, gate_b, b_w, b_b, c_w, c_b, d_w, d_b, out_w, out_b, a_log):
        import jax, jax.numpy as jnp
        import numpy as np
        DIM = 128
        EXPAND = 2
        INNER = DIM * EXPAND
        B = 4
        S = 256
        EPS = 1e-06

        def _linear_params(key, fan_in, fan_out):
            kw, kb = jax.random.split(key)
            bound = 1.0 / np.sqrt(fan_in)
            w = jax.random.uniform(kw, (fan_out, fan_in), jnp.float32, -bound, bound)
            b = jax.random.uniform(kb, (fan_out,), jnp.float32, -bound, bound)
            return (w, b)
        residual = x
        xn = x * jax.lax.rsqrt(jnp.mean(x * x, axis=-1, keepdims=True) + EPS) * norm_w
        u = jnp.einsum('bsd,id->bsi', xn, in_w) + in_b
        g = jax.nn.sigmoid(jnp.einsum('bsd,id->bsi', xn, gate_w) + gate_b)
        u = u * g
        b = jnp.einsum('bsi,ji->bsj', u, b_w) + b_b
        c = jnp.einsum('bsi,ji->bsj', u, c_w) + c_b
        d = jnp.einsum('bsi,ji->bsj', u, d_w) + d_b
        a = jnp.exp(-jax.nn.softplus(a_log))

        def step(h, b_t):
            h = a * h + b_t
            return (h, h)
        h0 = jnp.zeros((x.shape[0], b.shape[-1]), x.dtype)
        _, hs = jax.lax.scan(step, h0, jnp.swapaxes(b, 0, 1))
        hs = jnp.swapaxes(hs, 0, 1)
        y = c * hs + d
        y = jnp.einsum('bsi,di->bsd', y, out_w) + out_b
        return residual + y

    def _L1_ffn_ref(x, Wq, Wkv, Ws, Wd, Wo):
        import jax, jax.numpy as jnp
        import numpy as np
        B, T, DIM = (4, 128, 128)
        H, E, DH, K = (8, 5, 64, 3)

        def _topk_mask(s, k):
            idx = jax.lax.top_k(s, k)[1]
            return jnp.sum(jax.nn.one_hot(idx, s.shape[-1], dtype=s.dtype), axis=-2)
        b, t, _ = x.shape
        scale = DH ** (-0.5)
        ss = jax.nn.sigmoid(x @ Ws).reshape(b, t, H, E)
        sd = jax.nn.sigmoid(x @ Wd).reshape(b, t, H, E)
        ms = _topk_mask(ss, K)
        md = _topk_mask(sd, K)
        ss_g = ss * ms
        sd_g = sd * md
        q5 = (x @ Wq).reshape(b, t, H, E, DH)
        kv = (x @ Wkv).reshape(b, t, 2, H, E, DH)
        k5, v5 = (kv[:, :, 0], kv[:, :, 1])
        q = jnp.einsum('bthed,bthe->bhtd', q5, sd_g)
        k = jnp.einsum('bthed,bthe->bhtd', k5, ss_g)
        v = jnp.einsum('bthed,bthe->bhtd', v5, ss_g)
        attn = jax.nn.softmax(jnp.einsum('bhid,bhjd->bhij', q * scale, k), axis=-1)
        out = jnp.einsum('bhij,bhjd->bihd', attn, v)
        o5 = jnp.einsum('bthd,dm->bthm', out, Wo).reshape(b, t, H, E, DIM)
        return jnp.einsum('bthem,bthe->btm', o5, md)

    def _L2_attn_ref(z, wq, wk, wv, fcq_w, fcq_b, fck_w, fck_b, fcv_w, fcv_b, fco_w, fco_b):
        import jax, jax.numpy as jnp
        import numpy as np
        N_HEAD = 16
        D_K = 64
        D_V = 64
        EMBED = 128
        BATCH = 4
        SEQ = 256
        b, n, _ = z.shape
        scale = jnp.sqrt(jnp.float32(D_K))
        q = z @ wq @ fcq_w + fcq_b
        k = z @ wk @ fck_w + fck_b
        v = z @ wv @ fcv_w + fcv_b
        q = q.reshape(b, n, N_HEAD, D_K)
        k = k.reshape(b, n, N_HEAD, D_K)
        v = v.reshape(b, n, N_HEAD, D_V)
        scores = jnp.einsum('bihd,bjhd->bhij', q, k) / scale
        attn = jax.nn.softmax(scores, axis=-1)
        out = jnp.einsum('bhij,bjhd->bihd', attn, v)
        out = out.reshape(b, n, N_HEAD * D_V)
        return out @ fco_w + fco_b

    def _L2_ffn_ref(input, Wg, W1, b1, W2, b2):
        import jax, jax.numpy as jnp
        import numpy as np
        E = 8
        D = 128
        H = 256
        TOP_K = 2
        logits = jnp.einsum('bsd,de->bse', input, Wg)
        probs = jax.nn.softmax(logits, axis=-1)
        top_vals, top_idx = jax.lax.top_k(probs, TOP_K)
        top_vals = top_vals / jnp.sum(top_vals, axis=-1, keepdims=True)
        onehot = jax.nn.one_hot(top_idx, E, dtype=input.dtype)
        mask = jnp.sum(onehot, axis=2)
        scores = jnp.sum(onehot * top_vals[..., None], axis=2)
        xm = input[None] * jnp.moveaxis(mask, -1, 0)[..., None]
        h = jnp.einsum('ebsd,edh->ebsh', xm, W1) + b1[:, None, None, :]
        h = jax.nn.relu(h)
        y = jnp.einsum('ebsh,ehd->ebsd', h, W2) + b2[:, None, None, :]
        out = jnp.sum(y * jnp.moveaxis(scores, -1, 0)[..., None], axis=0)
        return out

    def _L3_attn_ref(hidden_states, Wq, Wk, Wv, Wb, conv_q, conv_k, conv_v, fir_s, fir_m, fir_l, gate_w, gate_b, log_temp, eps_param, norm_w, Wo):
        import jax, jax.numpy as jnp
        import numpy as np
        from jax.scipy.linalg import solve_triangular
        B, L, D, H = (1, 256, 128, 4)
        DK = DV = D // H
        CONV = 4
        FIR_S, FIR_M, FIR_L = (3, 15, 63)
        CHUNK = 32

        def _l2norm(x):
            return x * jax.lax.rsqrt(jnp.sum(x * x, -1, keepdims=True) + 1e-06)

        def _short_conv(x, w):
            K = w.shape[-1]
            l = x.shape[1]
            xp = jnp.pad(x, ((0, 0), (K - 1, 0), (0, 0)))
            y = sum((xp[:, j:j + l, :] * w[:, j] for j in range(K)))
            return jax.nn.silu(y)

        def _fir(x, filt):
            b, l, h, d = x.shape
            K = filt.shape[-1]
            xf = jnp.transpose(x.reshape(b, l, h * d), (0, 2, 1))
            y = jax.lax.conv_general_dilated(xf, filt.reshape(h * d, 1, K), (1,), [(K - 1, 0)], feature_group_count=h * d)
            return jnp.transpose(y, (0, 2, 1)).reshape(b, l, h, d)

        def _delta_rule_chunkwise(q, k, v, beta):
            b, h, Lq, dk = q.shape
            c = CHUNK
            n = Lq // c
            q = _l2norm(q)
            k = _l2norm(k)
            v = v * beta[..., None]
            kb = k * beta[..., None]
            rs = lambda t: t.reshape(b, h, n, c, t.shape[-1])
            qc, kc, vc, kbc = (rs(q), rs(k), rs(v), rs(kb))
            tri_strict = jnp.tril(jnp.ones((c, c), bool), -1)
            A = jnp.where(tri_strict, -(kbc @ jnp.swapaxes(kc, -1, -2)), 0.0)
            eye = jnp.eye(c, dtype=q.dtype)
            M = eye - A
            T = solve_triangular(M, jnp.broadcast_to(eye, M.shape), lower=True)
            u = T @ vc
            w = T @ kbc
            causal = jnp.tril(jnp.ones((c, c), bool))

            def step(S, inp):
                q_i, k_i, u_i, w_i = inp
                attn = jnp.where(causal, q_i @ jnp.swapaxes(k_i, -1, -2), 0.0)
                u_adj = u_i - w_i @ S
                o_i = q_i @ S + attn @ u_adj
                return (S + jnp.swapaxes(k_i, -1, -2) @ u_adj, o_i)
            S0 = jnp.zeros((b, h, dk, v.shape[-1]), q.dtype)
            mv = lambda t: jnp.moveaxis(t, 2, 0)
            _, o = jax.lax.scan(step, S0, (mv(qc), mv(kc), mv(u), mv(w)))
            return jnp.moveaxis(o, 0, 2).reshape(b, h, Lq, -1)

        def _rmsnorm(x, w, eps=1e-05):
            return x * jax.lax.rsqrt(jnp.mean(x * x, -1, keepdims=True) + eps) * w
        b, l, d = hidden_states.shape
        q = _short_conv(hidden_states @ Wq.T, conv_q).reshape(b, l, H, DK)
        k = _short_conv(hidden_states @ Wk.T, conv_k).reshape(b, l, H, DK)
        v_direct = _short_conv(hidden_states @ Wv.T, conv_v).reshape(b, l, H, DV)
        beta = jax.nn.sigmoid(hidden_states @ Wb.T)
        tp = lambda t: jnp.transpose(t, (0, 2, 1, 3))
        delta_out = tp(_delta_rule_chunkwise(tp(q), tp(k), tp(v_direct), jnp.transpose(beta, (0, 2, 1))))
        local_s = _fir(v_direct, fir_s)
        local_m = _fir(v_direct, fir_m)
        local_l = _fir(v_direct, fir_l)
        logits = jnp.einsum('bld,hpd->blhp', hidden_states, gate_w) + gate_b
        temp = jnp.exp(log_temp).reshape(1, 1, H, 1)
        probs = jax.nn.softmax(logits / temp, -1)
        eps = jnp.clip(eps_param, 0.0, 0.2).reshape(1, 1, H, 1)
        probs = probs * (1.0 - 5.0 * eps) + eps
        o = probs[..., 0:1] * local_s + probs[..., 1:2] * local_m + probs[..., 2:3] * local_l + probs[..., 3:4] * delta_out + probs[..., 4:5] * v_direct
        o = _rmsnorm(o, norm_w)
        return o.reshape(b, l, H * DV) @ Wo.T

    def _L3_ffn_ref(x, Wg, W_in, W_out):
        import math
        import jax, jax.numpy as jnp
        import numpy as np
        B, T, H = (4, 256, 128)
        E, K, F = (8, 2, 256)
        CAP_FACTOR = 1.25

        def _moe_forward(x, Wg, W_in, W_out):
            b, t, h = x.shape
            xf = x.reshape(-1, h)
            S = xf.shape[0]
            C = int(math.ceil(K * S / E * CAP_FACTOR))
            logits = xf @ Wg
            probs = jax.nn.softmax(logits, axis=-1)
            top_vals, top_idx = jax.lax.top_k(probs, K)
            flat_idx = top_idx.T.reshape(-1)
            onehot = jax.nn.one_hot(flat_idx, E, dtype=jnp.int32)
            cum = jnp.cumsum(onehot, axis=0) - 1
            loc = jnp.take_along_axis(cum, flat_idx[:, None], axis=1)[:, 0]
            loc = loc.reshape(K, S).T
            keep = loc < C
            gates = top_vals * keep.astype(top_vals.dtype)
            denom = jnp.maximum(gates.sum(-1, keepdims=True), 1e-09)
            gates = gates / denom
            loc_c = jnp.where(keep, loc, C)
            e_flat = top_idx.reshape(-1)
            l_flat = loc_c.reshape(-1)
            xk = jnp.broadcast_to(xf[:, None, :], (S, K, h)).reshape(-1, h)
            xk = jnp.where(keep.reshape(-1, 1), xk, 0.0)
            buf = jnp.zeros((E, C + 1, h), x.dtype).at[e_flat, l_flat].set(xk)
            inp = buf[:, :C]
            hid = jnp.einsum('ech,ehf->ecf', inp, W_in)
            a, g = jnp.split(hid, 2, axis=-1)
            hid = jax.nn.gelu(a, approximate=False) * g
            out_e = jnp.einsum('ecf,efh->ech', hid, W_out)
            out_pad = jnp.concatenate([out_e, jnp.zeros((E, 1, h), out_e.dtype)], axis=1)
            gathered = out_pad[e_flat, l_flat].reshape(S, K, h)
            y = (gathered * gates[..., None]).sum(axis=1)
            return y.reshape(b, t, h)
        return _moe_forward(x, Wg, W_in, W_out)
    x = L0_attn_x
    xn = _layernorm(x, axis=-1)
    s = _L0_attn_ref(xn, L0_attn_W_in, L0_attn_W_out)
    g = _silu(_L0_ffn_ref(xn, L0_ffn_W1, L0_ffn_b1, L0_ffn_W2, L0_ffn_b2, L0_ffn_Wr, L0_ffn_br))
    x = x + s * g
    xn = _layernorm(x, axis=-1)
    s = _L1_attn_ref(xn, L1_attn_norm_w, L1_attn_in_w, L1_attn_in_b, L1_attn_gate_w, L1_attn_gate_b, L1_attn_b_w, L1_attn_b_b, L1_attn_c_w, L1_attn_c_b, L1_attn_d_w, L1_attn_d_b, L1_attn_out_w, L1_attn_out_b, L1_attn_a_log)
    g = _silu(_L1_ffn_ref(xn, L1_ffn_Wq, L1_ffn_Wkv, L1_ffn_Ws, L1_ffn_Wd, L1_ffn_Wo))
    x = x + s * g
    xn = _layernorm(x, axis=-1)
    s = _L2_attn_ref(xn, L2_attn_wq, L2_attn_wk, L2_attn_wv, L2_attn_fcq_w, L2_attn_fcq_b, L2_attn_fck_w, L2_attn_fck_b, L2_attn_fcv_w, L2_attn_fcv_b, L2_attn_fco_w, L2_attn_fco_b)
    g = _silu(_L2_ffn_ref(xn, L2_ffn_Wg, L2_ffn_W1, L2_ffn_b1, L2_ffn_W2, L2_ffn_b2))
    x = x + s * g
    xn = _layernorm(x, axis=-1)
    s = _L3_attn_ref(xn, L3_attn_Wq, L3_attn_Wk, L3_attn_Wv, L3_attn_Wb, L3_attn_conv_q, L3_attn_conv_k, L3_attn_conv_v, L3_attn_fir_s, L3_attn_fir_m, L3_attn_fir_l, L3_attn_gate_w, L3_attn_gate_b, L3_attn_log_temp, L3_attn_eps_param, L3_attn_norm_w, L3_attn_Wo)
    g = _silu(_L3_ffn_ref(xn, L3_ffn_Wg, L3_ffn_W_in, L3_ffn_W_out))
    x = x + s * g
    return x

_drawn_inputs = setup_inputs


def setup_inputs(seed=0):
    import zlib

    import numpy as np

    out = dict(_drawn_inputs(seed))
    spreads = {'L1_attn_norm_w': (1.0, 0.2),
     'L1_attn_a_log': (0.0, 0.1),
     'L2_ffn_b1': (0.0, 0.1),
     'L2_ffn_b2': (0.0, 0.1),
     'L3_attn_gate_b': (0.0, 0.1),
     'L3_attn_log_temp': (0.0, 0.1),
     'L3_attn_eps_param': (0.019999999552965164, 0.2),
     'L3_attn_norm_w': (1.0, 0.2)}
    factors = {}
    for name, (base, spread) in spreads.items():
        noise = np.random.default_rng([zlib.crc32(name.encode()), seed]).standard_normal(out[name].shape)
        drawn = base * np.exp(spread * noise) if base else spread * noise
        out[name] = jnp.asarray(drawn.astype(out[name].dtype))
    for name, factor in factors.items():
        out[name] = (out[name] * factor).astype(out[name].dtype)
    return out
```

```python
import numpy as np
import concourse.bass as bass
from concourse import mybir
from contextlib import ExitStack

F32 = mybir.dt.float32
ALU = mybir.AluOpType
ACT = mybir.ActivationFunctionType
AX = mybir.AxisListType

P = 128
BATCH, SEQ = 16, 256
TOKENS = BATCH * SEQ
GW = 512
GROUPS = TOKENS // GW
BPG = GW // SEQ
TPG = GW // P
TILES = TOKENS // P
EXPERTS = 8


class Engine:

    def __init__(self, name, ctx, nc):
        self.name, self.ctx, self.nc = name, ctx, nc
        self.queue, self.seen = [], {}
        self.sem, self.count = None, 0

    def phase(self, label):
        self.sem = self.ctx.enter_context(self.nc.semaphore(f"{self.name}_{label}"))
        self.count = 0

    def wait(self, after):
        for token in flat(after):
            sem, value = token
            if self.seen.get(id(sem), 0) < value:
                self.seen[id(sem)] = value
                self.queue.append(lambda eng, s=sem, v=value: eng.wait_ge(s, v))

    def run(self, emit, after=(), signal=True):
        self.wait(after)
        if not signal:
            self.queue.append(emit)
            return None
        self.count += 1
        sem = self.sem
        self.queue.append(lambda eng: emit(eng).then_inc(sem, 1))
        return (sem, self.count)

    def play(self, eng):
        for item in self.queue:
            item(eng)


def flat(after):
    if after is None:
        return []
    if isinstance(after, tuple) and len(after) == 2 and isinstance(after[1], int):
        return [after]
    return [t for a in after for t in flat(a)]


class Slot:
    def __init__(self, tensor, index):
        self.tensor, self.index, self.after = tensor, index, []

    def __getitem__(self, key):
        return self.tensor[key]


class Pool:

    def __init__(self, slots):
        self.free = list(slots)

    def take(self):
        assert self.free, "no buffer is free here"
        return self.free.pop(0)

    def put(self, slot, readers):
        slot.after = flat(readers)
        self.free.append(slot)


def interleave(*streams):
    live = list(streams)
    while live:
        for item in list(live):
            gen, turns = item
            for _ in range(turns):
                if next(gen, "end") == "end":
                    live.remove(item)
                    break


class Kernel:
    def __init__(self, nc, ins, out):
        self.nc, self.ins, self.out = nc, ins, out
        self.ctx = ExitStack()
        self.V = Engine("vector", self.ctx, nc)
        self.A = Engine("scalar", self.ctx, nc)
        self.G = Engine("gpsimd", self.ctx, nc)
        self.T = Engine("tensor", self.ctx, nc)
        self.D = Engine("sync", self.ctx, nc)
        self.stores = []

    def sb(self, name, shape, dt=F32):
        return self.ctx.enter_context(self.nc.sbuf_tensor(name, shape, dt))

    def phase(self, label):
        for e in (self.V, self.A, self.G, self.T):
            e.phase(label)

    def load(self, name, pairs, after=()):
        sem = self.ctx.enter_context(self.nc.semaphore(f"load_{name}"))
        self.D.wait(after)
        for dst, src in pairs:
            self.D.queue.append(lambda eng, d=dst, s=src: eng.dma_start(d, s).then_inc(sem, 16))
        return (sem, 16 * len(pairs))

    def mm(self, products, after=(), start=True, stop=True):
        self.T.wait(after)
        token = None
        n = len(products)
        for i, (o, l, r) in enumerate(products):
            token = self.T.run(lambda eng, o=o, l=l, r=r, a=(start and i == 0), z=(stop and i == n - 1):
                               eng.matmul(o, l, r, start=a, stop=z, skip_group_check=True),
                               signal=(i == n - 1))
        return token

    def mms(self, products, after=()):
        self.T.wait(after)
        token = None
        for i, (o, l, r) in enumerate(products):
            token = self.T.run(lambda eng, o=o, l=l, r=r: eng.matmul(o, l, r, start=True, stop=True,
                                                                     skip_group_check=True),
                               signal=(i == len(products) - 1))
        return token

    def turn(self, pairs, after=()):
        self.T.wait(after)
        token = None
        for i, (o, a) in enumerate(pairs):
            k = a.shape[0]
            token = self.T.run(lambda eng, o=o, a=a, k=k: eng.transpose(o, a, self.ident[0:k, 0:k]),
                               signal=(i == len(pairs) - 1))
        return token

    def tt(self, out, a, b, op, after=(), on=None):
        return (on or self.V).run(lambda eng: eng.tensor_tensor(out, a, b, op), after)

    def ts(self, out, a, s1, s2, op0, op1=None, after=(), on=None):
        if op1 is None:
            return (on or self.V).run(lambda eng: eng.tensor_scalar(out, a, s1, None, op0), after)
        return (on or self.V).run(lambda eng: eng.tensor_scalar(out, a, s1, s2, op0, op1), after)

    def recip(self, out, a, after=()):
        return self.V.run(lambda eng: eng.reciprocal(out, a), after)

    def stt(self, out, a, s, b, op0, op1, after=()):
        return self.V.run(lambda eng: eng.scalar_tensor_tensor(out=out, in0=a, scalar=s, in1=b, op0=op0, op1=op1), after)

    def red(self, out, a, op, after=()):
        return self.V.run(lambda eng: eng.tensor_reduce(out, a, AX.X, op), after)

    def scan(self, out, decay, add, after=()):
        return self.V.run(lambda eng: eng.tensor_tensor_scan(out, decay, add, 0.0, ALU.mult, ALU.add), after)

    def act(self, out, a, func, bias=None, scale=1.0, accum=None, after=()):
        def emit(eng):
            kw = {"scale": scale}
            if bias is not None:
                kw["bias"] = bias
            if accum is not None:
                kw["accum_out"] = accum
            return eng.activation(out, a, func, **kw)
        return self.A.run(emit, after)

    def vcopy(self, out, a, after=(), on=None):
        return (on or self.V).run(lambda eng: eng.tensor_copy(out, a), after)

    def acopy(self, out, a, after=(), scale=1.0):
        return self.act(out, a, ACT.Copy, scale=scale, after=after)

    def fill(self, out, value, after=(), on=None):
        return (on or self.G).run(lambda eng: eng.memset(out, value), after)

    def keep_where(self, ap, pattern, base, mult, op, fill, after=()):
        return self.G.run(lambda eng: eng.affine_select(out=ap, in_=ap, compare_op=op, fill=fill, base=base,
                                                        pattern=pattern, channel_multiplier=mult), after)

    def setup(self):
        self.xT = self.sb("x_channels", [P, TOKENS])
        self.xn = self.sb("normed_channels", [P, TOKENS])
        self.ident = self.sb("identity", [P, P])
        self.mean_w = self.sb("mean_weights", [P, P])
        self.eps = self.sb("eps_columns", [P, 4])
        self.sel = self.sb("select_expert", [EXPERTS, EXPERTS, P])
        self.scratch = Pool([Slot(self.sb(f"scratch{i}", [P, GW]), i) for i in range(SCRATCH)])
        self.banks = Pool([Slot(self.ctx.enter_context(self.nc.psum_tensor(f"bank{i}", [P, GW], F32)), i)
                           for i in range(8)])
        self.stats = Pool([Slot(self.sb(f"stats{i}", [P, 16]), i) for i in range(12)])
        self.phase("setup")
        t = [self.fill(self.ident[:, :], 0.0), self.fill(self.sel[:, :, :], 0.0),
             self.fill(self.mean_w[:, :], 1.0 / P)]
        for i, e in enumerate((1e-5, 1e-6, 0.0, 1.0)):
            t.append(self.fill(self.eps[:, i:i + 1], e))
        a = self.keep_where(self.ident[:, :], [[-1, P]], 0, 1, ALU.not_equal, 1.0, after=t)
        b = self.keep_where(self.sel[:, :, :], [[-1, EXPERTS], [0, P]], 0, 1, ALU.not_equal, 1.0, after=t)
        self.const = [a, b]
        for e in (self.V, self.A, self.T):
            e.wait(self.const)
        self.x_ready = [self.load(f"x{g}", [(self.cols(self.xT, g), self.ins["x"][:, g * GW:(g + 1) * GW])])
                        for g in range(GROUPS)]
        self.xn_ready = [None] * GROUPS
        self.xn_read = [[] for _ in range(GROUPS)]

    def cols(self, t, g):
        return t[:, g * GW:(g + 1) * GW]

    def layernorm(self, g):
        x, xn = self.cols(self.xT, g), self.cols(self.xn, g)
        mean, sq, var = self.banks.take(), self.scratch.take(), self.banks.take()
        t_mean = self.mm([(mean[:, :], self.mean_w[:, :], x)], after=[mean.after, self.x_ready[g]])
        yield
        t_d = self.tt(xn, x, mean[:, :], ALU.subtract, after=[t_mean, self.xn_read[g]])
        self.banks.put(mean, t_d)
        t_sq = self.act(sq[:, :], xn, ACT.Square, after=[t_d, sq.after])
        yield
        t_var = self.mm([(var[:, :], self.mean_w[:, :], sq[:, :])], after=[t_sq, var.after])
        yield
        t_sd = self.act(sq[:, :], var[:, :], ACT.Sqrt, bias=self.eps[:, 0:1], after=t_var)
        self.banks.put(var, t_sd)
        yield
        t_r = self.recip(sq[:, :], sq[:, :], after=t_sd)
        self.xn_ready[g] = self.tt(xn, xn, sq[:, :], ALU.mult, after=[t_r, t_d])
        self.scratch.put(sq, self.xn_ready[g])
        self.xn_read[g] = []
        yield

    def all_groups(self, body, width=2):
        for g in range(0, GROUPS, width):
            interleave(*[(body(h), 1) for h in range(g, g + width)])

    def one_hot_first(self, mask, score, tmp, col, weight, n, w, after):
        v3 = lambda a: a.rearrange("p (n w) -> p n w", w=w)
        b = lambda c: c.unsqueeze(2).to_broadcast([P, n, w])
        t = self.red(col, v3(score), ALU.max, after=after)
        t = self.tt(v3(tmp), v3(score), b(col), ALU.is_equal, after=t)
        t = self.tt(tmp, tmp, weight, ALU.mult, after=t)
        t = self.red(col, v3(tmp), ALU.max, after=t)
        t = self.tt(v3(mask), v3(tmp), b(col), ALU.is_equal, after=t)
        return t

    def softmax_experts(self, name, Wr, after, bias=None):
        N = TILES * EXPERTS
        bank = self.banks.take()
        t = self.mms([(bank[:, i * EXPERTS:(i + 1) * EXPERTS], self.xn[:, i * P:(i + 1) * P], Wr)
                      for i in range(TILES)], after=[bank.after, after, self.xn_ready])
        v3 = lambda a: a.rearrange("p (n w) -> p n w", w=EXPERTS)
        bc = lambda c: c.unsqueeze(2).to_broadcast([P, TILES, EXPERTS])
        lg, pr, col = self.scratch.take(), self.scratch.take(), self.scratch.take()
        l, p, c = lg[:, 0:N], pr[:, 0:N], col[:, 0:TILES]
        if bias is None:
            t = self.vcopy(l, bank[:, 0:N], after=[t, lg.after])
        else:
            t = self.tt(v3(l), v3(bank[:, 0:N]), bias.unsqueeze(1).to_broadcast([P, TILES, EXPERTS]), ALU.add,
                        after=[t, lg.after])
        self.banks.put(bank, t)
        t = self.red(c, v3(l), ALU.max, after=[t, col.after])
        t = self.tt(v3(l), v3(l), bc(c), ALU.subtract, after=t)
        t_e = self.act(p, l, ACT.Exp, after=[t, pr.after])
        t = self.red(c, v3(p), ALU.add, after=[t_e, t])
        t = self.recip(c, c, after=t)
        t = self.tt(v3(p), v3(p), bc(c), ALU.mult, after=t)
        self.scratch.put(col, t)
        return lg, pr, t

    def gates_to_rows(self, gates, gt, g, after):
        bank = self.banks.take()
        t = self.turn([(bank[0:EXPERTS, i * P:(i + 1) * P],
                        gates[:, (TPG * g + i) * EXPERTS:(TPG * g + i + 1) * EXPERTS]) for i in range(TPG)],
                      after=[bank.after, after])
        t = self.vcopy(gt[0:EXPERTS, :], bank[0:EXPERTS, :], after=[t, gt.after])
        self.banks.put(bank, t)
        return t

    def experts(self, g, gt, t_gt, acc, nf, hidden, W2, b2, after, skew=3):
        x = self.cols(self.xn, g)
        pending = []
        state = {"first": b2 is None}
        if b2 is not None:
            self.mm([(acc[:, :], b2, gt[0:EXPERTS, :])], after=[acc.after, t_gt, after], stop=False)
        total = EXPERTS * nf
        done = 0

        def flush():
            nonlocal done
            e, f, slot, t = pending.pop(0)
            tok = self.mm([(acc[:, :], W2(e, f), slot[:, :])], after=[t] + ([acc.after] if state["first"] else []),
                          start=state["first"], stop=(done == total - 1))
            state["first"] = False
            self.scratch.put(slot, tok)
            done += 1
            return tok
        for e in range(EXPERTS):
            gate = self.banks.take()
            t_gate = self.mm([(gate[:, :], self.sel[:, e, :], gt[0:EXPERTS, :])], after=[gate.after, t_gt])
            used = []
            for f in range(nf):
                slot, t = hidden(e, f, x, gate, t_gate)
                used.append(t)
                pending.append((e, f, slot, t))
                if len(pending) > skew:
                    flush()
                yield
            self.banks.put(gate, used)
        while pending:
            tok = flush()
        self.scratch.put(gt, tok)
        self.t_acc = tok
        yield

    def gate_and_add(self, g, acc, t_acc, s, silu=None):
        x = self.cols(self.xT, g)
        if silu is None:
            sl = self.scratch.take()
            t = self.act(sl[:, :], acc[:, :], ACT.Silu, after=[t_acc, sl.after])
            self.banks.put(acc, t)
        else:
            sl, t = silu, t_acc
        t = self.tt(sl[:, :], sl[:, :], s[:, :], ALU.mult, after=[t, s.token])
        self.scratch.put(s, t)
        self.x_ready[g] = self.tt(x, x, sl[:, :], ALU.add, after=t)
        self.scratch.put(sl, self.x_ready[g])
        self.xn_read[g] = [t_acc]
        if self.last_layer:
            self.D.wait(self.x_ready[g])
            sem = self.ctx.enter_context(self.nc.semaphore(f"store_group{g}"))
            self.D.queue.append(lambda eng: eng.dma_start(self.out[:, g * GW:(g + 1) * GW], x).then_inc(sem, 16))
            self.stores.append((sem, 16))

    def banks_readers(self):
        return [s.after for s in self.banks.free + self.scratch.free + self.stats.free]

    def finish(self):
        self.D.wait(self.stores)
        with self.nc.Block() as block:
            block.sync(self.D.play)
            block.vector(self.V.play)
            block.scalar(self.A.play)
            block.gpsimd(self.G.play)
            block.tensor(self.T.play)
        self.ctx.close()

LAYERS = [0,1,2,3]
SCRATCH = 38
REGION_WORDS = (10300, 12200)


L0_HEADS = 16
L0_DH = P // L0_HEADS
L0_ORDERS = (1, 2, 3, 4, 5)
L0_FF = 4


def chebyshev_weights():
    order = 6
    alpha = (np.arange(order, dtype=np.float32) + 1.0) ** (-1.5)
    tail = np.flip(np.cumsum(np.flip(alpha)))
    beta = np.concatenate([np.zeros(1, np.float32), tail[1:].astype(np.float32), np.zeros(order - 1, np.float32)])
    return beta / beta.sum()


def layer0(k, region):
    nc, ins = k.nc, k.ins
    beta = chebyshev_weights()
    assert [i for i in range(len(beta)) if beta[i] != 0] == list(L0_ORDERS)
    k.phase("L0")
    take = region.take
    W1 = take("p (e f) -> p e f", e=EXPERTS, f=512)
    W2 = take("p (e c d) -> p e c d", e=EXPERTS, c=L0_FF, d=P)
    b1 = take("p (n) -> p n", n=EXPERTS * L0_FF)
    b2 = take("p (n) -> p n", n=P)[0:EXPERTS, :]
    Wr = take("p (n) -> p n", n=EXPERTS)
    br = take("p (n) -> p n", n=EXPERTS)
    Win = take("p (n) -> p n", n=3 * P)
    Wout = take("p (n) -> p n", n=P)
    NO = len(L0_ORDERS)
    rows = NO * L0_HEADS
    head_sum = take("p (o r) -> p o r", o=NO, r=rows)
    head_back = take("p (n) -> p n", n=P)[0:rows, :]
    ones = take("p (n) -> p n", n=SEQ)
    gates = take("p (n) -> p n", n=TILES * EXPERTS)
    weight = take("p (n w) -> p n w", n=TILES, w=EXPERTS)
    small = k.load("L0_small", [(Wr, ins["L0_Wr"][:, :]), (br, ins["L0_br"][:, :].broadcast_to([P, EXPERTS])),
                                (Win, ins["L0_Win"][:, :]), (Wout, ins["L0_Wout"][:, :]), (b1, ins["L0_b1"][:, :]),
                                (b2, ins["L0_b2"][:, :])], after=region.free_after)
    big = k.load("L0_experts", [(W1[:, e, :], ins["L0_W1"][e, :, :]) for e in range(EXPERTS)] +
                 [(W2[:, e, :, :], ins["L0_W2"][e, :, :].rearrange("(c p) d -> p c d", p=P)) for e in range(EXPERTS)])
    t = [k.fill(head_sum, 0.0, after=region.free_after), k.fill(ones, 1.0)]
    const = [t[1]]
    for o in range(NO):
        v = head_sum[:, o, o * L0_HEADS:(o + 1) * L0_HEADS]
        t1 = k.fill(v, 1.0, after=t)
        t2 = k.keep_where(v, [[-L0_DH, L0_HEADS]], 0, 1, ALU.is_ge, 0.0, after=t1)
        const.append(k.keep_where(v, [[L0_DH, L0_HEADS]], L0_DH - 1, -1, ALU.is_ge, 0.0, after=t2))
    hb = head_back.rearrange("p (h d) -> p h d", d=L0_DH)
    bank, buf = k.banks.take(), k.scratch.take()
    t0 = k.ts(buf[:, 0:rows], head_sum[:, 0, :], float(beta[L0_ORDERS[0]]), None, ALU.mult, after=[const, buf.after])
    for o in range(1, NO):
        t0 = k.stt(buf[:, 0:rows], head_sum[:, o, :], float(beta[L0_ORDERS[o]]), buf[:, 0:rows], ALU.mult, ALU.add, after=t0)
    t0 = k.turn([(bank[0:rows, 0:P], buf[:, 0:rows])], after=[bank.after, t0])
    t0 = k.vcopy(head_back, bank[0:rows, 0:P], after=t0)
    k.banks.put(bank, t0)
    k.scratch.put(buf, t0)
    for e in range(EXPERTS):
        const.append(k.fill(weight[:, :, e:e + 1], float(EXPERTS - e)))
    const.append(t0)
    k.T.wait(const)
    k.V.wait(const)

    k.all_groups(k.layernorm)

    W = TILES * EXPERTS
    lg, pr, t_p = k.softmax_experts("L0", Wr, small, bias=br)
    tmp, col = k.scratch.take(), k.scratch.take()
    t = k.one_hot_first(gates, lg[:, 0:W], tmp[:, 0:W], col[:, 0:TILES], weight.rearrange("p n w -> p (n w)"),
                        TILES, EXPERTS, after=[t_p, tmp.after, col.after])
    t_gates = k.tt(gates, gates, pr[:, 0:W], ALU.mult, after=[t, t_p])
    for s in (lg, pr, tmp, col):
        k.scratch.put(s, t_gates)

    def attention(g):
        x = k.cols(k.xn, g)
        k.T.wait(small)
        xs = []
        for i in range(2):
            b, s = k.banks.take(), k.scratch.take()
            t = k.mm([(b[:, :], Win[:, i * P:(i + 1) * P], x)], after=[b.after, k.xn_ready[g]])
            t = k.act(s[:, :], b[:, :], ACT.Copy, scale=float(1.0 / np.sqrt(np.float32(L0_DH))), after=[t, s.after])
            k.banks.put(b, t)
            t = k.ts(s[:, :], s[:, :], -1.0 + 1e-6, 1.0 - 1e-6, ALU.max, ALU.min, after=t)
            xs.append((s, t))
            yield
        b, v = k.banks.take(), k.scratch.take()
        t = k.mm([(b[:, :], Win[:, 2 * P:3 * P], x)], after=b.after)
        t_v = k.acopy(v[:, :], b[:, :], after=[t, v.after])
        k.banks.put(b, t_v)
        yield
        prev, cur, dbl = [None, None], [xs[0], xs[1]], []
        for s, t in xs:
            d = k.scratch.take()
            dbl.append((d, k.ts(d[:, :], s[:, :], 2.0, None, ALU.mult, after=[t, d.after])))
        num = k.scratch.take()
        sums = [k.banks.take(), k.banks.take()]
        t_num = None
        t_sum = [None, None]
        for o in range(NO):
            if o > 0:
                for i in range(2):
                    n = k.scratch.take()
                    (cs, ct), (ds, dt) = cur[i], dbl[i]
                    t = k.tt(n[:, :], ds[:, :], cs[:, :], ALU.mult, after=[ct, dt, n.after])
                    if prev[i] is None:
                        t = k.ts(n[:, :], n[:, :], -1.0, None, ALU.add, after=t)
                    else:
                        ps, pt = prev[i]
                        t = k.tt(n[:, :], n[:, :], ps[:, :], ALU.subtract, after=[t, pt], on=k.G)
                        k.scratch.put(ps, [t, t_sum[i], t_num])
                    prev[i], cur[i] = cur[i], (n, t)
            for i in range(2):
                s, t = cur[i]
                t_sum[i] = k.mm([(sums[i][0:rows, :], head_sum[:, o, :], s[:, :])],
                                after=[t] + ([sums[i].after] if o == 0 else []), start=(o == 0), stop=(o == NO - 1))
            yield
            kv, cu = k.scratch.take(), k.scratch.take()
            t = k.tt(kv[:, :], cur[1][0][:, :], v[:, :], ALU.mult, after=[cur[1][1], t_v, kv.after])
            t_c = [k.scan(cu[:, j * SEQ:(j + 1) * SEQ], ones, kv[:, j * SEQ:(j + 1) * SEQ], after=[t, cu.after])
                   for j in range(BPG)]
            dst = num if o == 0 else kv
            t = k.stt(dst[:, :], cur[0][0][:, :], float(beta[L0_ORDERS[o]]), cu[:, :], ALU.mult, ALU.mult,
                      after=[t_c, cur[0][1]] + ([num.after] if o == 0 else []))
            t_q = t
            if o > 0:
                t = k.tt(num[:, :], num[:, :], kv[:, :], ALU.add, after=[t, t_num], on=k.G)
            k.scratch.put(kv, t)
            k.scratch.put(cu, t_q)
            t_num = t
            yield
        for i in range(2):
            for s in (prev[i][0], cur[i][0], dbl[i][0]):
                k.scratch.put(s, [t_num, t_sum[i]])
        k.scratch.put(v, t_num)
        kc, den = k.scratch.take(), k.banks.take()
        t_c = [k.scan(kc[0:rows, j * SEQ:(j + 1) * SEQ], ones[0:rows, :], sums[1][0:rows, j * SEQ:(j + 1) * SEQ],
                      after=[t_sum[1], kc.after]) for j in range(BPG)]
        t = k.tt(kc[0:rows, :], kc[0:rows, :], sums[0][0:rows, :], ALU.mult, after=[t_c, t_sum[0]])
        k.banks.put(sums[0], t)
        k.banks.put(sums[1], t)
        yield
        t = k.mm([(den[:, :], head_back, kc[0:rows, :])], after=[t, den.after])
        t = k.ts(kc[:, :], den[:, :], 1e-7, None, ALU.add, after=t)
        k.banks.put(den, t)
        t = k.recip(kc[:, :], kc[:, :], after=t)
        t = k.tt(num[:, :], num[:, :], kc[:, :], ALU.mult, after=[t, t_num])
        k.scratch.put(kc, t)
        yield
        b, s = k.banks.take(), k.scratch.take()
        t = k.mm([(b[:, :], Wout, num[:, :])], after=[t, b.after])
        s.token = k.acopy(s[:, :], b[:, :], after=[t, s.after])
        k.scratch.put(num, t)
        k.banks.put(b, s.token)
        k.mixed[g] = s
        yield

    def ffn(g):
        k.T.wait(big)
        gt = k.scratch.take()
        t_gt = k.gates_to_rows(gates, gt, g, t_gates)
        acc = k.banks.take()

        def hidden(e, f, x, gate, t_gate):
            b, s = k.banks.take(), k.scratch.take()
            t = k.mm([(b[:, :], W1[:, e, f * P:(f + 1) * P], x)], after=b.after)
            n = e * L0_FF + f
            t = k.act(s[:, :], b[:, :], ACT.Gelu, bias=b1[:, n:n + 1], after=[t, s.after, small])
            k.banks.put(b, t)
            return s, k.tt(s[:, :], s[:, :], gate[:, :], ALU.mult, after=[t, t_gate])

        yield from k.experts(g, gt, t_gt, acc, L0_FF, hidden, lambda e, f: W2[:, e, f, :], b2, after=small)
        k.gate_and_add(g, acc, k.t_acc, k.mixed[g])
        yield

    run_layer(k, attention, ffn, 1, 2)
    return k.x_ready


def run_layer(k, mix, ffn, mix_turns, ffn_turns):
    k.mixed = [None] * GROUPS
    interleave((mix(0), 1))
    for g in range(GROUPS):
        streams = [(ffn(g), ffn_turns)]
        if g + 1 < GROUPS:
            streams.append((mix(g + 1), mix_turns))
        interleave(*streams)


class Region:

    def __init__(self, tensor, words, free_after):
        self.tensor, self.words, self.free_after, self.at = tensor, words, free_after, 0

    def take(self, pattern, **sizes):
        n = int(np.prod(list(sizes.values())))
        n += -n % 8
        assert self.at + n <= self.words, ("region", self.at + n)
        ap = self.tensor[:, self.at:self.at + int(np.prod(list(sizes.values())))]
        self.at += n
        return ap if len(sizes) == 1 else ap.rearrange(pattern, **sizes)


L1_INNER = 2
L1_H, L1_E, L1_DH, L1_K = 8, 5, 64, 3
L1_ROW = L1_H * L1_DH


def top_mask(k, mask, score, tmp, pick, col, weight, n, w, count, after):
    t = after
    for r in range(count):
        t = k.one_hot_first(pick, score, tmp, col, weight, n, w, after=t)
        if r == 0:
            t_m = k.vcopy(mask, pick, after=t)
        else:
            t_m = k.tt(mask, mask, pick, ALU.add, after=[t, t_m])
        if r < count - 1:
            t = k.stt(score, pick, -4.0, score, ALU.mult, ALU.add, after=t)
        t = [t, t_m]
    return t


def attention_scores(k, q, kk, scale, after, rsum):
    bank, p, st = k.banks.take(), k.scratch.take(), k.stats.take()
    t = k.mms([(bank[:, i * SEQ:(i + 1) * SEQ], q[:, i * P:(i + 1) * P], kk) for i in range(2)],
              after=[bank.after, after])
    mx = st[:, 0:2]
    t_m = k.red(mx, bank[:, :].rearrange("p (i j) -> p i j", j=SEQ), ALU.max, after=[t, st.after])
    t_n = k.ts(mx, mx, -scale, None, ALU.mult, after=t_m)
    t_e = [k.act(p[:, i * SEQ:(i + 1) * SEQ], bank[:, i * SEQ:(i + 1) * SEQ], ACT.Exp, bias=mx[:, i:i + 1], scale=scale,
                 accum=rsum[:, i:i + 1], after=[t_n, p.after]) for i in range(2)]
    k.banks.put(bank, t_e)
    k.stats.put(st, t_e)
    return p, t_e


def turned_scores(k, p, t_p, on_vector):
    bank, pt = k.banks.take(), k.scratch.take()
    t = k.turn([(bank[:, jc * SEQ + i * P:jc * SEQ + (i + 1) * P], p[:, i * SEQ + jc * P:i * SEQ + (jc + 1) * P])
                for jc in range(2) for i in range(2)], after=[bank.after, t_p])
    k.scratch.put(p, t)
    copy = k.vcopy if on_vector else k.acopy
    t = copy(pt[:, :], bank[:, :], after=[t, pt.after])
    k.banks.put(bank, t)
    return pt, t


def layer1(k, region):
    nc, ins = k.nc, k.ins
    k.phase("L1")
    take = region.take
    Iw = take("p (n) -> p n", n=256)
    Gw = take("p (n) -> p n", n=256)
    Bw, Cw, Dw = [take("p (c n) -> p c n", c=2, n=256) for _ in range(3)]
    Ow = take("p (c n) -> p c n", c=2, n=P)
    cols = take("p (n) -> p n", n=16)
    decay = take("p (c n) -> p c n", c=2, n=SEQ)
    one = take("p (n) -> p n", n=SEQ)
    Wsd = take("p (n) -> p n", n=2 * L1_H * L1_E)
    Wx = {kind: take("p (e n) -> p e n", e=L1_E, n=L1_ROW) for kind in ("q", "k", "v")}
    Wo = take("p (c n) -> p c n", c=3, n=P)
    NR = TPG * 2 * L1_H
    weight = take("p (n w) -> p n w", n=NR, w=L1_E)
    small = k.load("L1_small", [(Iw, ins["L1_Iw"][:, :]), (Gw, ins["L1_Gw"][:, :]), (cols, ins["L1_cols"][:, :])] +
                   [(w, ins[n][:, :].rearrange("(c p) n -> p c n", p=P))
                    for w, n in ((Bw, "L1_Bw"), (Cw, "L1_Cw"), (Dw, "L1_Dw"), (Ow, "L1_Ow"))], after=region.free_after)
    big = k.load("L1_ffn", [(Wsd, ins["L1_Wsd"][:, :])] +
                 [(Wx[n], ins[f"L1_W{n}"][:, :].rearrange("p (e n) -> p e n", e=L1_E)) for n in ("q", "k", "v")] +
                 [(Wo[:, 0:2, :], ins["L1_Wo"][0:2 * P, :].rearrange("(c p) n -> p c n", p=P)),
                  (Wo[0:64, 2, :], ins["L1_Wo"][2 * P:, :])])
    const = [k.fill(one, 1.0, after=region.free_after)]
    for e in range(L1_E):
        const.append(k.fill(weight[:, :, e:e + 1], float(L1_E - e), after=region.free_after))
    in_b, gate_b, b_b, c_b, d_b, a_log = [cols[:, 2 * i:2 * i + 2] for i in range(6)]
    out_b, norm_w = cols[:, 12:13], cols[:, 13:14]
    t_a = k.act(a_log, a_log, ACT.Sigmoid, scale=-1.0, after=small)
    t_decay = [k.ts(decay[:, c, :], one, a_log[:, c:c + 1], None, ALU.mult, after=[t_a, const]) for c in range(2)]
    k.V.wait([const, t_decay, small])
    k.all_groups(k.layernorm)

    def recurrence(g):
        x = k.cols(k.xn, g)
        sq, b = k.scratch.take(), k.banks.take()
        t = k.act(sq[:, :], x, ACT.Square, after=[k.xn_ready[g], sq.after])
        t = k.mm([(b[:, :], k.mean_w[:, :], sq[:, :])], after=[t, b.after])
        t = k.act(sq[:, :], b[:, :], ACT.Sqrt, bias=k.eps[:, 1:2], after=t)
        k.banks.put(b, t)
        yield
        t = k.recip(sq[:, :], sq[:, :], after=t)
        t_r = k.stt(sq[:, :], x, norm_w, sq[:, :], ALU.mult, ALU.mult, after=[t, k.xn_ready[g]])
        xr = sq
        k.T.wait(small)
        u = []
        for c in range(2):
            s = k.scratch.take()
            bg, bu = k.banks.take(), k.banks.take()
            t_g = k.mm([(bg[:, :], Gw[:, c * P:(c + 1) * P], xr[:, :])], after=[t_r, bg.after])
            t_u = k.mm([(bu[:, :], Iw[:, c * P:(c + 1) * P], xr[:, :])], after=bu.after)
            t = k.act(s[:, :], bg[:, :], ACT.Sigmoid, bias=gate_b[:, c:c + 1], after=[t_g, s.after])
            k.banks.put(bg, t)
            t = k.stt(s[:, :], bu[:, :], in_b[:, c:c + 1], s[:, :], ALU.add, ALU.mult, after=[t_u, t])
            k.banks.put(bu, t)
            u.append((s, t))
            yield
        k.scratch.put(xr, t_u)
        ys = []
        for c in range(2):
            sl = slice(c * P, (c + 1) * P)
            bb, bc = k.banks.take(), k.banks.take()
            s, h = k.scratch.take(), k.scratch.take()
            t_b = k.mm([(bb[:, :], Bw[:, i, sl], u[i][0][:, :]) for i in range(2)], after=[u[0][1], u[1][1], bb.after])
            t_c = k.mm([(bc[:, :], Cw[:, i, sl], u[i][0][:, :]) for i in range(2)], after=bc.after)
            t = k.act(s[:, :], bb[:, :], ACT.Identity, bias=b_b[:, c:c + 1], after=[t_b, s.after])
            k.banks.put(bb, t)
            t = [k.scan(h[:, j * SEQ:(j + 1) * SEQ], decay[:, c, :], s[:, j * SEQ:(j + 1) * SEQ], after=[t, h.after])
                 for j in range(BPG)]
            t = k.stt(h[:, :], bc[:, :], c_b[:, c:c + 1], h[:, :], ALU.add, ALU.mult, after=[t, t_c])
            k.banks.put(bc, t)
            k.scratch.put(s, t)
            yield
            bd = k.banks.take()
            t_d = k.mm([(bd[:, :], Dw[:, i, sl], u[i][0][:, :]) for i in range(2)], after=bd.after)
            t = k.stt(h[:, :], bd[:, :], d_b[:, c:c + 1], h[:, :], ALU.add, ALU.add, after=[t, t_d])
            k.banks.put(bd, t)
            ys.append((h, t))
            yield
        for s, _ in u:
            k.scratch.put(s, t_d)
        b, s = k.banks.take(), k.scratch.take()
        t = k.mm([(b[:, :], Ow[:, i, :], ys[i][0][:, :]) for i in range(2)], after=[ys[0][1], ys[1][1], b.after])
        for y, _ in ys:
            k.scratch.put(y, t)
        s.token = k.stt(s[:, :], b[:, :], out_b, x, ALU.add, ALU.add, after=[t, s.after])
        k.banks.put(b, s.token)
        k.mixed[g] = s
        yield

    def gated(g):
        k.T.wait(big)
        x = k.cols(k.xn, g)
        W = 2 * L1_H * L1_E
        NW = TPG * W
        bank, sg, mk, sc, tmp, pick, col = [k.banks.take()] + [k.scratch.take() for _ in range(6)]
        t = k.mms([(bank[:, i * W:(i + 1) * W], x[:, i * P:(i + 1) * P], Wsd) for i in range(TPG)],
                  after=[bank.after, k.xn_ready[g]])
        t_s = k.act(sg[:, 0:NW], bank[:, 0:NW], ACT.Sigmoid, after=[t, sg.after])
        k.banks.put(bank, t_s)
        t = k.vcopy(sc[:, 0:NW], sg[:, 0:NW], after=[t_s, sc.after, tmp.after, pick.after, col.after, mk.after])
        t = top_mask(k, mk[:, 0:NW], sc[:, 0:NW], tmp[:, 0:NW], pick[:, 0:NW], col[:, 0:NR],
                     weight.rearrange("p n w -> p (n w)"), NR, L1_E, L1_K, after=t)
        t_g = k.tt(sg[:, 0:NW], sg[:, 0:NW], mk[:, 0:NW], ALU.mult, after=t)
        for s in (sc, tmp, pick, col):
            k.scratch.put(s, t_g)
        yield
        fo = k.scratch.take()
        fo_tokens = []
        gview = lambda s, i, which, e: s[:, 0:NW].rearrange("p (n w h e) -> p n w h e", n=TPG, w=2, h=L1_H, e=L1_E)[:, i, which, :, e].unsqueeze(2).to_broadcast([P, L1_H, L1_DH])
        heads = lambda a: a.rearrange("p (h d) -> p h d", d=L1_DH)
        for b in range(BPG):
            turned = {"q": [k.scratch.take(), k.scratch.take()], "k": [k.scratch.take(), k.scratch.take()]}
            t_turned = {"q": [], "k": []}
            vs = []
            for i in (2 * b, 2 * b + 1):
                for kind, which in (("q", 1), ("k", 0), ("v", 0)):
                    acc, t_acc = k.scratch.take(), None
                    for e in range(L1_E):
                        bank = k.banks.take()
                        t = k.mm([(bank[:, :], x[:, i * P:(i + 1) * P], Wx[kind][:, e, :])], after=bank.after)
                        dst = acc if e == 0 else k.scratch.take()
                        t = k.tt(heads(dst[:, :]), heads(bank[:, :]), gview(sg, i, which, e), ALU.mult, after=[t, t_g, dst.after])
                        k.banks.put(bank, t)
                        if e > 0:
                            t = k.tt(acc[:, :], acc[:, :], dst[:, :], ALU.add, after=[t, t_acc], on=k.G)
                            k.scratch.put(dst, t)
                        t_acc = t
                        yield
                    if kind == "v":
                        vs.append((acc, t_acc))
                    else:
                        bank = k.banks.take()
                        t = k.turn([(bank[:, m * P:(m + 1) * P], acc[:, m * P:(m + 1) * P]) for m in range(4)],
                                   after=[t_acc, bank.after])
                        k.scratch.put(acc, t)
                        for s in range(2):
                            dst = turned[kind][s]
                            t2 = k.acopy(dst[:, :].rearrange("p (m t) -> p m t", t=SEQ)[:, :, (i % 2) * P:(i % 2 + 1) * P],
                                         bank[:, s * SEQ:(s + 1) * SEQ].rearrange("p (m t) -> p m t", t=P),
                                         after=[t, dst.after])
                            t_turned[kind].append(t2)
                        k.banks.put(bank, t_turned[kind][-2:])
                        yield
            O = [k.banks.take(), k.banks.take()]
            rs = k.stats.take()
            rsv = rs[:, 0:16].rearrange("p (h i) -> p h i", i=2)
            units, t_pv, t_ps = [], None, []

            def second():
                nonlocal t_pv
                h, p, t_p = units.pop(0)
                pt, t = turned_scores(k, p, t_p, False)
                t_pv = k_pv(h, pt, t)
                k.scratch.put(pt, t_pv)

            def k_pv(h, pt, t):
                for i in range(2):
                    tok = k.mm([(O[i][:, h * L1_DH:(h + 1) * L1_DH], pt[:, jc * SEQ + i * P:jc * SEQ + (i + 1) * P],
                                 vs[jc][0][:, h * L1_DH:(h + 1) * L1_DH]) for jc in range(2)],
                               after=[t, vs[jc_last][1], vs[0][1], O[i].after])
                return tok
            jc_last = 1
            for h in range(L1_H):
                m, r = h // 2, (h % 2) * 64
                q = turned["q"][m // 2][r:r + 64, (m % 2) * SEQ:(m % 2 + 1) * SEQ]
                kk = turned["k"][m // 2][r:r + 64, (m % 2) * SEQ:(m % 2 + 1) * SEQ]
                p, t_p = attention_scores(k, q, kk, L1_DH ** -0.5, [t_turned["q"], t_turned["k"], rs.after], rsv[:, h, :])
                units.append((h, p, t_p))
                t_ps.append(t_p)
                if len(units) > 2:
                    second()
                yield
            while units:
                second()
                yield
            for kind in ("q", "k"):
                for s in turned[kind]:
                    k.scratch.put(s, t_pv)
            for v, _ in vs:
                k.scratch.put(v, t_pv)
            t_r = k.recip(rs[:, 0:16], rs[:, 0:16], after=t_ps)
            for i in range(2):
                n = 2 * b + i
                o, mixd, tmp = k.scratch.take(), k.scratch.take(), None
                t_o = k.tt(heads(o[:, :]), heads(O[i][:, :]), rsv[:, :, i].unsqueeze(2).to_broadcast([P, L1_H, L1_DH]),
                           ALU.mult, after=[t_pv, t_r, o.after])
                k.banks.put(O[i], t_o)
                ts = []
                for e in range(L1_E):
                    tmp = k.scratch.take()
                    t = k.tt(heads(tmp[:, :]), heads(o[:, :]), gview(mk, n, 1, e), ALU.mult, after=[t_o, tmp.after], on=k.G)
                    t2 = k.red(mixd[:, e * L1_DH:(e + 1) * L1_DH], tmp[:, :].rearrange("p (h d) -> p d h", d=L1_DH), ALU.add,
                               after=[t, mixd.after])
                    k.scratch.put(tmp, t2)
                    ts.append(t2)
                    yield
                k.scratch.put(o, t)
                bank, at = k.banks.take(), k.scratch.take()
                t = k.turn([(bank[0:w, c * P:(c + 1) * P], mixd[:, c * P:c * P + w]) for c, w in ((0, P), (1, P), (2, 64))],
                           after=[ts, bank.after])
                k.scratch.put(mixd, t)
                t_c = [k.acopy(at[:, 0:2 * P], bank[:, 0:2 * P], after=[t, at.after]),
                       k.acopy(at[0:64, 2 * P:3 * P], bank[0:64, 2 * P:3 * P], after=t)]
                k.banks.put(bank, t_c)
                bank = k.banks.take()
                t = k.mm([(bank[:, 0:P], Wo[0:w, c, :], at[0:w, c * P:(c + 1) * P]) for c, w in ((0, P), (1, P), (2, 64))],
                         after=[t_c, bank.after])
                k.scratch.put(at, t)
                t = k.act(fo[:, n * P:(n + 1) * P], bank[:, 0:P], ACT.Silu, after=[t, fo.after])
                k.banks.put(bank, t)
                fo_tokens.append(t)
                yield
            k.stats.put(rs, t_o)
        for s in (sg, mk):
            k.scratch.put(s, [t, t_o, fo_tokens, ts])
        k.gate_and_add(g, None, fo_tokens, k.mixed[g], silu=fo)
        yield

    run_layer(k, recurrence, gated, 1, 4)
    return k.x_ready


def layouts1(a):
    T = lambda n: a[n].T
    cols = np.concatenate([columns(a["L1_attn_" + n]) for n in
                           ("in_b", "gate_b", "b_b", "c_b", "d_b", "a_log", "out_b", "norm_w")] +
                          [np.zeros((P, 2), np.float32)], axis=1)
    H, E, DH = L1_H, L1_E, L1_DH
    by_expert = lambda w: w.reshape(P, H, E, DH).transpose(0, 2, 1, 3).reshape(P, E * H * DH)
    kv = a["L1_ffn_Wkv"].reshape(P, 2, H * E * DH)
    return {"L1_Iw": T("L1_attn_in_w"), "L1_Gw": T("L1_attn_gate_w"), "L1_Bw": T("L1_attn_b_w"),
            "L1_Cw": T("L1_attn_c_w"), "L1_Dw": T("L1_attn_d_w"), "L1_Ow": T("L1_attn_out_w"), "L1_cols": cols,
            "L1_Wsd": np.concatenate([a["L1_ffn_Ws"], a["L1_ffn_Wd"]], axis=1),
            "L1_Wq": by_expert(a["L1_ffn_Wq"]), "L1_Wk": by_expert(kv[:, 0]), "L1_Wv": by_expert(kv[:, 1]),
            "L1_Wo": a["L1_ffn_Wo"].reshape(DH, E, P).transpose(1, 0, 2).reshape(E * DH, P)}


L2_HEADS, L2_DH = 16, 64
L2_PAIRS = L2_HEADS // 2
L2_FF = 2


def top2_gates(k, gates, pr, t_p, weight, spare, both=None):
    W = TILES * EXPERTS
    v3 = lambda s: s[:, 0:W].rearrange("p (n w) -> p n w", w=EXPERTS)
    sc, tmp, m1, m2, col = spare
    t = k.vcopy(sc[:, 0:W], pr[:, 0:W], after=[t_p, [s.after for s in spare]])
    t1 = k.one_hot_first(m1[:, 0:W], sc[:, 0:W], tmp[:, 0:W], col[:, 0:TILES], weight, TILES, EXPERTS, after=t)
    t = k.stt(sc[:, 0:W], m1[:, 0:W], -4.0, sc[:, 0:W], ALU.mult, ALU.add, after=t1)
    t2 = k.one_hot_first(m2[:, 0:W], sc[:, 0:W], tmp[:, 0:W], col[:, 0:TILES], weight, TILES, EXPERTS, after=t)
    if both is not None:
        return [t1, t2]
    t = k.tt(tmp[:, 0:W], m1[:, 0:W], m2[:, 0:W], ALU.add, after=[t1, t2])
    t = k.tt(gates, tmp[:, 0:W], pr[:, 0:W], ALU.mult, after=t)
    g3 = gates.rearrange("p (n w) -> p n w", w=EXPERTS)
    t = k.red(col[:, 0:TILES], g3, ALU.add, after=t)
    t = k.recip(col[:, 0:TILES], col[:, 0:TILES], after=t)
    return k.tt(g3, g3, col[:, 0:TILES].unsqueeze(2).to_broadcast([P, TILES, EXPERTS]), ALU.mult, after=t)


def layer2(k, region):
    nc, ins = k.nc, k.ins
    k.phase("L2")
    take = region.take
    Wqk = take("p (n) -> p n", n=P)
    Wv = take("p (n) -> p n", n=L2_DH)
    Fqk = take("p (n) -> p n", n=L2_HEADS * L2_DH)
    Fv = take("p (n) -> p n", n=L2_HEADS * L2_DH)
    Fv_b = take("p (n) -> p n", n=L2_HEADS * L2_DH)
    Fo = take("p (c n) -> p c n", c=L2_PAIRS, n=P)
    cols = take("p (n) -> p n", n=2 * L2_PAIRS + 1)
    W1 = take("p (e f) -> p e f", e=EXPERTS, f=L2_FF * P)
    W2 = take("p (e c d) -> p e c d", e=EXPERTS, c=L2_FF, d=P)
    b1 = take("p (n) -> p n", n=EXPERTS * L2_FF)
    b2 = take("p (n) -> p n", n=P)[0:EXPERTS, :]
    Wg = take("p (n) -> p n", n=EXPERTS)
    gates = take("p (n) -> p n", n=TILES * EXPERTS)
    weight = take("p (n w) -> p n w", n=TILES, w=EXPERTS)
    loaded = k.load("L2", [(Wg, ins["L2_Wg"][:, :]), (Wqk, ins["L2_Wqk"][:, :]), (Wv, ins["L2_Wv"][:, :]),
                           (cols, ins["L2_cols"][:, :]), (Fqk, ins["L2_Fqk"][:, :]), (Fv[0:L2_DH, :], ins["L2_Fv"][:, :]),
                           (Fv_b, ins["L2_Fv_b"][:, :].broadcast_to([P, L2_HEADS * L2_DH])),
                           (Fo, ins["L2_Fo"][:, :].rearrange("(c p) n -> p c n", p=P))], after=region.free_after)
    big = k.load("L2_experts", [(b1, ins["L2_b1"][:, :]), (b2, ins["L2_b2"][:, :]),
                                (W1, ins["L2_W1"].rearrange("e d f -> d e f"))] +
                 [(W2[:, e, :, :], ins["L2_W2"][e, :, :].rearrange("(c p) d -> p c d", p=P)) for e in range(EXPERTS)])
    fq_b, fk_b, fo_b = cols[:, 0:8], cols[:, 8:16], cols[:, 16:17]
    const = [k.fill(weight[:, :, e:e + 1], float(EXPERTS - e), after=region.free_after) for e in range(EXPERTS)]
    k.all_groups(k.layernorm)
    k.V.wait([const, loaded])
    k.A.wait(loaded)
    k.T.wait(loaded)
    lg, pr, t_p = k.softmax_experts("L2", Wg, loaded)
    k.scratch.put(lg, t_p)
    spare = [k.scratch.take() for _ in range(5)]
    t_gates = top2_gates(k, gates, pr, t_p, weight.rearrange("p n w -> p (n w)"), spare)
    for s in spare + [pr]:
        k.scratch.put(s, t_gates)

    def attention(g):
        x = k.cols(k.xn, g)
        bz, bv, zqk, zv = k.banks.take(), k.banks.take(), k.scratch.take(), k.scratch.take()
        t = k.mm([(bz[:, :], Wqk, x)], after=[bz.after, k.xn_ready[g]])
        t_z = k.acopy(zqk[:, :], bz[:, :], after=[t, zqk.after])
        t = k.mm([(bv[0:L2_DH, :], Wv, x)], after=bv.after)
        t_zv = k.acopy(zv[0:L2_DH, :], bv[0:L2_DH, :], after=[t, zv.after])
        k.banks.put(bz, t_z)
        k.banks.put(bv, t_zv)
        yield
        v = [[None, None] for _ in range(TPG)]
        for i in range(TPG):
            for c in range(2):
                b, s = k.banks.take(), k.scratch.take()
                t_fv = k.mm([(b[:, :], zv[0:L2_DH, i * P:(i + 1) * P], Fv[0:L2_DH, c * GW:(c + 1) * GW])], after=[b.after, t_zv])
                t = k.tt(s[:, :], b[:, :], Fv_b[:, c * GW:(c + 1) * GW], ALU.add, after=[t_fv, s.after])
                k.banks.put(b, t)
                v[i][c] = (s, t)
                yield
        k.scratch.put(zv, t_fv)
        acc = k.banks.take()
        units = []
        state = {"folded": 0}

        def second():
            m, half, b, O, p, t_p, qk = units.pop(0)
            h = 2 * m + half
            pt, t = turned_scores(k, p, t_p, h % 4 == 0)
            cs = slice((h % 8) * L2_DH, (h % 8 + 1) * L2_DH)
            r = half * L2_DH
            vv = [v[2 * b + jc][h // 8] for jc in range(2)]
            t_pv = k.mm([(O[r:r + L2_DH, b * SEQ:(b + 1) * SEQ], vv[jc][0][:, cs], pt[:, jc * SEQ:(jc + 1) * SEQ])
                         for jc in range(2)], after=[t, vv[0][1], vv[1][1], O.after])
            k.scratch.put(pt, t_pv)
            if half == 1 and b == BPG - 1:
                s = k.scratch.take()
                t = k.acopy(s[:, :], O[:, :], after=[t_pv, s.after])
                k.banks.put(O, t)
                for q in qk:
                    k.scratch.put(q, t_pv)
                state["t"] = k.mm([(acc[:, :], Fo[:, m, :], s[:, :])], after=[t] + ([acc.after] if m == 0 else []),
                                  start=(m == 0), stop=(m == L2_PAIRS - 1))
                k.scratch.put(s, state["t"])

        for m in range(L2_PAIRS):
            qk = []
            for r, bias in ((0, fq_b), (L2_DH, fk_b)):
                b, s = k.banks.take(), k.scratch.take()
                t = k.mm([(b[:, :], Fqk[r:r + L2_DH, m * P:(m + 1) * P], zqk[r:r + L2_DH, :])], after=[b.after, t_z])
                t = k.ts(s[:, :], b[:, :], bias[:, m:m + 1], None, ALU.add, after=[t, s.after])
                k.banks.put(b, t)
                qk.append((s, t))
            O = k.banks.take()
            for b in range(BPG):
                for half in range(2):
                    r, sl = half * L2_DH, slice(b * SEQ, (b + 1) * SEQ)
                    rs = k.stats.take()
                    p, t_e = attention_scores(k, qk[0][0][r:r + L2_DH, sl], qk[1][0][r:r + L2_DH, sl], 1.0 / 8.0,
                                              [qk[0][1], qk[1][1], rs.after], rs[:, 0:2])
                    t_r = k.recip(rs[:, 0:2], rs[:, 0:2], after=t_e)
                    t_p = [k.ts(p[:, i * SEQ:(i + 1) * SEQ], p[:, i * SEQ:(i + 1) * SEQ], rs[:, i:i + 1], None, ALU.mult,
                                after=[t_r, t_e]) for i in range(2)]
                    k.stats.put(rs, t_p)
                    units.append((m, half, b, O, p, t_p, [qk[0][0], qk[1][0]]))
                    if len(units) > 2:
                        second()
                    yield
        while units:
            second()
            yield
        k.scratch.put(zqk, state["t"])
        for i in range(TPG):
            for s, _ in v[i]:
                k.scratch.put(s, state["t"])
        s = k.scratch.take()
        s.token = k.act(s[:, :], acc[:, :], ACT.Identity, bias=fo_b, after=[state["t"], s.after])
        k.banks.put(acc, s.token)
        k.mixed[g] = s
        yield

    def ffn(g):
        k.T.wait(big)
        gt = k.scratch.take()
        t_gt = k.gates_to_rows(gates, gt, g, t_gates)
        acc = k.banks.take()

        def hidden(e, f, x, gate, t_gate):
            b, s = k.banks.take(), k.scratch.take()
            t = k.mm([(b[:, :], W1[:, e, f * P:(f + 1) * P], x)], after=b.after)
            n = e * L2_FF + f
            t = k.act(s[:, :], b[:, :], ACT.Relu, bias=b1[:, n:n + 1], after=[t, s.after, big])
            k.banks.put(b, t)
            return s, k.tt(s[:, :], s[:, :], gate[:, :], ALU.mult, after=[t, t_gate])

        yield from k.experts(g, gt, t_gt, acc, L2_FF, hidden, lambda e, f: W2[:, e, f, :], b2, after=big)
        k.gate_and_add(g, acc, k.t_acc, k.mixed[g])
        yield

    run_layer(k, attention, ffn, 3, 1)
    return k.x_ready


def layouts2(a):
    return {"L2_Wqk": np.concatenate([a["L2_attn_wq"], a["L2_attn_wk"]], axis=1), "L2_Wv": a["L2_attn_wv"],
            "L2_Fqk": np.concatenate([a["L2_attn_fcq_w"], a["L2_attn_fck_w"]], axis=0), "L2_Fv": a["L2_attn_fcv_w"],
            "L2_Fv_b": a["L2_attn_fcv_b"].reshape(1, -1), "L2_Fo": a["L2_attn_fco_w"],
            "L2_cols": np.concatenate([columns(a["L2_attn_" + n]) for n in ("fcq_b", "fck_b", "fco_b")], axis=1),
            "L2_Wg": a["L2_ffn_Wg"], "L2_W1": a["L2_ffn_W1"], "L2_W2": a["L2_ffn_W2"],
            "L2_b1": columns(a["L2_ffn_b1"]), "L2_b2": a["L2_ffn_b2"]}


L3_H, L3_D = 4, 32
L3_CONV = 4
L3_FIRS = (3, 15, 63)
L3_LMAX = max(L3_FIRS)
L3_CHUNK = 32
L3_CPT = P // L3_CHUNK
L3_CHUNKS = SEQ // L3_CHUNK
L3_PATHS = 5
L3_LEVELS = 5
L3_FF = 2
L3_CAPACITY = -(-2 * TOKENS * 5 // (EXPERTS * 4))
L3_PE_TAPS = 45


def l3_constants():
    r, c = np.arange(P)[:, None], np.arange(P)[None, :]
    same = r // L3_CHUNK == c // L3_CHUNK
    masks = [(r >> (n + 1) == c >> (n + 1)) & ((r >> n) % 2 == 0) & ((c >> n) % 2 == 1) for n in range(L3_LEVELS)]
    masks.append(same & (r <= c))
    masks.append(same)
    masks.append(r < c)
    path = np.zeros((P, L3_PATHS, P), np.float32)
    for h in range(L3_H):
        for p in range(L3_PATHS):
            path[h * L3_PATHS + p, p, h * L3_D:(h + 1) * L3_D] = 1.0
    return np.concatenate([np.concatenate(masks, axis=1).astype(np.float32), path.reshape(P, -1)], axis=1)


def layer3(k, region, filters):
    nc, ins = k.nc, k.ins
    k.phase("L3")
    take = region.take
    Wqkv = take("p (n) -> p n", n=3 * P)
    Wo = take("p (n) -> p n", n=P)
    Wb = take("p (n) -> p n", n=L3_H)
    taps = take("p (n) -> p n", n=3 * L3_CONV + sum(L3_FIRS) + 1)
    GW_ = take("p (n) -> p n", n=L3_H * L3_PATHS)
    row = take("p (n) -> p n", n=L3_H * (L3_PATHS + 2))
    consts = take("p (n) -> p n", n=8 * P + L3_PATHS * P)
    mask = [consts[:, i * P:(i + 1) * P] for i in range(8)]
    path = consts[:, 8 * P:].rearrange("p (q n) -> p q n", q=L3_PATHS)[0:L3_H * L3_PATHS]
    causal, head_block, earlier = mask[5], mask[6], mask[7]
    Wbx = take("p (h d) -> p h d", h=L3_H, d=L3_D)
    head_mean = take("p (n) -> p n", n=P)
    all_ones = take("p (n) -> p n", n=P)
    W1 = take("p (e f) -> p e f", e=EXPERTS, f=2 * L3_FF * P)
    W2 = take("p (e c d) -> p e c d", e=EXPERTS, c=L3_FF, d=P)
    Wg = take("p (n) -> p n", n=EXPERTS)
    gates = take("p (n) -> p n", n=TILES * EXPERTS)
    weight = take("p (n w) -> p n w", n=TILES, w=EXPERTS)
    NP = L3_H * L3_PATHS
    probs = take("p (n) -> p n", n=TILES * NP)
    diag = filters.take("p (j n) -> p j n", j=L3_PE_TAPS, n=P)
    loaded = k.load("L3", [(Wqkv, ins["L3_Wqkv"][:, :]), (Wo, ins["L3_Wo"][:, :]), (Wb, ins["L3_Wb"][:, :]),
                           (taps, ins["L3_taps"][:, :]), (GW_, ins["L3_gate_w"][:, :]), (consts, ins["L3_consts"][:, :]),
                           (row, ins["L3_row"][:, :].broadcast_to([P, L3_H * (L3_PATHS + 2)])), (Wg, ins["L3_Wg"][:, :])],
                    after=region.free_after)
    big = k.load("L3_experts", [(W1, ins["L3_W1"].rearrange("e d f -> d e f"))] +
                 [(W2[:, e, :, :], ins["L3_W2"][e, :, :].rearrange("(c p) d -> p c d", p=P)) for e in range(EXPERTS)])
    free = region.free_after
    const = [k.fill(weight[:, :, e:e + 1], float(EXPERTS - e), after=free) for e in range(EXPERTS)]
    const.append(k.fill(all_ones, 1.0, after=free))
    const.append(k.ts(head_mean, head_block, 1.0 / L3_D, None, ALU.mult, after=[loaded, free]))
    const.append(k.vcopy(Wbx, Wb.unsqueeze(2).to_broadcast([P, L3_H, L3_D]), after=[loaded, free]))
    conv_w = [taps[:, i * L3_CONV:(i + 1) * L3_CONV] for i in range(3)]
    fir_at = [3 * L3_CONV + sum(L3_FIRS[:i]) for i in range(3)]
    fir_w = [taps[:, a:a + n] for a, n in zip(fir_at, L3_FIRS)]
    norm_w = taps[:, fir_at[2] + L3_FIRS[2]:fir_at[2] + L3_FIRS[2] + 1]
    for j in range(L3_PE_TAPS):
        const.append(k.ts(diag[:, j, :], k.ident[:, :], fir_w[2][:, j:j + 1], None, ALU.mult, after=[loaded, filters.free_after]))
    CP, VP = L3_CONV - 1, L3_LMAX - 1
    pads = Pool([Slot(filters.take("p (b t) -> p b t", b=BPG, t=CP + SEQ), i) for i in range(2)])
    vpads = Pool([Slot(filters.take("p (b t) -> p b t", b=BPG, t=VP + SEQ), i) for i in range(2)])
    for s in pads.free:
        s.after = flat([k.fill(s[:, :, 0:CP], 0.0, after=filters.free_after), filters.free_after])
    for s in vpads.free:
        s.after = flat([k.fill(s[:, :, 0:VP], 0.0, after=filters.free_after), filters.free_after])
    gate_b, log_t, eps = row[:, 0:NP], row[:, NP:NP + L3_H], row[:, NP + L3_H:NP + 2 * L3_H]
    rs = k.scratch.take()
    inv_t, keep = rs[:, 0:L3_H], rs[:, L3_H:2 * L3_H]
    t1 = k.act(inv_t, log_t, ACT.Exp, scale=-1.0, after=[loaded, rs.after])
    t = k.ts(eps, eps, 0.0, 0.2, ALU.max, ALU.min, after=loaded)
    t2 = k.ts(keep, eps, -5.0, 1.0, ALU.mult, ALU.add, after=[t, rs.after])
    k.V.wait([const, loaded, t1, t2])
    k.T.wait([const, loaded])
    k.all_groups(k.layernorm)

    HT = 16
    for half in range(TILES // HT):
        bank, cl = k.banks.take(), k.scratch.take()
        n = HT * NP
        t = k.mms([(bank[:, i * NP:(i + 1) * NP], k.xn[:, (half * HT + i) * P:(half * HT + i + 1) * P], GW_)
                   for i in range(HT)], after=[bank.after, k.xn_ready])
        pr = probs[:, half * n:(half + 1) * n]
        rows = pr.rearrange("p (n w) -> p n w", w=L3_PATHS)
        c = cl[:, 0:HT * L3_H]
        bc = c.unsqueeze(2).to_broadcast([P, HT * L3_H, L3_PATHS])
        by_tile = pr.rearrange("p (i n) -> p i n", i=HT)
        t = k.tt(by_tile, bank[:, 0:n].rearrange("p (i n) -> p i n", i=HT), gate_b.unsqueeze(1).to_broadcast([P, HT, NP]),
                 ALU.add, after=[t, free])
        k.banks.put(bank, t)

        def per_head(v, op, t):
            toks = []
            for h in range(L3_H):
                a = by_tile[:, :, h * L3_PATHS:(h + 1) * L3_PATHS]
                toks.append(k.ts(a, a, v[:, h:h + 1], None, op, after=t))
            return toks
        t = per_head(inv_t, ALU.mult, t)
        t = k.red(c, rows, ALU.max, after=[t, cl.after])
        t = k.tt(rows, rows, bc, ALU.subtract, after=t)
        t_e = k.act(pr, pr, ACT.Exp, after=t)
        t = k.red(c, rows, ALU.add, after=[t_e, t])
        t = k.recip(c, c, after=t)
        t = k.tt(rows, rows, bc, ALU.mult, after=t)
        k.scratch.put(cl, t)
        t = per_head(keep, ALU.mult, t)
        t_probs = per_head(eps, ALU.add, t)
    k.scratch.put(rs, t_probs)

    W = TILES * EXPERTS
    v3 = lambda a: a.rearrange("p (n w) -> p n w", w=EXPERTS)
    lg, pr, t_p = k.softmax_experts("L3", Wg, loaded)
    k.scratch.put(lg, t_p)
    spare = [k.scratch.take() for _ in range(5)]
    sc, tmp, m1, m2, col = spare
    t = top2_gates(k, None, pr, t_p, weight.rearrange("p n w -> p (n w)"), spare, both=True)
    total = k.scratch.take()
    base = None
    kept = []
    for which, m in enumerate((m1, m2)):
        loc, tot = k.banks.take(), k.banks.take()
        t_l = k.mm([(loc[:, 0:W], earlier, m[:, 0:W])], after=[t, loc.after])
        t_t = k.mm([(tot[:, 0:W], all_ones, m[:, 0:W])], after=[t, tot.after])
        t_c = k.vcopy(sc[:, 0:W], tot[:, 0:W], after=[t_t, kept])
        t_s = [k.scan(tmp[:, e:W:EXPERTS], all_ones[:, 0:TILES], sc[:, e:W:EXPERTS], after=[t_c, kept])
               for e in range(EXPERTS)]
        t_x = k.tt(sc[:, 0:W], tmp[:, 0:W], sc[:, 0:W], ALU.subtract, after=t_s)
        t_x = k.tt(sc[:, 0:W], sc[:, 0:W], loc[:, 0:W], ALU.add, after=[t_x, t_l])
        if which == 1:
            t_x = k.tt(v3(sc[:, 0:W]), v3(sc[:, 0:W]), total[:, 0:EXPERTS].unsqueeze(1).to_broadcast([P, TILES, EXPERTS]),
                       ALU.add, after=[t_x, base])
        else:
            base = k.vcopy(total[:, 0:EXPERTS], tmp[:, W - EXPERTS:W], after=[t_s, total.after])
        k.banks.put(loc, t_x)
        k.banks.put(tot, t_c)
        t_k = k.stt(m[:, 0:W], sc[:, 0:W], float(L3_CAPACITY), m[:, 0:W], ALU.is_lt, ALU.mult, after=[t_x, t_l, t_t])
        kept = [kept, t_k, base]
    t = k.tt(sc[:, 0:W], m1[:, 0:W], m2[:, 0:W], ALU.add, after=kept)
    t = k.tt(gates, sc[:, 0:W], pr[:, 0:W], ALU.mult, after=[t, free])
    t = k.red(col[:, 0:TILES], v3(gates), ALU.add, after=t)
    t = k.ts(col[:, 0:TILES], col[:, 0:TILES], 1e-9, None, ALU.max, after=t)
    t = k.recip(col[:, 0:TILES], col[:, 0:TILES], after=t)
    t_gates = k.tt(v3(gates), v3(gates), col[:, 0:TILES].unsqueeze(2).to_broadcast([P, TILES, EXPERTS]), ALU.mult, after=t)
    for s in spare + [pr, total]:
        k.scratch.put(s, t_gates)

    four = lambda m: m.unsqueeze(1).to_broadcast([P, TPG, P])
    tiles = lambda a: a.rearrange("p (i n) -> p i n", n=P)
    batches = lambda a: a.rearrange("p (b t) -> p b t", b=BPG)

    def unit_rows(s, t, eps_col, weights, scale_col=None):
        sq, b = k.scratch.take(), k.banks.take()
        t1 = k.act(sq[:, :], s[:, :], ACT.Square, after=[t, sq.after])
        t1 = k.mm([(b[:, :], weights, sq[:, :])], after=[t1, b.after])
        t1 = k.act(sq[:, :], b[:, :], ACT.Sqrt, bias=eps_col, after=t1)
        k.banks.put(b, t1)
        t1 = k.recip(sq[:, :], sq[:, :], after=t1)
        if scale_col is None:
            t1 = k.tt(s[:, :], s[:, :], sq[:, :], ALU.mult, after=[t1, t])
        else:
            t1 = k.stt(s[:, :], s[:, :], scale_col, sq[:, :], ALU.mult, ALU.mult, after=[t1, t])
        k.scratch.put(sq, t1)
        return t1

    prepared = {}

    def prepare(g):
        x = k.cols(k.xn, g)
        rows = []
        for n in range(3):
            b, pad, s = k.banks.take(), pads.take(), k.scratch.take()
            t = k.mm([(b[:, :], Wqkv[:, n * P:(n + 1) * P], x)], after=[b.after, k.xn_ready[g]])
            t = k.acopy(pad[:, :, CP:], batches(b[:, :]), after=[t, pad.after])
            k.banks.put(b, t)
            t = k.ts(batches(s[:, :]), pad[:, :, 0:SEQ], conv_w[n][:, 0:1], None, ALU.mult, after=[t, s.after])
            for j in range(1, L3_CONV):
                t = k.stt(batches(s[:, :]), pad[:, :, j:j + SEQ], conv_w[n][:, j:j + 1], batches(s[:, :]), ALU.mult, ALU.add,
                          after=t)
            pads.put(pad, t)
            if n < 2:
                t = k.act(s[:, :], s[:, :], ACT.Silu, after=t)
                rows.append((s, t))
            else:
                v = vpads.take()
                t = k.act(v[:, :, VP:], batches(s[:, :]), ACT.Silu, after=[t, v.after])
                k.scratch.put(s, t)
                t_v = t
            yield
        (q, t_q), (kk, t_k) = rows
        t_q = unit_rows(q, t_q, k.eps[:, 1:2], head_block)
        yield
        t_k = unit_rows(kk, t_k, k.eps[:, 1:2], head_block)
        yield
        b, beta, kb, vb = k.banks.take(), k.scratch.take(), k.scratch.take(), k.scratch.take()
        t = k.mm([(b[:, :], Wbx.rearrange("p h d -> p (h d)"), x)], after=b.after)
        t = k.act(beta[:, :], b[:, :], ACT.Sigmoid, after=[t, beta.after])
        k.banks.put(b, t)
        t_kb = k.tt(kb[:, :], kk[:, :], beta[:, :], ALU.mult, after=[t, t_k, kb.after])
        t_vb = k.tt(batches(vb[:, :]), v[:, :, VP:], batches(beta[:, :]), ALU.mult, after=[t, t_v, vb.after])
        k.scratch.put(beta, [t_kb, t_vb])
        yield
        nat = []
        for s, t in ((kk, t_k), (kb, t_kb), (vb, t_vb)):
            b, o = k.banks.take(), k.scratch.take()
            t = k.turn([(b[:, i * P:(i + 1) * P], s[:, i * P:(i + 1) * P]) for i in range(TPG)], after=[t, b.after])
            t2 = k.acopy(o[:, :], b[:, :], after=[t, o.after])
            k.banks.put(b, t2)
            nat.append((o, t2))
            yield
        k.scratch.put(vb, t)
        (k_nat, t_kn), (kb_nat, t_kbn), (vb_nat, t_vbn) = nat
        attn = []
        for h in range(L3_H):
            r = slice(h * L3_D, (h + 1) * L3_D)
            b, s = k.banks.take(), k.scratch.take()
            t = k.mms([(b[:, i * P:(i + 1) * P], kk[r, i * P:(i + 1) * P], q[r, i * P:(i + 1) * P]) for i in range(TPG)],
                      after=[t_k, t_q, b.after])
            t = k.tt(tiles(s[:, :]), tiles(b[:, :]), four(causal), ALU.mult, after=[t, s.after])
            k.banks.put(b, t)
            attn.append((s, t))
            yield
        u_bank, w_bank = k.banks.take(), k.banks.take()
        t_u = t_w = None
        last_gram = None

        def inverse(h):
            r = slice(h * L3_D, (h + 1) * L3_D)
            b, gram, inv, invT, lm = k.banks.take(), *[k.scratch.take() for _ in range(4)]
            t = k.mms([(b[:, i * P:(i + 1) * P], kk[r, i * P:(i + 1) * P], kb[r, i * P:(i + 1) * P]) for i in range(TPG)],
                      after=[t_k, t_kb, b.after])
            gram_read.append(t)
            t_g = k.acopy(gram[:, :], b[:, :], after=[t, gram.after])
            k.banks.put(b, t_g)
            yield
            t = k.tt(tiles(lm[:, :]), tiles(gram[:, :]), four(mask[0]), ALU.mult, after=[t_g, lm.after], on=k.G)
            t_lm = k.G.run(lambda eng: eng.tensor_tensor(tiles(invT[:, :]), four(k.ident[:, :]), tiles(lm[:, :]), ALU.subtract),
                           [t, invT.after])
            t_T = t_lm
            t_i = k.V.run(lambda eng: eng.transpose(inv[:, :], invT[:, :]), [t_T, inv.after])
            t_read = t_lm
            yield
            for n in range(1, L3_LEVELS):
                t_lm = k.tt(tiles(lm[:, :]), tiles(gram[:, :]), four(mask[n]), ALU.mult, after=t_read, on=k.G)
                bx, xs = k.banks.take(), k.scratch.take()
                t = k.mms([(bx[:, i * P:(i + 1) * P], lm[:, i * P:(i + 1) * P], inv[:, i * P:(i + 1) * P]) for i in range(TPG)],
                          after=[t_lm, t_i, bx.after])
                t_read = t
                t = k.acopy(xs[:, :], bx[:, :], after=[t, xs.after])
                k.banks.put(bx, t)
                yield
                by = k.banks.take()
                t_y = k.mms([(by[:, i * P:(i + 1) * P], invT[:, i * P:(i + 1) * P], xs[:, i * P:(i + 1) * P]) for i in range(TPG)],
                            after=[t, t_T, by.after])
                k.scratch.put(xs, t_y)
                t_i = k.tt(inv[:, :], inv[:, :], by[:, :], ALU.subtract, after=[t_y, t_i, t_read])
                k.banks.put(by, t_i)
                t_T = k.V.run(lambda eng: eng.transpose(invT[:, :], inv[:, :]), [t_i, t_y])
                yield
            k.scratch.put(gram, t_lm)
            k.scratch.put(lm, t_read)
            k.scratch.put(inv, t_T)
            cs = slice(h * L3_D, (h + 1) * L3_D)
            k.T.wait([u_bank.after, w_bank.after])
            tu = k.mms([(u_bank[:, i * P + h * L3_D:i * P + (h + 1) * L3_D], invT[:, i * P:(i + 1) * P],
                         vb_nat[:, i * P + h * L3_D:i * P + (h + 1) * L3_D]) for i in range(TPG)], after=[t_T, t_vbn])
            tw = k.mms([(w_bank[cs, i * P:(i + 1) * P], kb_nat[:, i * P + h * L3_D:i * P + (h + 1) * L3_D],
                         invT[:, i * P:(i + 1) * P]) for i in range(TPG)], after=[t_T, t_kbn])
            k.scratch.put(invT, [tu, tw])
            done.append([tu, tw])
            yield

        gram_read, done = [], []
        for pair in ((0, 1), (2, 3)):
            two = [inverse(h) for h in pair]
            live = list(two)
            while live:
                for gen in list(live):
                    if next(gen, "end") == "end":
                        live.remove(gen)
                yield
        k.scratch.put(kk, [gram_read, [t for _, t in attn]])
        k.scratch.put(kb, gram_read)
        u, w = k.scratch.take(), k.scratch.take()
        t_u = k.acopy(u[:, :], u_bank[:, :], after=[done, u.after])
        t_w = k.acopy(w[:, :], w_bank[:, :], after=[done, w.after])
        k.banks.put(u_bank, t_u)
        k.banks.put(w_bank, t_w)
        k.scratch.put(kb_nat, done)
        k.scratch.put(vb_nat, done)
        prepared[g] = dict(q=(q, t_q), k_nat=(k_nat, t_kn), attn=attn, u=(u, t_u), w=(w, t_w), v=(v, t_v))
        yield

    def recur(g):
        d = prepared.pop(g)
        (q, t_q), (k_nat, t_kn), (u, t_u), (w, t_w), (v, t_v) = d["q"], d["k_nat"], d["u"], d["w"], d["v"]
        S = [k.scratch.take(), k.scratch.take()]
        t_S = k.fill(S[0][:, 0:BPG * P], 0.0, after=S[0].after)
        t_read = [[], S[1].after]
        s_bank, o_bank, w_bank = k.banks.take(), k.banks.take(), k.banks.take()
        t_o = []
        t_wread = w_bank.after
        for c in range(L3_CHUNKS):
            cur, nxt = S[c % 2], S[(c + 1) % 2]
            ci, tl = c % L3_CPT, c // L3_CPT
            r = slice(ci * L3_CHUNK, (ci + 1) * L3_CHUNK)
            at = lambda b: (TPG // BPG * b + tl) * P + ci * L3_CHUNK
            rd = []
            if c > 0:
                t = k.mms([(w_bank[r, b * P:(b + 1) * P], w[:, at(b):at(b) + L3_CHUNK], cur[:, b * P:(b + 1) * P])
                           for b in range(BPG)], after=[t_S, t_w, t_wread])
                rd.append(t)
                uu = tiles(u[:, :])[r, tl::TPG // BPG, :]
                t_u = [t_u, k.tt(uu, uu, w_bank[r, 0:BPG * P].rearrange("p (b n) -> p b n", b=BPG), ALU.subtract, after=[t, t_u])]
                t_wread = t_u[1]
            t = k.mms([(o_bank[:, at(b):at(b) + L3_CHUNK], cur[:, b * P:(b + 1) * P], q[:, at(b):at(b) + L3_CHUNK])
                       for b in range(BPG)], after=[t_S, t_q, o_bank.after])
            rd.append(t)
            t_o.append(t)
            t_read[c % 2] = rd
            yield
            if c < L3_CHUNKS - 1:
                for b in range(BPG):
                    col = (TPG // BPG * b + tl) * P
                    t = k.mm([(s_bank[:, b * P:(b + 1) * P], k_nat[r, col:col + P], u[r, col:col + P])],
                             after=[t_u, t_kn, s_bank.after], start=(c == 0 and b == 0), stop=(c == L3_CHUNKS - 2))
                t_S = k.tt(nxt[:, 0:BPG * P].rearrange("p (b n) -> p b n", b=BPG),
                           s_bank[:, 0:BPG * P].rearrange("p (b n) -> p b n", b=BPG),
                           head_block.unsqueeze(1).to_broadcast([P, BPG, P]), ALU.mult, after=[t, t_read[(c + 1) % 2]])
                k.T.wait(t_S)
                yield
        k.banks.put(s_bank, t_S)
        k.banks.put(w_bank, t_wread)
        for s in S:
            k.scratch.put(s, t_read)
        k.scratch.put(w, t_read)
        k.scratch.put(q, t_read)
        k.scratch.put(k_nat, t_S)
        b, dl = k.banks.take(), k.scratch.take()
        t_i = None
        for h in range(L3_H):
            s, t = d["attn"][h]
            t_i = k.mms([(b[h * L3_D:(h + 1) * L3_D, i * P:(i + 1) * P], u[:, i * P + h * L3_D:i * P + (h + 1) * L3_D],
                          s[:, i * P:(i + 1) * P]) for i in range(TPG)], after=[t_u, t, b.after])
            k.scratch.put(s, t_i)
        k.scratch.put(u, t_i)
        t = k.acopy(dl[:, :], o_bank[:, :], after=[t_o, dl.after])
        k.banks.put(o_bank, t)
        t_dl = k.tt(dl[:, :], dl[:, :], b[:, :], ALU.add, after=[t, t_i])
        k.banks.put(b, t_dl)
        yield
        b, pt = k.banks.take(), k.scratch.take()
        t = k.turn([(b[0:NP, i * P:(i + 1) * P], probs[:, (TPG * g + i) * NP:(TPG * g + i + 1) * NP]) for i in range(TPG)],
                   after=[b.after, t_probs])
        t_pt = k.acopy(pt[0:NP, :], b[0:NP, :], after=[t, pt.after])
        k.banks.put(b, t_pt)
        yield
        o = k.scratch.take()
        state = {"t": None}

        def add_path(p, value, t_value):
            b = k.banks.take()
            t = k.mm([(b[:, :], path[:, p, :], pt[0:NP, :])], after=[t_pt, b.after])
            dst = o if state["t"] is None else k.scratch.take()
            t = k.tt(batches(dst[:, :]), batches(b[:, :]), value, ALU.mult, after=[t, t_value, dst.after])
            k.banks.put(b, t)
            used = t
            if dst is not o:
                t = k.tt(o[:, :], o[:, :], dst[:, :], ALU.add, after=[t, state["t"]], on=k.G)
                k.scratch.put(dst, t)
            state["t"] = t
            return used

        t = add_path(3, batches(dl[:, :]), t_dl)
        k.scratch.put(dl, t)
        yield
        add_path(4, v[:, :, VP:], t_v)
        yield
        for n, K in enumerate(L3_FIRS):
            s = k.scratch.take()
            on_pe = L3_PE_TAPS if n == 2 else 0
            t_f = None
            if on_pe:
                b = k.banks.take()
                for j0 in range(0, on_pe, 5):
                    j1 = min(on_pe, j0 + 5)
                    t_f = k.mm([(b[:, :], diag[:, j, :], v[:, :, VP - K + 1 + j:VP - K + 1 + j + SEQ]) for j in range(j0, j1)],
                               after=[t_v, b.after], start=(j0 == 0), stop=(j1 == on_pe))
                    yield
            t = None
            for j in range(on_pe, K):
                src = v[:, :, VP - K + 1 + j:VP - K + 1 + j + SEQ]
                if t is None and not on_pe:
                    t = k.ts(batches(s[:, :]), src, fir_w[n][:, j:j + 1], None, ALU.mult, after=[s.after, t_v])
                else:
                    prev = batches(b[:, :]) if t is None else batches(s[:, :])
                    t = k.stt(batches(s[:, :]), src, fir_w[n][:, j:j + 1], prev, ALU.mult, ALU.add,
                              after=[t, s.after, t_v, t_f])
                    if on_pe and j == on_pe:
                        k.banks.put(b, t)
                if j % 3 == 2:
                    yield
            t = add_path(n, batches(s[:, :]), t)
            k.scratch.put(s, t)
            yield
        vpads.put(v, t)
        k.scratch.put(pt, t)
        t = unit_rows(o, state["t"], k.eps[:, 0:1], head_mean, norm_w)
        yield
        b, s = k.banks.take(), k.scratch.take()
        t = k.mm([(b[:, :], Wo, o[:, :])], after=[t, b.after])
        s.token = k.acopy(s[:, :], b[:, :], after=[t, s.after])
        k.scratch.put(o, t)
        k.banks.put(b, s.token)
        k.mixed[g] = s
        yield

    def ffn(g):
        k.T.wait(big)
        gt = k.scratch.take()
        t_gt = k.gates_to_rows(gates, gt, g, t_gates)
        acc = k.banks.take()

        def hidden(e, f, x, gate, t_gate):
            ba, bg, s = k.banks.take(), k.banks.take(), k.scratch.take()
            t = k.mm([(ba[:, :], W1[:, e, f * P:(f + 1) * P], x)], after=ba.after)
            t_g = k.mm([(bg[:, :], W1[:, e, (L3_FF + f) * P:(L3_FF + f + 1) * P], x)], after=bg.after)
            t = k.act(s[:, :], ba[:, :], ACT.Gelu, after=[t, s.after])
            k.banks.put(ba, t)
            t = k.tt(s[:, :], s[:, :], bg[:, :], ALU.mult, after=[t, t_g])
            k.banks.put(bg, t)
            return s, k.tt(s[:, :], s[:, :], gate[:, :], ALU.mult, after=[t, t_gate])

        yield from k.experts(g, gt, t_gt, acc, L3_FF, hidden, lambda e, f: W2[:, e, f, :], None, after=[], skew=2)
        k.gate_and_add(g, acc, k.t_acc, k.mixed[g])
        yield

    k.mixed = [None] * GROUPS
    interleave((prepare(0), 1))
    for g in range(GROUPS):
        streams = [(recur(g), 1)]
        if g + 1 < GROUPS:
            streams.append((prepare(g + 1), 1))
        interleave(*streams)
    for g in range(GROUPS):
        interleave((ffn(g), 1))
    return k.x_ready


def layouts3(a):
    g = lambda n: a["L3_attn_" + n]
    return {"L3_Wqkv": np.concatenate([g("Wq").T, g("Wk").T, g("Wv").T], axis=1), "L3_Wo": g("Wo").T, "L3_Wb": g("Wb").T,
            "L3_taps": np.concatenate([g("conv_q"), g("conv_k"), g("conv_v")] +
                                      [g("fir_" + n).reshape(P, -1) for n in "sml"] +
                                      [np.tile(g("norm_w"), L3_H).reshape(P, 1)], axis=1),
            "L3_gate_w": g("gate_w").reshape(L3_H * L3_PATHS, P).T,
            "L3_row": np.concatenate([g(n).reshape(1, -1) for n in ("gate_b", "log_temp", "eps_param")], axis=1),
            "L3_consts": l3_constants(), "L3_Wg": a["L3_ffn_Wg"], "L3_W1": a["L3_ffn_W_in"], "L3_W2": a["L3_ffn_W_out"]}


def columns(v):
    return v.reshape(-1, P).T


def layouts(a):
    d = {"x": a["L0_attn_x"].reshape(TOKENS, P).T}
    if 0 in LAYERS:
        d.update({
            "L0_W1": a["L0_ffn_W1"], "L0_W2": a["L0_ffn_W2"], "L0_b1": columns(a["L0_ffn_b1"]), "L0_b2": a["L0_ffn_b2"],
            "L0_Wr": a["L0_ffn_Wr"], "L0_br": a["L0_ffn_br"].reshape(1, EXPERTS),
            "L0_Win": a["L0_attn_W_in"].T, "L0_Wout": a["L0_attn_W_out"].T})
    if 1 in LAYERS:
        d.update(layouts1(a))
    if 2 in LAYERS:
        d.update(layouts2(a))
    if 3 in LAYERS:
        d.update(layouts3(a))
    return d


def build(nc, ins, out, layers=LAYERS):
    k = Kernel(nc, ins, out)
    k.setup()
    words = REGION_WORDS
    regions = [k.sb("weights_even", [P, words[0]]), k.sb("weights_odd", [P, words[1]])]
    free = [[], []]
    for n in layers:
        k.last_layer = n == layers[-1]
        own, other = [Region(regions[m], words[m], free[m]) for m in (n % 2, 1 - n % 2)]
        done = layer3(k, own, other) if n == 3 else (layer0, layer1, layer2)[n](k, own)
        free[n % 2] = [done, k.banks_readers()]
    k.finish()


def kernel(**inputs):
    import concourse.bacc as bacc
    from concourse.bass_utils import run_bass_kernel_spmd

    arrays = {name: np.ascontiguousarray(a) for name, a in layouts({n: np.asarray(a) for n, a in inputs.items()}).items()}
    nc = bacc.Bacc("TRN2", target_bir_lowering=False, num_devices=1)
    ins = {name: nc.dram_tensor(f"in_{name}", a.shape, mybir.dt.from_np(a.dtype), kind="ExternalInput").ap()
           for name, a in arrays.items()}
    out = nc.dram_tensor("out_x", (P, TOKENS), F32, kind="ExternalOutput").ap()
    build(nc, ins, out)
    r = run_bass_kernel_spmd(nc, [{f"in_{name}": a for name, a in arrays.items()}], core_ids=[0])
    return np.ascontiguousarray(r.results[0]["out_x"].T).reshape(BATCH, SEQ, P)
```

```python
import numpy as np
import concourse.bass as bass
from concourse import mybir
from contextlib import ExitStack

F32 = mybir.dt.float32
ALU = mybir.AluOpType
ACT = mybir.ActivationFunctionType
AX = mybir.AxisListType

P = 128
BATCH, SEQ = 16, 256
TOKENS = BATCH * SEQ
GW = 512
GROUPS = TOKENS // GW
BPG = GW // SEQ
TPG = GW // P
TILES = TOKENS // P
EXPERTS = 8


class Engine:

    def __init__(self, name, ctx, nc):
        self.name, self.ctx, self.nc = name, ctx, nc
        self.queue, self.seen = [], {}
        self.sem, self.count = None, 0

    def phase(self, label):
        self.sem = self.ctx.enter_context(self.nc.semaphore(f"{self.name}_{label}"))
        self.count = 0

    def wait(self, after):
        for token in flat(after):
            sem, value = token
            if self.seen.get(id(sem), 0) < value:
                self.seen[id(sem)] = value
                self.queue.append(lambda eng, s=sem, v=value: eng.wait_ge(s, v))

    def run(self, emit, after=(), signal=True):
        self.wait(after)
        if not signal:
            self.queue.append(emit)
            return None
        self.count += 1
        sem = self.sem
        self.queue.append(lambda eng: emit(eng).then_inc(sem, 1))
        return (sem, self.count)

    def play(self, eng):
        for item in self.queue:
            item(eng)


def flat(after):
    if after is None:
        return []
    if isinstance(after, tuple) and len(after) == 2 and isinstance(after[1], int):
        return [after]
    return [t for a in after for t in flat(a)]


class Slot:
    def __init__(self, tensor, index):
        self.tensor, self.index, self.after = tensor, index, []

    def __getitem__(self, key):
        return self.tensor[key]


class Pool:

    def __init__(self, slots):
        self.free = list(slots)
        self.slots = len(self.free)

    def take(self):
        assert self.free, ("no buffer is free here", self.slots)
        return self.free.pop(0)

    def put(self, slot, readers):
        slot.after = flat(readers)
        self.free.append(slot)


class Lane:

    def __init__(self, turns, pieces):
        self.turns, self.pieces, self.current = turns, list(pieces), None

    def step(self):
        while True:
            if self.current is None:
                if not self.pieces or not self.pieces[0][0]():
                    return False
                self.current = self.pieces.pop(0)[1]()
            if next(self.current, "end") != "end":
                return True
            self.current = None

    def over(self):
        return self.current is None and not self.pieces


def run_lanes(*lanes):
    while not all(lane.over() for lane in lanes):
        moved = False
        for lane in lanes:
            for _ in range(lane.turns):
                if not lane.step():
                    break
                moved = True
        assert moved or all(lane.over() for lane in lanes), "no lane may go on"


def interleave(*gens):
    run_lanes(*[Lane(1, [(lambda: True, lambda g=g: g)]) for g in gens])


def staged(units, *stages):
    last = max(lag for lag, _ in stages)
    for n in range(len(units) + last):
        for lag, f in stages:
            if 0 <= n - lag < len(units):
                f(units[n - lag])
        yield


class Kernel:
    def __init__(self, nc, ins, out):
        self.nc, self.ins, self.out = nc, ins, out
        self.ctx = ExitStack()
        self.V = Engine("vector", self.ctx, nc)
        self.A = Engine("scalar", self.ctx, nc)
        self.G = Engine("gpsimd", self.ctx, nc)
        self.T = Engine("tensor", self.ctx, nc)
        self.D = Engine("sync", self.ctx, nc)
        self.stores = []

    def sb(self, name, shape, dt=F32):
        return self.ctx.enter_context(self.nc.sbuf_tensor(name, shape, dt))

    def phase(self, label):
        for e in (self.V, self.A, self.G, self.T):
            e.phase(label)

    def load(self, name, pairs, after=()):
        sem = self.ctx.enter_context(self.nc.semaphore(f"load_{name}"))
        self.D.wait(after)
        for dst, src in pairs:
            self.D.queue.append(lambda eng, d=dst, s=src: eng.dma_start(d, s).then_inc(sem, 16))
        return (sem, 16 * len(pairs))

    def mm(self, products, after=(), start=True, stop=True):
        self.T.wait(after)
        token = None
        n = len(products)
        for i, (o, l, r) in enumerate(products):
            token = self.T.run(lambda eng, o=o, l=l, r=r, a=(start and i == 0), z=(stop and i == n - 1):
                               eng.matmul(o, l, r, start=a, stop=z, skip_group_check=True),
                               signal=(i == n - 1))
        return token

    def mms(self, products, after=()):
        self.T.wait(after)
        token = None
        for i, (o, l, r) in enumerate(products):
            token = self.T.run(lambda eng, o=o, l=l, r=r: eng.matmul(o, l, r, start=True, stop=True,
                                                                     skip_group_check=True),
                               signal=(i == len(products) - 1))
        return token

    def turn(self, pairs, after=()):
        self.T.wait(after)
        token = None
        for i, (o, a) in enumerate(pairs):
            k = a.shape[0]
            token = self.T.run(lambda eng, o=o, a=a, k=k: eng.transpose(o, a, self.ident[0:k, 0:k]),
                               signal=(i == len(pairs) - 1))
        return token

    def tt(self, out, a, b, op, after=(), on=None):
        return (on or self.V).run(lambda eng: eng.tensor_tensor(out, a, b, op), after)

    def ts(self, out, a, s1, s2, op0, op1=None, after=(), on=None):
        if op1 is None:
            return (on or self.V).run(lambda eng: eng.tensor_scalar(out, a, s1, None, op0), after)
        return (on or self.V).run(lambda eng: eng.tensor_scalar(out, a, s1, s2, op0, op1), after)

    def recip(self, out, a, after=()):
        return self.V.run(lambda eng: eng.reciprocal(out, a), after)

    def stt(self, out, a, s, b, op0, op1, after=()):
        return self.V.run(lambda eng: eng.scalar_tensor_tensor(out=out, in0=a, scalar=s, in1=b, op0=op0, op1=op1), after)

    def red(self, out, a, op, after=(), negate=False):
        return self.V.run(lambda eng: eng.tensor_reduce(out, a, AX.X, op, negate=negate), after)

    def scan(self, out, decay, add, after=()):
        return self.V.run(lambda eng: eng.tensor_tensor_scan(out, decay, add, 0.0, ALU.mult, ALU.add), after)

    def act(self, out, a, func, bias=None, scale=1.0, accum=None, after=()):
        def emit(eng):
            kw = {"scale": scale}
            if bias is not None:
                kw["bias"] = bias
            if accum is not None:
                kw["accum_out"] = accum
            return eng.activation(out, a, func, **kw)
        return self.A.run(emit, after)

    def vcopy(self, out, a, after=(), on=None):
        return (on or self.V).run(lambda eng: eng.tensor_copy(out, a), after)

    def acopy(self, out, a, after=(), scale=1.0):
        return self.act(out, a, ACT.Copy, scale=scale, after=after)

    def fill(self, out, value, after=(), on=None):
        return (on or self.G).run(lambda eng: eng.memset(out, value), after)

    def keep_where(self, ap, pattern, base, mult, op, fill, after=()):
        return self.G.run(lambda eng: eng.affine_select(out=ap, in_=ap, compare_op=op, fill=fill, base=base,
                                                        pattern=pattern, channel_multiplier=mult), after)

    def setup(self):
        self.xT = self.sb("x_channels", [P, TOKENS])
        self.xn = self.sb("normed_channels", [P, TOKENS])
        self.ident = self.sb("identity", [P, P])
        self.mean_w = self.sb("mean_weights", [P, P])
        self.eps = self.sb("eps_columns", [P, 4])
        self.scratch = Pool([Slot(self.sb(f"scratch{i}", [P, GW]), i) for i in range(SCRATCH)])
        self.banks = Pool([Slot(self.ctx.enter_context(self.nc.psum_tensor(f"bank{i}", [P, GW], F32)), i)
                           for i in range(8)])
        self.gate_slots = Pool([Slot(self.sb(f"gate_tile{i}", [P, GW]), i) for i in range(GATE_SLOTS)])
        for slot in self.gate_slots.free:
            slot.sem, slot.landed = self.ctx.enter_context(self.nc.semaphore(f"gate_tile{slot.index}")), 0
        self.stats = Pool([Slot(self.sb(f"stats{i}", [P, 16]), i) for i in range(12)])
        self.phase("setup")
        t = [self.fill(self.ident[:, :], 0.0),
             self.fill(self.mean_w[:, :], 1.0 / P)]
        for i, e in enumerate((1e-5, 1e-6, 0.0, 1.0)):
            t.append(self.fill(self.eps[:, i:i + 1], e))
        a = self.keep_where(self.ident[:, :], [[-1, P]], 0, 1, ALU.not_equal, 1.0, after=t)
        self.const = [a, t]
        for e in (self.V, self.A, self.T):
            e.wait(self.const)
        self.x_ready = [self.load(f"x{g}", [(self.cols(self.xT, g), self.ins["x"][:, g * GW:(g + 1) * GW])])
                        for g in range(GROUPS)]
        self.xn_ready = [None] * GROUPS
        self.t_acc = [None] * GROUPS
        self.xn_read = [[] for _ in range(GROUPS)]

    def cols(self, t, g):
        return t[:, g * GW:(g + 1) * GW]

    def layernorm(self, g):
        x, xn = self.cols(self.xT, g), self.cols(self.xn, g)
        mean, sq, var = self.banks.take(), self.scratch.take(), self.banks.take()
        t_mean = self.mm([(mean[:, :], self.mean_w[:, :], x)], after=[mean.after, self.x_ready[g]])
        yield
        t_d = self.tt(xn, x, mean[:, :], ALU.subtract, after=[t_mean, self.xn_read[g]])
        self.banks.put(mean, t_d)
        t_sq = self.act(sq[:, :], xn, ACT.Square, after=[t_d, sq.after])
        yield
        t_var = self.mm([(var[:, :], self.mean_w[:, :], sq[:, :])], after=[t_sq, var.after])
        yield
        t_r = self.inverse_root(sq[:, :], var, self.eps[:, 0:1], t_var)
        yield
        self.xn_ready[g] = self.tt(xn, xn, sq[:, :], ALU.mult, after=[t_r, t_d])
        self.scratch.put(sq, self.xn_ready[g])
        self.xn_read[g] = []
        yield

    def inverse_root(self, out, bank, eps, after):
        t = self.act(out, bank[:, :], ACT.Ln, bias=eps, after=after)
        self.banks.put(bank, t)
        return self.act(out, out, ACT.Exp, scale=-0.5, after=t)

    def first_layernorm(self):
        if self.first_layer:
            for g in range(0, GROUPS, 4):
                interleave(*[self.layernorm(h) for h in range(g, g + 4)])

    def one_hot_first(self, mask, score, tmp, col, weight, n, w, after):
        v3 = lambda a: a.rearrange("p (n w) -> p n w", w=w)
        b = lambda c: c.unsqueeze(2).to_broadcast([P, n, w])
        t = self.red(col, v3(score), ALU.max, after=after)
        t = self.tt(v3(tmp), v3(score), b(col), ALU.is_equal, after=t)
        t = self.tt(tmp, tmp, weight, ALU.mult, after=t)
        t = self.red(col, v3(tmp), ALU.max, after=t)
        t = self.tt(v3(mask), v3(tmp), b(col), ALU.is_equal, after=t)
        return t

    def softmax_experts(self, name, Wr, after, bias=None):
        N = TILES * EXPERTS
        bank = self.banks.take()
        t = self.mms([(bank[:, i * EXPERTS:(i + 1) * EXPERTS], self.xn[:, i * P:(i + 1) * P], Wr)
                      for i in range(TILES)], after=[bank.after, after, self.xn_ready])
        v3 = lambda a: a.rearrange("p (n w) -> p n w", w=EXPERTS)
        bc = lambda c: c.unsqueeze(2).to_broadcast([P, TILES, EXPERTS])
        lg, pr, col = self.scratch.take(), self.scratch.take(), self.scratch.take()
        l, p, c = lg[:, 0:N], pr[:, 0:N], col[:, 0:TILES]
        if bias is None:
            t = self.vcopy(l, bank[:, 0:N], after=[t, lg.after])
        else:
            t = self.tt(v3(l), v3(bank[:, 0:N]), bias.unsqueeze(1).to_broadcast([P, TILES, EXPERTS]), ALU.add,
                        after=[t, lg.after])
        self.banks.put(bank, t)
        t = self.red(c, v3(l), ALU.max, after=[t, col.after])
        t = self.tt(v3(l), v3(l), bc(c), ALU.subtract, after=t)
        t_e = self.act(p, l, ACT.Exp, after=[t, pr.after])
        t = self.red(c, v3(p), ALU.add, after=[t_e, t])
        t = self.recip(c, c, after=t)
        t = self.tt(v3(p), v3(p), bc(c), ALU.mult, after=t)
        self.scratch.put(col, t)
        return lg, pr, t

    def gates_to_rows(self, gates, label, after):
        rows = self.nc.dram_tensor(f"gate_rows_{label}", (EXPERTS, TOKENS), F32).ap()
        sem = self.ctx.enter_context(self.nc.semaphore(f"gate_rows_{label}"))
        for g in range(GROUPS):
            bank, gt = self.banks.take(), self.scratch.take()
            t = self.turn([(bank[0:EXPERTS, i * P:(i + 1) * P],
                            gates[:, (TPG * g + i) * EXPERTS:(TPG * g + i + 1) * EXPERTS]) for i in range(TPG)],
                          after=[bank.after, after])
            t = self.vcopy(gt[0:EXPERTS, :], bank[0:EXPERTS, :], after=[t, gt.after])
            self.banks.put(bank, t)
            self.D.wait(t)
            self.D.queue.append(lambda eng, g=g, gt=gt: eng.dma_start(rows[:, g * GW:(g + 1) * GW], gt[0:EXPERTS, :])
                                .then_inc(sem, 16))
            self.scratch.put(gt, (sem, 16 * GROUPS))
        self.stores.append((sem, 16 * GROUPS))
        return rows, (sem, 16 * GROUPS)

    def gate_tile(self, rows, t_rows, e, g):
        slot = self.gate_slots.take()
        slot.landed += 16
        self.D.wait([t_rows, slot.after])
        src = rows[e:e + 1, g * GW:(g + 1) * GW].broadcast_to([P, GW])
        self.D.queue.append(lambda eng: eng.dma_start(slot[:, :], src).then_inc(slot.sem, 16))
        slot.token = (slot.sem, slot.landed)
        return slot

    def experts(self, g, rows, acc, nf, hidden, W2, b2, after, skew=4, ahead=4):
        x = self.cols(self.xn, g)
        units = [{"e": e, "f": f} for e in range(EXPERTS) for f in range(nf)]
        gates, used = {}, {e: [] for e in range(EXPERTS)}

        def fetch(u):
            if u["f"] == 0:
                gates[u["e"]] = self.gate_tile(*rows, u["e"], g)

        def up(u):
            e = u["e"]
            u["slot"], u["t"] = hidden(e, u["f"], x, gates[e])
            used[e].append(u["t"])
            if u["f"] == nf - 1:
                self.gate_slots.put(gates[e], used[e])

        def down(u):
            n = u["e"] * nf + u["f"]
            tok = self.mm([(acc[:, :], W2(u["e"], u["f"]), u["slot"][:, :])], after=[u["t"]] + ([acc.after] if n == 0 else []),
                          start=(n == 0), stop=(n == len(units) - 1 and b2 is None))
            self.scratch.put(u["slot"], tok)
            self.t_acc[g] = tok

        yield from staged(units, (0, fetch), (ahead, up), (ahead + skew, down))
        if b2 is not None:
            gt = self.gate_slots.take()
            gt.landed += 16
            self.D.wait(gt.after)
            self.D.queue.append(lambda eng: eng.dma_start(gt[0:EXPERTS, :], rows[0][:, g * GW:(g + 1) * GW]).then_inc(gt.sem, 16))
            self.t_acc[g] = self.mm([(acc[:, :], b2, gt[0:EXPERTS, :])], after=[(gt.sem, gt.landed), after], start=False)
            self.gate_slots.put(gt, self.t_acc[g])

    def gate_and_add(self, g, acc, t_acc, s, silu=None):
        x = self.cols(self.xT, g)
        if silu is None:
            sl = self.scratch.take()
            t = self.act(sl[:, :], acc[:, :], ACT.Silu, after=[t_acc, sl.after])
            self.banks.put(acc, t)
        else:
            sl, t = silu, t_acc
        t = self.tt(sl[:, :], sl[:, :], s[:, :], ALU.mult, after=[t, s.token])
        self.scratch.put(s, t)
        self.x_ready[g] = self.tt(x, x, sl[:, :], ALU.add, after=t)
        self.scratch.put(sl, self.x_ready[g])
        self.xn_read[g] = [t_acc, s.token]
        if self.last_layer:
            self.D.wait(self.x_ready[g])
            sem = self.ctx.enter_context(self.nc.semaphore(f"store_group{g}"))
            self.D.queue.append(lambda eng: eng.dma_start(self.out[:, g * GW:(g + 1) * GW], x).then_inc(sem, 16))
            self.stores.append((sem, 16))
        else:
            yield
            yield from self.layernorm(g)

    def banks_readers(self):
        return [s.after for s in self.banks.free + self.scratch.free + self.stats.free]

    def finish(self):
        self.D.wait(self.stores)
        with self.nc.Block() as block:
            block.sync(self.D.play)
            block.vector(self.V.play)
            block.scalar(self.A.play)
            block.gpsimd(self.G.play)
            block.tensor(self.T.play)
        self.ctx.close()

LAYERS = [0,1,2,3]
SCRATCH = 38
REGION_WORDS = (10300, 12200)
GATE_SLOTS = 4


L0_HEADS = 16
L0_DH = P // L0_HEADS
L0_ORDERS = (1, 2, 3, 4, 5)
L0_FF = 4


def chebyshev_weights():
    order = 6
    alpha = (np.arange(order, dtype=np.float32) + 1.0) ** (-1.5)
    tail = np.flip(np.cumsum(np.flip(alpha)))
    beta = np.concatenate([np.zeros(1, np.float32), tail[1:].astype(np.float32), np.zeros(order - 1, np.float32)])
    return beta / beta.sum()


def layer0(k, region):
    nc, ins = k.nc, k.ins
    beta = chebyshev_weights()
    assert [i for i in range(len(beta)) if beta[i] != 0] == list(L0_ORDERS)
    k.phase("L0")
    take = region.take
    W1 = take("p (e f) -> p e f", e=EXPERTS, f=512)
    W2 = take("p (e c d) -> p e c d", e=EXPERTS, c=L0_FF, d=P)
    b1 = take("p (n) -> p n", n=EXPERTS * L0_FF)
    b2 = take("p (n) -> p n", n=P)[0:EXPERTS, :]
    Wr = take("p (n) -> p n", n=EXPERTS)
    br = take("p (n) -> p n", n=EXPERTS)
    Win = take("p (n) -> p n", n=3 * P)
    Wout = take("p (n) -> p n", n=P)
    NO = len(L0_ORDERS)
    rows = NO * L0_HEADS
    head_sum = take("p (o r) -> p o r", o=NO, r=rows)
    head_back = take("p (n) -> p n", n=P)[0:rows, :]
    ones = take("p (n) -> p n", n=SEQ)
    gates = take("p (n) -> p n", n=TILES * EXPERTS)
    weight = take("p (n w) -> p n w", n=TILES, w=EXPERTS)
    small = k.load("L0_small", [(Wr, ins["L0_Wr"][:, :]), (br, ins["L0_br"][:, :].broadcast_to([P, EXPERTS])),
                                (Win, ins["L0_Win"][:, :]), (Wout, ins["L0_Wout"][:, :]), (b1, ins["L0_b1"][:, :]),
                                (b2, ins["L0_b2"][:, :])], after=region.free_after)
    big = k.load("L0_experts", [(W1[:, e, :], ins["L0_W1"][e, :, :]) for e in range(EXPERTS)] +
                 [(W2[:, e, :, :], ins["L0_W2"][e, :, :].rearrange("(c p) d -> p c d", p=P)) for e in range(EXPERTS)])
    t = [k.fill(head_sum, 0.0, after=region.free_after), k.fill(ones, 1.0)]
    const = [t[1]]
    for o in range(NO):
        v = head_sum[:, o, o * L0_HEADS:(o + 1) * L0_HEADS]
        t1 = k.fill(v, 1.0, after=t)
        t2 = k.keep_where(v, [[-L0_DH, L0_HEADS]], 0, 1, ALU.is_ge, 0.0, after=t1)
        const.append(k.keep_where(v, [[L0_DH, L0_HEADS]], L0_DH - 1, -1, ALU.is_ge, 0.0, after=t2))
    hb = head_back.rearrange("p (h d) -> p h d", d=L0_DH)
    bank, buf = k.banks.take(), k.scratch.take()
    t0 = k.ts(buf[:, 0:rows], head_sum[:, 0, :], float(beta[L0_ORDERS[0]]), None, ALU.mult, after=[const, buf.after])
    for o in range(1, NO):
        t0 = k.stt(buf[:, 0:rows], head_sum[:, o, :], float(beta[L0_ORDERS[o]]), buf[:, 0:rows], ALU.mult, ALU.add, after=t0)
    t0 = k.turn([(bank[0:rows, 0:P], buf[:, 0:rows])], after=[bank.after, t0])
    t0 = k.vcopy(head_back, bank[0:rows, 0:P], after=t0)
    k.banks.put(bank, t0)
    k.scratch.put(buf, t0)
    for e in range(EXPERTS):
        const.append(k.fill(weight[:, :, e:e + 1], float(EXPERTS - e)))
    const.append(t0)
    k.T.wait(const)
    k.V.wait(const)

    k.first_layernorm()

    W = TILES * EXPERTS
    lg, pr, t_p = k.softmax_experts("L0", Wr, small, bias=br)
    tmp, col = k.scratch.take(), k.scratch.take()
    t = k.one_hot_first(gates, lg[:, 0:W], tmp[:, 0:W], col[:, 0:TILES], weight.rearrange("p n w -> p (n w)"),
                        TILES, EXPERTS, after=[t_p, tmp.after, col.after])
    t_gates = k.tt(gates, gates, pr[:, 0:W], ALU.mult, after=[t, t_p])
    for s in (lg, pr, tmp, col):
        k.scratch.put(s, t_gates)
    gate_rows = k.gates_to_rows(gates, "L0", t_gates)

    def attention(g):
        x = k.cols(k.xn, g)
        k.T.wait(small)
        xs = []
        for i in range(2):
            b, s = k.banks.take(), k.scratch.take()
            t = k.mm([(b[:, :], Win[:, i * P:(i + 1) * P], x)], after=[b.after, k.xn_ready[g]])
            t = k.act(s[:, :], b[:, :], ACT.Copy, scale=float(1.0 / np.sqrt(np.float32(L0_DH))), after=[t, s.after])
            k.banks.put(b, t)
            t = k.ts(s[:, :], s[:, :], -1.0 + 1e-6, 1.0 - 1e-6, ALU.max, ALU.min, after=t)
            xs.append((s, t))
            yield
        b, v = k.banks.take(), k.scratch.take()
        t = k.mm([(b[:, :], Win[:, 2 * P:3 * P], x)], after=b.after)
        t_v = k.acopy(v[:, :], b[:, :], after=[t, v.after])
        k.banks.put(b, t_v)
        yield
        prev, cur, dbl = [None, None], [xs[0], xs[1]], []
        for s, t in xs:
            d = k.scratch.take()
            dbl.append((d, k.ts(d[:, :], s[:, :], 2.0, None, ALU.mult, after=[t, d.after])))
        num = k.scratch.take()
        sums = [k.banks.take(), k.banks.take()]
        t_num = None
        t_sum = [None, None]
        for o in range(NO):
            if o > 0:
                for i in range(2):
                    n = k.scratch.take()
                    (cs, ct), (ds, dt) = cur[i], dbl[i]
                    t = k.tt(n[:, :], ds[:, :], cs[:, :], ALU.mult, after=[ct, dt, n.after])
                    if prev[i] is None:
                        t = k.ts(n[:, :], n[:, :], -1.0, None, ALU.add, after=t)
                    else:
                        ps, pt = prev[i]
                        t = k.tt(n[:, :], n[:, :], ps[:, :], ALU.subtract, after=[t, pt], on=k.G)
                        k.scratch.put(ps, [t, t_sum[i], t_num])
                    prev[i], cur[i] = cur[i], (n, t)
            for i in range(2):
                s, t = cur[i]
                t_sum[i] = k.mm([(sums[i][0:rows, :], head_sum[:, o, :], s[:, :])],
                                after=[t] + ([sums[i].after] if o == 0 else []), start=(o == 0), stop=(o == NO - 1))
            yield
            kv, cu = k.scratch.take(), k.scratch.take()
            t = k.tt(kv[:, :], cur[1][0][:, :], v[:, :], ALU.mult, after=[cur[1][1], t_v, kv.after])
            t_c = [k.scan(cu[:, j * SEQ:(j + 1) * SEQ], ones, kv[:, j * SEQ:(j + 1) * SEQ], after=[t, cu.after])
                   for j in range(BPG)]
            dst = num if o == 0 else kv
            t = k.stt(dst[:, :], cur[0][0][:, :], float(beta[L0_ORDERS[o]]), cu[:, :], ALU.mult, ALU.mult,
                      after=[t_c, cur[0][1]] + ([num.after] if o == 0 else []))
            t_q = t
            if o > 0:
                t = k.tt(num[:, :], num[:, :], kv[:, :], ALU.add, after=[t, t_num], on=k.G)
            k.scratch.put(kv, t)
            k.scratch.put(cu, t_q)
            t_num = t
            yield
        for i in range(2):
            for s in (prev[i][0], cur[i][0], dbl[i][0]):
                k.scratch.put(s, [t_num, t_sum[i]])
        k.scratch.put(v, t_num)
        kc, den = k.scratch.take(), k.banks.take()
        t_c = [k.scan(kc[0:rows, j * SEQ:(j + 1) * SEQ], ones[0:rows, :], sums[1][0:rows, j * SEQ:(j + 1) * SEQ],
                      after=[t_sum[1], kc.after]) for j in range(BPG)]
        t = k.tt(kc[0:rows, :], kc[0:rows, :], sums[0][0:rows, :], ALU.mult, after=[t_c, t_sum[0]])
        k.banks.put(sums[0], t)
        k.banks.put(sums[1], t)
        yield
        t = k.mm([(den[:, :], head_back, kc[0:rows, :])], after=[t, den.after])
        t = k.ts(kc[:, :], den[:, :], 1e-7, None, ALU.add, after=t)
        k.banks.put(den, t)
        t = k.recip(kc[:, :], kc[:, :], after=t)
        t = k.tt(num[:, :], num[:, :], kc[:, :], ALU.mult, after=[t, t_num])
        k.scratch.put(kc, t)
        yield
        b, s = k.banks.take(), k.scratch.take()
        t = k.mm([(b[:, :], Wout, num[:, :])], after=[t, b.after])
        s.token = k.acopy(s[:, :], b[:, :], after=[t, s.after])
        k.scratch.put(num, t)
        k.banks.put(b, s.token)
        k.mixed[g] = s
        yield

    def ffn(g):
        k.T.wait([big, small])
        acc = k.banks.take()

        def hidden(e, f, x, gate):
            b, s = k.banks.take(), k.scratch.take()
            t = k.mm([(b[:, :], W1[:, e, f * P:(f + 1) * P], x)], after=b.after)
            n = e * L0_FF + f
            t = k.act(s[:, :], b[:, :], ACT.Gelu, bias=b1[:, n:n + 1], after=[t, s.after, small])
            k.banks.put(b, t)
            return s, k.tt(s[:, :], s[:, :], gate[:, :], ALU.mult, after=[t, gate.token])

        yield from k.experts(g, gate_rows, acc, L0_FF, hidden, lambda e, f: W2[:, e, f, :], b2, after=small)
        yield from k.gate_and_add(g, acc, k.t_acc[g], k.mixed[g])

    run_layer(k, attention, ffn, 1, 2)
    return k.x_ready


def run_layer(k, mix, ffn, mix_turns, ffn_turns):
    k.mixed = [None] * GROUPS
    passed = []

    def experts(g):
        yield from ffn(g)
        passed.append(g)

    run_lanes(Lane(mix_turns, [(lambda g=g: len(passed) >= g - 1, lambda g=g: mix(g)) for g in range(GROUPS)]),
              Lane(ffn_turns, [(lambda g=g: k.mixed[g] is not None, lambda g=g: experts(g)) for g in range(GROUPS)]))


class Region:

    def __init__(self, tensor, words, free_after):
        self.tensor, self.words, self.free_after, self.at = tensor, words, free_after, 0

    def take(self, pattern, **sizes):
        n = int(np.prod(list(sizes.values())))
        n += -n % 8
        assert self.at + n <= self.words, ("region", self.at + n)
        ap = self.tensor[:, self.at:self.at + int(np.prod(list(sizes.values())))]
        self.at += n
        return ap if len(sizes) == 1 else ap.rearrange(pattern, **sizes)


L1_INNER = 2
L1_H, L1_E, L1_DH, L1_K = 8, 5, 64, 3
L1_ROW = L1_H * L1_DH


def top_mask(k, mask, score, tmp, pick, col, weight, n, w, count, after):
    t = after
    for r in range(count):
        t = k.one_hot_first(pick, score, tmp, col, weight, n, w, after=t)
        if r == 0:
            t_m = k.vcopy(mask, pick, after=t)
        else:
            t_m = k.tt(mask, mask, pick, ALU.add, after=[t, t_m])
        if r < count - 1:
            t = k.stt(score, pick, -4.0, score, ALU.mult, ALU.add, after=t)
        t = [t, t_m]
    return t


def scores_exp(k, q, kk, after, rsum):
    bank, p, st = k.banks.take(), k.scratch.take(), k.stats.take()
    t = k.mms([(bank[:, i * SEQ:(i + 1) * SEQ], q[:, i * P:(i + 1) * P], kk) for i in range(2)],
              after=[bank.after, after])
    mx = st[:, 0:2]
    t_m = k.red(mx, bank[:, :].rearrange("p (i j) -> p i j", j=SEQ), ALU.max, after=[t, st.after], negate=True)
    t_e = [k.act(p[:, i * SEQ:(i + 1) * SEQ], bank[:, i * SEQ:(i + 1) * SEQ], ACT.Exp, bias=mx[:, i:i + 1],
                 accum=rsum[:, i:i + 1], after=[t_m, p.after]) for i in range(2)]
    k.banks.put(bank, t_e)
    k.stats.put(st, t_e)
    return p, t_e


def turned_scores(k, p, t_p, on_vector):
    bank, pt = k.banks.take(), k.scratch.take()
    t = k.turn([(bank[:, jc * SEQ + i * P:jc * SEQ + (i + 1) * P], p[:, i * SEQ + jc * P:i * SEQ + (jc + 1) * P])
                for jc in range(2) for i in range(2)], after=[bank.after, t_p])
    k.scratch.put(p, t)
    copy = k.vcopy if on_vector else k.acopy
    t = copy(pt[:, :], bank[:, :], after=[t, pt.after])
    k.banks.put(bank, t)
    return pt, t


def layer1(k, region):
    nc, ins = k.nc, k.ins
    k.phase("L1")
    take = region.take
    Iw = take("p (n) -> p n", n=256)
    Gw = take("p (n) -> p n", n=256)
    Bw, Cw, Dw = [take("p (c n) -> p c n", c=2, n=256) for _ in range(3)]
    Ow = take("p (c n) -> p c n", c=2, n=P)
    cols = take("p (n) -> p n", n=16)
    decay = take("p (c n) -> p c n", c=2, n=SEQ)
    one = take("p (n) -> p n", n=SEQ)
    Wsd = take("p (n) -> p n", n=2 * L1_H * L1_E)
    Wx = {kind: take("p (e n) -> p e n", e=L1_E, n=L1_ROW) for kind in ("q", "k", "v")}
    Wo = take("p (c n) -> p c n", c=3, n=P)
    NR = TPG * 2 * L1_H
    weight = take("p (n w) -> p n w", n=NR, w=L1_E)
    small = k.load("L1_small", [(Iw, ins["L1_Iw"][:, :]), (Gw, ins["L1_Gw"][:, :]), (cols, ins["L1_cols"][:, :])] +
                   [(w, ins[n][:, :].rearrange("(c p) n -> p c n", p=P))
                    for w, n in ((Bw, "L1_Bw"), (Cw, "L1_Cw"), (Dw, "L1_Dw"), (Ow, "L1_Ow"))], after=region.free_after)
    big = k.load("L1_ffn", [(Wsd, ins["L1_Wsd"][:, :])] +
                 [(Wx[n], ins[f"L1_W{n}"][:, :].rearrange("p (e n) -> p e n", e=L1_E)) for n in ("q", "k", "v")] +
                 [(Wo[:, 0:2, :], ins["L1_Wo"][0:2 * P, :].rearrange("(c p) n -> p c n", p=P)),
                  (Wo[0:64, 2, :], ins["L1_Wo"][2 * P:, :])])
    const = [k.fill(one, 1.0, after=region.free_after)]
    for e in range(L1_E):
        const.append(k.fill(weight[:, :, e:e + 1], float(L1_E - e), after=region.free_after))
    in_b, gate_b, b_b, c_b, d_b, a_log = [cols[:, 2 * i:2 * i + 2] for i in range(6)]
    out_b, norm_w = cols[:, 12:13], cols[:, 13:14]
    t_a = k.act(a_log, a_log, ACT.Sigmoid, scale=-1.0, after=small)
    t_decay = [k.ts(decay[:, c, :], one, a_log[:, c:c + 1], None, ALU.mult, after=[t_a, const]) for c in range(2)]
    k.V.wait([const, t_decay, small])
    k.first_layernorm()

    def recurrence(g):
        x = k.cols(k.xn, g)
        sq, b = k.scratch.take(), k.banks.take()
        t = k.act(sq[:, :], x, ACT.Square, after=[k.xn_ready[g], sq.after])
        t = k.mm([(b[:, :], k.mean_w[:, :], sq[:, :])], after=[t, b.after])
        yield
        t = k.inverse_root(sq[:, :], b, k.eps[:, 1:2], t)
        t_r = k.stt(sq[:, :], x, norm_w, sq[:, :], ALU.mult, ALU.mult, after=[t, k.xn_ready[g]])
        xr = sq
        k.T.wait(small)
        u = []
        for c in range(2):
            s = k.scratch.take()
            bg, bu = k.banks.take(), k.banks.take()
            t_g = k.mm([(bg[:, :], Gw[:, c * P:(c + 1) * P], xr[:, :])], after=[t_r, bg.after])
            t_u = k.mm([(bu[:, :], Iw[:, c * P:(c + 1) * P], xr[:, :])], after=bu.after)
            t = k.act(s[:, :], bg[:, :], ACT.Sigmoid, bias=gate_b[:, c:c + 1], after=[t_g, s.after])
            k.banks.put(bg, t)
            t = k.stt(s[:, :], bu[:, :], in_b[:, c:c + 1], s[:, :], ALU.add, ALU.mult, after=[t_u, t])
            k.banks.put(bu, t)
            u.append((s, t))
            yield
        k.scratch.put(xr, t_u)
        ys = []
        for c in range(2):
            sl = slice(c * P, (c + 1) * P)
            bb, bc = k.banks.take(), k.banks.take()
            s, h = k.scratch.take(), k.scratch.take()
            t_b = k.mm([(bb[:, :], Bw[:, i, sl], u[i][0][:, :]) for i in range(2)], after=[u[0][1], u[1][1], bb.after])
            t_c = k.mm([(bc[:, :], Cw[:, i, sl], u[i][0][:, :]) for i in range(2)], after=bc.after)
            t = k.act(s[:, :], bb[:, :], ACT.Identity, bias=b_b[:, c:c + 1], after=[t_b, s.after])
            k.banks.put(bb, t)
            t = [k.scan(h[:, j * SEQ:(j + 1) * SEQ], decay[:, c, :], s[:, j * SEQ:(j + 1) * SEQ], after=[t, h.after])
                 for j in range(BPG)]
            t = k.stt(h[:, :], bc[:, :], c_b[:, c:c + 1], h[:, :], ALU.add, ALU.mult, after=[t, t_c])
            k.banks.put(bc, t)
            k.scratch.put(s, t)
            yield
            bd = k.banks.take()
            t_d = k.mm([(bd[:, :], Dw[:, i, sl], u[i][0][:, :]) for i in range(2)], after=bd.after)
            t = k.stt(h[:, :], bd[:, :], d_b[:, c:c + 1], h[:, :], ALU.add, ALU.add, after=[t, t_d])
            k.banks.put(bd, t)
            ys.append((h, t))
            yield
        for s, _ in u:
            k.scratch.put(s, t_d)
        b, s = k.banks.take(), k.scratch.take()
        t = k.mm([(b[:, :], Ow[:, i, :], ys[i][0][:, :]) for i in range(2)], after=[ys[0][1], ys[1][1], b.after])
        for y, _ in ys:
            k.scratch.put(y, t)
        s.token = k.stt(s[:, :], b[:, :], out_b, x, ALU.add, ALU.add, after=[t, s.after])
        k.banks.put(b, s.token)
        k.mixed[g] = s
        yield

    W = 2 * L1_H * L1_E
    NW = TPG * W
    heads = lambda a: a.rearrange("p (h d) -> p h d", d=L1_DH)
    routed, projected, gated_out, passed = {}, {}, {}, []

    def per_head(s, i, which, e):
        v = s[:, 0:NW].rearrange("p (n w h e) -> p n w h e", n=TPG, w=2, h=L1_H, e=L1_E)
        return v[:, i, which, :, e].unsqueeze(2).to_broadcast([P, L1_H, L1_DH])

    def route(g):
        k.T.wait(big)
        x = k.cols(k.xn, g)
        bank, sg, mk, sc, tmp, pick, col = [k.banks.take()] + [k.scratch.take() for _ in range(6)]
        t = k.mms([(bank[:, i * W:(i + 1) * W], x[:, i * P:(i + 1) * P], Wsd) for i in range(TPG)],
                  after=[bank.after, k.xn_ready[g]])
        t_s = k.act(sg[:, 0:NW], bank[:, 0:NW], ACT.Sigmoid, after=[t, sg.after])
        k.banks.put(bank, t_s)
        t = k.vcopy(sc[:, 0:NW], sg[:, 0:NW], after=[t_s, sc.after, tmp.after, pick.after, col.after, mk.after])
        t = top_mask(k, mk[:, 0:NW], sc[:, 0:NW], tmp[:, 0:NW], pick[:, 0:NW], col[:, 0:NR],
                     weight.rearrange("p n w -> p (n w)"), NR, L1_E, L1_K, after=t)
        t_g = k.tt(sg[:, 0:NW], sg[:, 0:NW], mk[:, 0:NW], ALU.mult, after=t)
        for s in (sc, tmp, pick, col):
            k.scratch.put(s, t_g)
        routed[g] = (sg, mk, t_g)

    def project(bt):
        g, b = bt // BPG, bt % BPG
        if b == 0:
            route(g)
        sg, mk, t_g = routed[g]
        x = k.cols(k.xn, g)
        turned = {"q": [k.scratch.take(), k.scratch.take()], "k": [k.scratch.take(), k.scratch.take()]}
        t_turned = {"q": [], "k": []}
        vs = []

        def product(u):
            i, kind, which, e = u["i"], u["kind"], u["which"], u["e"]
            bank, dst = k.banks.take(), k.scratch.take()
            t = k.mm([(bank[:, :], x[:, i * P:(i + 1) * P], Wx[kind][:, e, :])], after=bank.after)
            t = k.tt(heads(dst[:, :]), heads(bank[:, :]), per_head(sg, i, which, e), ALU.mult, after=[t, t_g, dst.after])
            k.banks.put(bank, t)
            u["dst"], u["t"] = dst, t

        def add(u):
            i, kind, e, dst, t = u["i"], u["kind"], u["e"], u["dst"], u["t"]
            if e == 0:
                u["all"]["sum"] = (dst, t)
            else:
                acc, t_acc = u["all"]["sum"]
                t = k.tt(acc[:, :], acc[:, :], dst[:, :], ALU.add, after=[t, t_acc], on=k.G)
                k.scratch.put(dst, t)
                u["all"]["sum"] = (acc, t)
            if kind == "v" and e == L1_E - 1:
                vs.append(u["all"]["sum"])

        def turn_sum(u):
            i, kind = u["i"], u["kind"]
            if kind == "v" or u["e"] < L1_E - 1:
                return
            acc, t = u["all"]["sum"]
            bank = k.banks.take()
            t = k.turn([(bank[:, m * P:(m + 1) * P], acc[:, m * P:(m + 1) * P]) for m in range(4)], after=[t, bank.after])
            k.scratch.put(acc, t)
            t2 = []
            for s in range(2):
                o = turned[kind][s]
                t2.append(k.acopy(o[:, :].rearrange("p (m t) -> p m t", t=SEQ)[:, :, (i % 2) * P:(i % 2 + 1) * P],
                                  bank[:, s * SEQ:(s + 1) * SEQ].rearrange("p (m t) -> p m t", t=P),
                                  scale=(L1_DH ** -0.5 if kind == "q" else 1.0), after=[t, o.after]))
            t_turned[kind] += t2
            k.banks.put(bank, t2)

        units = []
        for i in (2 * b, 2 * b + 1):
            for kind, which in (("q", 1), ("k", 0), ("v", 0)):
                shared = {}
                units += [{"i": i, "kind": kind, "which": which, "e": e, "all": shared} for e in range(L1_E)]
        yield from staged(units, (0, product), (1, add), (6, turn_sum))
        projected[bt] = (turned, t_turned, vs)

    def attend(bt):
        g, b = bt // BPG, bt % BPG
        sg, mk, t_g = routed[g]
        turned, t_turned, vs = projected.pop(bt)
        O = [k.banks.take(), k.banks.take()]
        rs = k.stats.take()
        rsv = rs[:, 0:2 * L1_H].rearrange("p (h i) -> p h i", i=2)
        done = []

        def scores(u):
            h = u["h"]
            m, r = h // 2, (h % 2) * L1_DH
            q, kk = [turned[n][m // 2][r:r + L1_DH, (m % 2) * SEQ:(m % 2 + 1) * SEQ] for n in ("q", "k")]
            u["p"], u["t"] = scores_exp(k, q, kk, [t_turned["q"], t_turned["k"], rs.after], rsv[:, h, :])
            u["sums"] = u["t"]

        def turn(u):
            u["pt"], u["t"] = turned_scores(k, u["p"], u["t"], u["h"] % 4 == 0)

        def times_v(u):
            h, pt = u["h"], u["pt"]
            for i in range(2):
                t = k.mm([(O[i][:, h * L1_DH:(h + 1) * L1_DH], pt[:, jc * SEQ + i * P:jc * SEQ + (i + 1) * P],
                           vs[jc][0][:, h * L1_DH:(h + 1) * L1_DH]) for jc in range(2)],
                         after=[u["t"], vs[0][1], vs[1][1], O[i].after])
            k.scratch.put(pt, t)
            done.append(t)

        units = [{"h": h} for h in range(L1_H)]
        yield from staged(units, (0, scores), (3, turn), (5, times_v))
        t_pv = done[-1]
        for s in turned["q"] + turned["k"] + [v for v, _ in vs]:
            k.scratch.put(s, t_pv)
        t_r = k.recip(rs[:, 0:2 * L1_H], rs[:, 0:2 * L1_H], after=[u["sums"] for u in units])
        if b == 0:
            gated_out[g] = [k.scratch.take(), []]
        fo, fo_tokens = gated_out[g]
        for i in range(2):
            n = 2 * b + i
            o, mixd = k.scratch.take(), k.scratch.take()
            t_o = k.tt(heads(o[:, :]), heads(O[i][:, :]), rsv[:, :, i].unsqueeze(2).to_broadcast([P, L1_H, L1_DH]),
                       ALU.mult, after=[t_pv, t_r, o.after])
            k.banks.put(O[i], t_o)
            ts = []
            for e in range(L1_E):
                tmp = k.scratch.take()
                t = k.tt(heads(tmp[:, :]), heads(o[:, :]), per_head(mk, n, 1, e), ALU.mult, after=[t_o, tmp.after], on=k.G)
                t2 = k.red(mixd[:, e * L1_DH:(e + 1) * L1_DH], tmp[:, :].rearrange("p (h d) -> p d h", d=L1_DH), ALU.add,
                           after=[t, mixd.after])
                k.scratch.put(tmp, t2)
                ts.append(t2)
                yield
            k.scratch.put(o, t)
            bank, at = k.banks.take(), k.scratch.take()
            pieces = ((0, P), (1, P), (2, L1_E * L1_DH - 2 * P))
            t = k.turn([(bank[0:w, c * P:(c + 1) * P], mixd[:, c * P:c * P + w]) for c, w in pieces], after=[ts, bank.after])
            k.scratch.put(mixd, t)
            t_c = [k.acopy(at[:, 0:2 * P], bank[:, 0:2 * P], after=[t, at.after]),
                   k.acopy(at[0:64, 2 * P:3 * P], bank[0:64, 2 * P:3 * P], after=t)]
            k.banks.put(bank, t_c)
            yield
            bank = k.banks.take()
            t = k.mm([(bank[:, 0:P], Wo[0:w, c, :], at[0:w, c * P:(c + 1) * P]) for c, w in pieces], after=[t_c, bank.after])
            k.scratch.put(at, t)
            t = k.acopy(fo[:, n * P:(n + 1) * P], bank[:, 0:P], after=[t, fo.after])
            k.banks.put(bank, t)
            fo_tokens.append(t)
            yield
        k.stats.put(rs, t_o)
        if b == BPG - 1:
            routed.pop(g)
            for s in (sg, mk):
                k.scratch.put(s, [t_g, ts, t_o])
            t = k.act(fo[:, :], fo[:, :], ACT.Silu, after=fo_tokens)
            yield from k.gate_and_add(g, None, t, k.mixed[g], silu=fo)
            passed.append(g)

    k.mixed = [None] * GROUPS
    attended = []

    def attend_and_count(bt):
        yield from attend(bt)
        attended.append(bt)

    run_lanes(Lane(2, [(lambda bt=bt: len(attended) >= bt - 1, lambda bt=bt: project(bt)) for bt in range(BATCH)]),
              Lane(1, [(lambda g=g: len(passed) >= g - 1, lambda g=g: recurrence(g)) for g in range(GROUPS)]),
              Lane(1, [(lambda bt=bt: bt in projected and k.mixed[bt // BPG] is not None, lambda bt=bt: attend_and_count(bt))
                       for bt in range(BATCH)]))
    return k.x_ready


def layouts1(a):
    T = lambda n: a[n].T
    cols = np.concatenate([columns(a["L1_attn_" + n]) for n in
                           ("in_b", "gate_b", "b_b", "c_b", "d_b", "a_log", "out_b", "norm_w")] +
                          [np.zeros((P, 2), np.float32)], axis=1)
    H, E, DH = L1_H, L1_E, L1_DH
    by_expert = lambda w: w.reshape(P, H, E, DH).transpose(0, 2, 1, 3).reshape(P, E * H * DH)
    kv = a["L1_ffn_Wkv"].reshape(P, 2, H * E * DH)
    return {"L1_Iw": T("L1_attn_in_w"), "L1_Gw": T("L1_attn_gate_w"), "L1_Bw": T("L1_attn_b_w"),
            "L1_Cw": T("L1_attn_c_w"), "L1_Dw": T("L1_attn_d_w"), "L1_Ow": T("L1_attn_out_w"), "L1_cols": cols,
            "L1_Wsd": np.concatenate([a["L1_ffn_Ws"], a["L1_ffn_Wd"]], axis=1),
            "L1_Wq": by_expert(a["L1_ffn_Wq"]), "L1_Wk": by_expert(kv[:, 0]), "L1_Wv": by_expert(kv[:, 1]),
            "L1_Wo": a["L1_ffn_Wo"].reshape(DH, E, P).transpose(1, 0, 2).reshape(E * DH, P)}


L2_HEADS, L2_DH = 16, 64
L2_PAIRS = L2_HEADS // 2
L2_FF = 2


def top2_gates(k, gates, pr, t_p, weight, spare, both=None):
    W = TILES * EXPERTS
    v3 = lambda s: s[:, 0:W].rearrange("p (n w) -> p n w", w=EXPERTS)
    sc, tmp, m1, m2, col = spare
    t = k.vcopy(sc[:, 0:W], pr[:, 0:W], after=[t_p, [s.after for s in spare]])
    t1 = k.one_hot_first(m1[:, 0:W], sc[:, 0:W], tmp[:, 0:W], col[:, 0:TILES], weight, TILES, EXPERTS, after=t)
    t = k.stt(sc[:, 0:W], m1[:, 0:W], -4.0, sc[:, 0:W], ALU.mult, ALU.add, after=t1)
    t2 = k.one_hot_first(m2[:, 0:W], sc[:, 0:W], tmp[:, 0:W], col[:, 0:TILES], weight, TILES, EXPERTS, after=t)
    if both is not None:
        return [t1, t2]
    t = k.tt(tmp[:, 0:W], m1[:, 0:W], m2[:, 0:W], ALU.add, after=[t1, t2])
    t = k.tt(gates, tmp[:, 0:W], pr[:, 0:W], ALU.mult, after=t)
    g3 = gates.rearrange("p (n w) -> p n w", w=EXPERTS)
    t = k.red(col[:, 0:TILES], g3, ALU.add, after=t)
    t = k.recip(col[:, 0:TILES], col[:, 0:TILES], after=t)
    return k.tt(g3, g3, col[:, 0:TILES].unsqueeze(2).to_broadcast([P, TILES, EXPERTS]), ALU.mult, after=t)


def layer2(k, region):
    nc, ins = k.nc, k.ins
    k.phase("L2")
    take = region.take
    Wqk = take("p (n) -> p n", n=P)
    Wv = take("p (n) -> p n", n=L2_DH)
    Fqk = take("p (n) -> p n", n=L2_HEADS * L2_DH)
    Fv = take("p (n) -> p n", n=L2_HEADS * L2_DH)
    Fv_b = take("p (n) -> p n", n=L2_HEADS * L2_DH)
    Fo = take("p (c n) -> p c n", c=L2_PAIRS, n=P)
    cols = take("p (n) -> p n", n=2 * L2_PAIRS + 1)
    W1 = take("p (e f) -> p e f", e=EXPERTS, f=L2_FF * P)
    W2 = take("p (e c d) -> p e c d", e=EXPERTS, c=L2_FF, d=P)
    b1 = take("p (n) -> p n", n=EXPERTS * L2_FF)
    b2 = take("p (n) -> p n", n=P)[0:EXPERTS, :]
    Wg = take("p (n) -> p n", n=EXPERTS)
    gates = take("p (n) -> p n", n=TILES * EXPERTS)
    weight = take("p (n w) -> p n w", n=TILES, w=EXPERTS)
    loaded = k.load("L2", [(Wg, ins["L2_Wg"][:, :]), (Wqk, ins["L2_Wqk"][:, :]), (Wv, ins["L2_Wv"][:, :]),
                           (cols, ins["L2_cols"][:, :]), (Fqk, ins["L2_Fqk"][:, :]), (Fv[0:L2_DH, :], ins["L2_Fv"][:, :]),
                           (Fv_b, ins["L2_Fv_b"][:, :].broadcast_to([P, L2_HEADS * L2_DH])),
                           (Fo, ins["L2_Fo"][:, :].rearrange("(c p) n -> p c n", p=P))], after=region.free_after)
    big = k.load("L2_experts", [(b1, ins["L2_b1"][:, :]), (b2, ins["L2_b2"][:, :]),
                                (W1, ins["L2_W1"].rearrange("e d f -> d e f"))] +
                 [(W2[:, e, :, :], ins["L2_W2"][e, :, :].rearrange("(c p) d -> p c d", p=P)) for e in range(EXPERTS)])
    fq_b, fk_b, fo_b = cols[:, 0:8], cols[:, 8:16], cols[:, 16:17]
    const = [k.fill(weight[:, :, e:e + 1], float(EXPERTS - e), after=region.free_after) for e in range(EXPERTS)]
    k.first_layernorm()
    k.V.wait([const, loaded])
    k.A.wait(loaded)
    k.T.wait(loaded)
    lg, pr, t_p = k.softmax_experts("L2", Wg, loaded)
    k.scratch.put(lg, t_p)
    spare = [k.scratch.take() for _ in range(5)]
    t_gates = top2_gates(k, gates, pr, t_p, weight.rearrange("p n w -> p (n w)"), spare)
    for s in spare + [pr]:
        k.scratch.put(s, t_gates)
    gate_rows = k.gates_to_rows(gates, "L2", t_gates)

    def attention(g):
        x = k.cols(k.xn, g)
        bz, bv, zqk, zv = k.banks.take(), k.banks.take(), k.scratch.take(), k.scratch.take()
        t = k.mm([(bz[:, :], Wqk, x)], after=[bz.after, k.xn_ready[g]])
        t_z = k.acopy(zqk[:, :], bz[:, :], after=[t, zqk.after])
        t = k.mm([(bv[0:L2_DH, :], Wv, x)], after=bv.after)
        t_zv = k.acopy(zv[0:L2_DH, :], bv[0:L2_DH, :], after=[t, zv.after])
        k.banks.put(bz, t_z)
        k.banks.put(bv, t_zv)
        yield
        v = [[None, None] for _ in range(TPG)]
        for i in range(TPG):
            for c in range(2):
                b, s = k.banks.take(), k.scratch.take()
                t_fv = k.mm([(b[:, :], zv[0:L2_DH, i * P:(i + 1) * P], Fv[0:L2_DH, c * GW:(c + 1) * GW])], after=[b.after, t_zv])
                t = k.tt(s[:, :], b[:, :], Fv_b[:, c * GW:(c + 1) * GW], ALU.add, after=[t_fv, s.after])
                k.banks.put(b, t)
                v[i][c] = (s, t)
                yield
        k.scratch.put(zv, t_fv)
        acc = k.banks.take()
        pairs, state = {}, {}

        def scores(u):
            m, b, half = u["m"], u["b"], u["half"]
            if b == 0 and half == 0:
                qk = []
                for r, bias, scale in ((0, fq_b, L2_DH ** -0.5), (L2_DH, fk_b, 1.0)):
                    bk, s = k.banks.take(), k.scratch.take()
                    t = k.mm([(bk[:, :], Fqk[r:r + L2_DH, m * P:(m + 1) * P], zqk[r:r + L2_DH, :])], after=[bk.after, t_z])
                    t = k.ts(s[:, :], bk[:, :], bias[:, m:m + 1], scale, ALU.add, ALU.mult, after=[t, s.after])
                    k.banks.put(bk, t)
                    qk.append((s, t))
                pairs[m] = {"qk": qk}
            qk = pairs[m]["qk"]
            r, sl = half * L2_DH, slice(b * SEQ, (b + 1) * SEQ)
            rs = k.stats.take()
            p, t_e = scores_exp(k, qk[0][0][r:r + L2_DH, sl], qk[1][0][r:r + L2_DH, sl], [qk[0][1], qk[1][1], rs.after], rs[:, 0:2])
            t_r = k.recip(rs[:, 0:2], rs[:, 0:2], after=t_e)
            u["p"] = p
            u["t"] = [k.ts(p[:, i * SEQ:(i + 1) * SEQ], p[:, i * SEQ:(i + 1) * SEQ], rs[:, i:i + 1], None, ALU.mult,
                           after=[t_r, t_e]) for i in range(2)]
            k.stats.put(rs, u["t"])

        def turn(u):
            u["pt"], u["t"] = turned_scores(k, u["p"], u["t"], (2 * u["m"] + u["half"]) % 2 == 0)

        def times_v(u):
            m, b, half = u["m"], u["b"], u["half"]
            if b == 0 and half == 0:
                pairs[m]["O"] = k.banks.take()
            O = pairs[m]["O"]
            h = 2 * m + half
            cs = slice((h % 8) * L2_DH, (h % 8 + 1) * L2_DH)
            r = half * L2_DH
            vv = [v[2 * b + jc][h // 8] for jc in range(2)]
            t = k.mm([(O[r:r + L2_DH, b * SEQ:(b + 1) * SEQ], vv[jc][0][:, cs], u["pt"][:, jc * SEQ:(jc + 1) * SEQ])
                      for jc in range(2)], after=[u["t"], vv[0][1], vv[1][1], O.after])
            k.scratch.put(u["pt"], t)
            if b == BPG - 1 and half == 1:
                s = k.scratch.take()
                pairs[m]["s"], pairs[m]["t"] = s, k.acopy(s[:, :], O[:, :], after=[t, s.after])
                k.banks.put(O, pairs[m]["t"])
                for q, _ in pairs[m]["qk"]:
                    k.scratch.put(q, t)

        def fold(u):
            m = u["m"]
            if u["b"] == BPG - 1 and u["half"] == 1:
                state["t"] = k.mm([(acc[:, :], Fo[:, m, :], pairs[m]["s"][:, :])],
                                  after=[pairs[m]["t"]] + ([acc.after] if m == 0 else []),
                                  start=(m == 0), stop=(m == L2_PAIRS - 1))
                k.scratch.put(pairs[m]["s"], state["t"])

        units = [{"m": m, "b": b, "half": half} for m in range(L2_PAIRS) for b in range(BPG) for half in range(2)]
        yield from staged(units, (0, scores), (4, turn), (6, times_v), (8, fold))
        k.scratch.put(zqk, state["t"])
        for i in range(TPG):
            for s, _ in v[i]:
                k.scratch.put(s, state["t"])
        s = k.scratch.take()
        s.token = k.act(s[:, :], acc[:, :], ACT.Identity, bias=fo_b, after=[state["t"], s.after])
        k.banks.put(acc, s.token)
        k.mixed[g] = s
        yield

    def ffn(g):
        k.T.wait(big)
        acc = k.banks.take()

        def hidden(e, f, x, gate):
            b, s = k.banks.take(), k.scratch.take()
            t = k.mm([(b[:, :], W1[:, e, f * P:(f + 1) * P], x)], after=b.after)
            n = e * L2_FF + f
            t = k.act(s[:, :], b[:, :], ACT.Relu, bias=b1[:, n:n + 1], after=[t, s.after, big])
            k.banks.put(b, t)
            return s, k.tt(s[:, :], s[:, :], gate[:, :], ALU.mult, after=[t, gate.token])

        yield from k.experts(g, gate_rows, acc, L2_FF, hidden, lambda e, f: W2[:, e, f, :], b2, after=big)
        yield from k.gate_and_add(g, acc, k.t_acc[g], k.mixed[g])

    run_layer(k, attention, ffn, 2, 1)
    return k.x_ready


def layouts2(a):
    return {"L2_Wqk": np.concatenate([a["L2_attn_wq"], a["L2_attn_wk"]], axis=1), "L2_Wv": a["L2_attn_wv"],
            "L2_Fqk": np.concatenate([a["L2_attn_fcq_w"], a["L2_attn_fck_w"]], axis=0), "L2_Fv": a["L2_attn_fcv_w"],
            "L2_Fv_b": a["L2_attn_fcv_b"].reshape(1, -1), "L2_Fo": a["L2_attn_fco_w"],
            "L2_cols": np.concatenate([columns(a["L2_attn_" + n]) for n in ("fcq_b", "fck_b", "fco_b")], axis=1),
            "L2_Wg": a["L2_ffn_Wg"], "L2_W1": a["L2_ffn_W1"], "L2_W2": a["L2_ffn_W2"],
            "L2_b1": columns(a["L2_ffn_b1"]), "L2_b2": a["L2_ffn_b2"]}


L3_H, L3_D = 4, 32
L3_CONV = 4
L3_FIRS = (3, 15, 63)
L3_LMAX = max(L3_FIRS)
L3_CHUNK = 32
L3_CPT = P // L3_CHUNK
L3_CHUNKS = SEQ // L3_CHUNK
L3_PATHS = 5
L3_LEVELS = 5
L3_FF = 2
L3_CAPACITY = -(-2 * TOKENS * 5 // (EXPERTS * 4))
L3_PE_TAPS = 12


def l3_constants():
    r, c = np.arange(P)[:, None], np.arange(P)[None, :]
    same = r // L3_CHUNK == c // L3_CHUNK
    masks = [(r >> (n + 1) == c >> (n + 1)) & ((r >> n) % 2 == 0) & ((c >> n) % 2 == 1) for n in range(L3_LEVELS)]
    masks.append(same & (r <= c))
    masks.append(same)
    masks.append(r < c)
    path = np.zeros((P, L3_PATHS, P), np.float32)
    for h in range(L3_H):
        for p in range(L3_PATHS):
            path[h * L3_PATHS + p, p, h * L3_D:(h + 1) * L3_D] = 1.0
    return np.concatenate([np.concatenate(masks, axis=1).astype(np.float32), path.reshape(P, -1)], axis=1)


def layer3(k, region, filters):
    nc, ins = k.nc, k.ins
    k.phase("L3")
    take = region.take
    Wqkv = take("p (n) -> p n", n=3 * P)
    Wo = take("p (n) -> p n", n=P)
    Wb = take("p (n) -> p n", n=L3_H)
    taps = take("p (n) -> p n", n=3 * L3_CONV + sum(L3_FIRS) + 1)
    GW_ = take("p (n) -> p n", n=L3_H * L3_PATHS)
    row = take("p (n) -> p n", n=L3_H * (L3_PATHS + 2))
    consts = take("p (n) -> p n", n=8 * P + L3_PATHS * P)
    mask = [consts[:, i * P:(i + 1) * P] for i in range(8)]
    path = consts[:, 8 * P:].rearrange("p (q n) -> p q n", q=L3_PATHS)[0:L3_H * L3_PATHS]
    causal, head_block, earlier = mask[5], mask[6], mask[7]
    Wbx = take("p (h d) -> p h d", h=L3_H, d=L3_D)
    head_mean = take("p (n) -> p n", n=P)
    all_ones = take("p (n) -> p n", n=P)
    W1 = take("p (e f) -> p e f", e=EXPERTS, f=2 * L3_FF * P)
    W2 = take("p (e c d) -> p e c d", e=EXPERTS, c=L3_FF, d=P)
    Wg = take("p (n) -> p n", n=EXPERTS)
    gates = take("p (n) -> p n", n=TILES * EXPERTS)
    weight = take("p (n w) -> p n w", n=TILES, w=EXPERTS)
    NP = L3_H * L3_PATHS
    probs = take("p (n) -> p n", n=TILES * NP)
    diag = filters.take("p (j n) -> p j n", j=L3_PE_TAPS, n=P)
    loaded = k.load("L3", [(Wqkv, ins["L3_Wqkv"][:, :]), (Wo, ins["L3_Wo"][:, :]), (Wb, ins["L3_Wb"][:, :]),
                           (taps, ins["L3_taps"][:, :]), (GW_, ins["L3_gate_w"][:, :]), (consts, ins["L3_consts"][:, :]),
                           (row, ins["L3_row"][:, :].broadcast_to([P, L3_H * (L3_PATHS + 2)])), (Wg, ins["L3_Wg"][:, :])],
                    after=region.free_after)
    big = k.load("L3_experts", [(W1, ins["L3_W1"].rearrange("e d f -> d e f"))] +
                 [(W2[:, e, :, :], ins["L3_W2"][e, :, :].rearrange("(c p) d -> p c d", p=P)) for e in range(EXPERTS)])
    free = region.free_after
    const = [k.fill(weight[:, :, e:e + 1], float(EXPERTS - e), after=free) for e in range(EXPERTS)]
    const.append(k.fill(all_ones, 1.0, after=free))
    const.append(k.ts(head_mean, head_block, 1.0 / L3_D, None, ALU.mult, after=[loaded, free]))
    const.append(k.vcopy(Wbx, Wb.unsqueeze(2).to_broadcast([P, L3_H, L3_D]), after=[loaded, free]))
    conv_w = [taps[:, i * L3_CONV:(i + 1) * L3_CONV] for i in range(3)]
    fir_at = [3 * L3_CONV + sum(L3_FIRS[:i]) for i in range(3)]
    fir_w = [taps[:, a:a + n] for a, n in zip(fir_at, L3_FIRS)]
    norm_w = taps[:, fir_at[2] + L3_FIRS[2]:fir_at[2] + L3_FIRS[2] + 1]
    for j in range(L3_PE_TAPS):
        const.append(k.ts(diag[:, j, :], k.ident[:, :], fir_w[2][:, j:j + 1], None, ALU.mult, after=[loaded, filters.free_after]))
    CP, VP = L3_CONV - 1, L3_LMAX - 1
    pads = Pool([Slot(filters.take("p (b t) -> p b t", b=BPG, t=CP + SEQ), i) for i in range(2)])
    vpads = Pool([Slot(filters.take("p (b t) -> p b t", b=BPG, t=VP + SEQ), i) for i in range(2)])
    for s in pads.free:
        s.after = flat([k.fill(s[:, :, 0:CP], 0.0, after=filters.free_after), filters.free_after])
    for s in vpads.free:
        s.after = flat([k.fill(s[:, :, 0:VP], 0.0, after=filters.free_after), filters.free_after])
    gate_b, log_t, eps = row[:, 0:NP], row[:, NP:NP + L3_H], row[:, NP + L3_H:NP + 2 * L3_H]
    rs = k.scratch.take()
    inv_t, keep = rs[:, 0:L3_H], rs[:, L3_H:2 * L3_H]
    t1 = k.act(inv_t, log_t, ACT.Exp, scale=-1.0, after=[loaded, rs.after])
    t = k.ts(eps, eps, 0.0, 0.2, ALU.max, ALU.min, after=loaded)
    t2 = k.ts(keep, eps, -5.0, 1.0, ALU.mult, ALU.add, after=[t, rs.after])
    k.V.wait([const, loaded, t1, t2])
    k.T.wait([const, loaded])
    k.first_layernorm()

    HT = 16
    for half in range(TILES // HT):
        bank, cl = k.banks.take(), k.scratch.take()
        n = HT * NP
        t = k.mms([(bank[:, i * NP:(i + 1) * NP], k.xn[:, (half * HT + i) * P:(half * HT + i + 1) * P], GW_)
                   for i in range(HT)], after=[bank.after, k.xn_ready])
        pr = probs[:, half * n:(half + 1) * n]
        rows = pr.rearrange("p (n w) -> p n w", w=L3_PATHS)
        c = cl[:, 0:HT * L3_H]
        bc = c.unsqueeze(2).to_broadcast([P, HT * L3_H, L3_PATHS])
        by_tile = pr.rearrange("p (i n) -> p i n", i=HT)
        t = k.tt(by_tile, bank[:, 0:n].rearrange("p (i n) -> p i n", i=HT), gate_b.unsqueeze(1).to_broadcast([P, HT, NP]),
                 ALU.add, after=[t, free])
        k.banks.put(bank, t)

        def per_head(v, op, t):
            toks = []
            for h in range(L3_H):
                a = by_tile[:, :, h * L3_PATHS:(h + 1) * L3_PATHS]
                toks.append(k.ts(a, a, v[:, h:h + 1], None, op, after=t))
            return toks
        t = per_head(inv_t, ALU.mult, t)
        t = k.red(c, rows, ALU.max, after=[t, cl.after])
        t = k.tt(rows, rows, bc, ALU.subtract, after=t)
        t_e = k.act(pr, pr, ACT.Exp, after=t)
        t = k.red(c, rows, ALU.add, after=[t_e, t])
        t = k.recip(c, c, after=t)
        t = k.tt(rows, rows, bc, ALU.mult, after=t)
        k.scratch.put(cl, t)
        t = per_head(keep, ALU.mult, t)
        t_probs = per_head(eps, ALU.add, t)
    k.scratch.put(rs, t_probs)

    W = TILES * EXPERTS
    v3 = lambda a: a.rearrange("p (n w) -> p n w", w=EXPERTS)
    lg, pr, t_p = k.softmax_experts("L3", Wg, loaded)
    k.scratch.put(lg, t_p)
    spare = [k.scratch.take() for _ in range(5)]
    sc, tmp, m1, m2, col = spare
    t = top2_gates(k, None, pr, t_p, weight.rearrange("p n w -> p (n w)"), spare, both=True)
    total = k.scratch.take()
    base = None
    kept = []
    for which, m in enumerate((m1, m2)):
        loc, tot = k.banks.take(), k.banks.take()
        t_l = k.mm([(loc[:, 0:W], earlier, m[:, 0:W])], after=[t, loc.after])
        t_t = k.mm([(tot[:, 0:W], all_ones, m[:, 0:W])], after=[t, tot.after])
        t_c = k.vcopy(sc[:, 0:W], tot[:, 0:W], after=[t_t, kept])
        t_s = [k.scan(tmp[:, e:W:EXPERTS], all_ones[:, 0:TILES], sc[:, e:W:EXPERTS], after=[t_c, kept])
               for e in range(EXPERTS)]
        t_x = k.tt(sc[:, 0:W], tmp[:, 0:W], sc[:, 0:W], ALU.subtract, after=t_s)
        t_x = k.tt(sc[:, 0:W], sc[:, 0:W], loc[:, 0:W], ALU.add, after=[t_x, t_l])
        if which == 1:
            t_x = k.tt(v3(sc[:, 0:W]), v3(sc[:, 0:W]), total[:, 0:EXPERTS].unsqueeze(1).to_broadcast([P, TILES, EXPERTS]),
                       ALU.add, after=[t_x, base])
        else:
            base = k.vcopy(total[:, 0:EXPERTS], tmp[:, W - EXPERTS:W], after=[t_s, total.after])
        k.banks.put(loc, t_x)
        k.banks.put(tot, t_c)
        t_k = k.stt(m[:, 0:W], sc[:, 0:W], float(L3_CAPACITY), m[:, 0:W], ALU.is_lt, ALU.mult, after=[t_x, t_l, t_t])
        kept = [kept, t_k, base]
    t = k.tt(sc[:, 0:W], m1[:, 0:W], m2[:, 0:W], ALU.add, after=kept)
    t = k.tt(gates, sc[:, 0:W], pr[:, 0:W], ALU.mult, after=[t, free])
    t = k.red(col[:, 0:TILES], v3(gates), ALU.add, after=t)
    t = k.ts(col[:, 0:TILES], col[:, 0:TILES], 1e-9, None, ALU.max, after=t)
    t = k.recip(col[:, 0:TILES], col[:, 0:TILES], after=t)
    t_gates = k.tt(v3(gates), v3(gates), col[:, 0:TILES].unsqueeze(2).to_broadcast([P, TILES, EXPERTS]), ALU.mult, after=t)
    for s in spare + [pr, total]:
        k.scratch.put(s, t_gates)
    gate_rows = k.gates_to_rows(gates, "L3", t_gates)

    four = lambda m: m.unsqueeze(1).to_broadcast([P, TPG, P])
    tiles = lambda a: a.rearrange("p (i n) -> p i n", n=P)
    batches = lambda a: a.rearrange("p (b t) -> p b t", b=BPG)

    def unit_rows(s, t, eps_col, weights, scale_col=None):
        sq, b = k.scratch.take(), k.banks.take()
        t1 = k.act(sq[:, :], s[:, :], ACT.Square, after=[t, sq.after])
        t1 = k.mm([(b[:, :], weights, sq[:, :])], after=[t1, b.after])
        t1 = k.inverse_root(sq[:, :], b, eps_col, t1)
        if scale_col is None:
            t1 = k.tt(s[:, :], s[:, :], sq[:, :], ALU.mult, after=[t1, t])
        else:
            t1 = k.stt(s[:, :], s[:, :], scale_col, sq[:, :], ALU.mult, ALU.mult, after=[t1, t])
        k.scratch.put(sq, t1)
        return t1

    prepared = {}

    def prepare(g):
        x = k.cols(k.xn, g)
        rows = []
        for n in range(3):
            b, pad, s = k.banks.take(), pads.take(), k.scratch.take()
            t = k.mm([(b[:, :], Wqkv[:, n * P:(n + 1) * P], x)], after=[b.after, k.xn_ready[g]])
            t = k.acopy(pad[:, :, CP:], batches(b[:, :]), after=[t, pad.after])
            k.banks.put(b, t)
            t = k.ts(batches(s[:, :]), pad[:, :, 0:SEQ], conv_w[n][:, 0:1], None, ALU.mult, after=[t, s.after])
            for j in range(1, L3_CONV):
                t = k.stt(batches(s[:, :]), pad[:, :, j:j + SEQ], conv_w[n][:, j:j + 1], batches(s[:, :]), ALU.mult, ALU.add,
                          after=t)
            pads.put(pad, t)
            if n < 2:
                t = k.act(s[:, :], s[:, :], ACT.Silu, after=t)
                rows.append((s, t))
            else:
                v = vpads.take()
                t = k.act(v[:, :, VP:], batches(s[:, :]), ACT.Silu, after=[t, v.after])
                k.scratch.put(s, t)
                t_v = t
                values[g] = (v, t_v)
            yield
        (q, t_q), (kk, t_k) = rows
        t_q = unit_rows(q, t_q, k.eps[:, 1:2], head_block)
        yield
        t_k = unit_rows(kk, t_k, k.eps[:, 1:2], head_block)
        yield
        b, beta, kb, vb = k.banks.take(), k.scratch.take(), k.scratch.take(), k.scratch.take()
        t = k.mm([(b[:, :], Wbx.rearrange("p h d -> p (h d)"), x)], after=b.after)
        t = k.act(beta[:, :], b[:, :], ACT.Sigmoid, after=[t, beta.after])
        k.banks.put(b, t)
        t_kb = k.tt(kb[:, :], kk[:, :], beta[:, :], ALU.mult, after=[t, t_k, kb.after])
        t_vb = k.tt(batches(vb[:, :]), v[:, :, VP:], batches(beta[:, :]), ALU.mult, after=[t, t_v, vb.after])
        k.scratch.put(beta, [t_kb, t_vb])
        yield
        nat = []
        for s, t in ((kk, t_k), (kb, t_kb), (vb, t_vb)):
            b, o = k.banks.take(), k.scratch.take()
            t = k.turn([(b[:, i * P:(i + 1) * P], s[:, i * P:(i + 1) * P]) for i in range(TPG)], after=[t, b.after])
            t2 = k.acopy(o[:, :], b[:, :], after=[t, o.after])
            k.banks.put(b, t2)
            nat.append((o, t2))
            yield
        k.scratch.put(vb, t)
        (k_nat, t_kn), (kb_nat, t_kbn), (vb_nat, t_vbn) = nat
        u, w = k.scratch.take(), k.scratch.take()
        t_u, t_w = [], []

        def inverse(h):
            r = slice(h * L3_D, (h + 1) * L3_D)
            b, gram, inv, invT, lm = k.banks.take(), *[k.scratch.take() for _ in range(4)]
            t = k.mms([(b[:, i * P:(i + 1) * P], kk[r, i * P:(i + 1) * P], kb[r, i * P:(i + 1) * P]) for i in range(TPG)],
                      after=[t_k, t_kb, b.after])
            gram_read.append(t)
            t_g = k.acopy(gram[:, :], b[:, :], after=[t, gram.after])
            k.banks.put(b, t_g)
            yield
            t = k.tt(tiles(lm[:, :]), tiles(gram[:, :]), four(mask[0]), ALU.mult, after=[t_g, lm.after], on=k.G)
            t_lm = k.G.run(lambda eng: eng.tensor_tensor(tiles(invT[:, :]), four(k.ident[:, :]), tiles(lm[:, :]), ALU.subtract),
                           [t, invT.after])
            t_T = t_lm
            t_i = k.V.run(lambda eng: eng.transpose(inv[:, :], invT[:, :]), [t_T, inv.after])
            t_read = t_lm
            yield
            for n in range(1, L3_LEVELS):
                t_lm = k.tt(tiles(lm[:, :]), tiles(gram[:, :]), four(mask[n]), ALU.mult, after=t_read, on=k.G)
                bx, xs = k.banks.take(), k.scratch.take()
                t = k.mms([(bx[:, i * P:(i + 1) * P], lm[:, i * P:(i + 1) * P], inv[:, i * P:(i + 1) * P]) for i in range(TPG)],
                          after=[t_lm, t_i, bx.after])
                t_read = t
                t = k.acopy(xs[:, :], bx[:, :], after=[t, xs.after])
                k.banks.put(bx, t)
                yield
                by = k.banks.take()
                t_y = k.mms([(by[:, i * P:(i + 1) * P], invT[:, i * P:(i + 1) * P], xs[:, i * P:(i + 1) * P]) for i in range(TPG)],
                            after=[t, t_T, by.after])
                k.scratch.put(xs, t_y)
                t_i = k.tt(inv[:, :], inv[:, :], by[:, :], ALU.subtract, after=[t_y, t_i, t_read])
                k.banks.put(by, t_i)
                t_T = k.V.run(lambda eng: eng.transpose(invT[:, :], inv[:, :]), [t_i, t_y])
                yield
            k.scratch.put(gram, t_lm)
            k.scratch.put(lm, t_read)
            k.scratch.put(inv, t_T)
            cs = slice(h * L3_D, (h + 1) * L3_D)
            bu, bw = k.banks.take(), k.banks.take()
            of_head = lambda a: tiles(a)[:, :, cs]
            tu = k.mms([(bu[:, i * L3_D:(i + 1) * L3_D], invT[:, i * P:(i + 1) * P], vb_nat[:, i * P + h * L3_D:i * P + (h + 1) * L3_D])
                        for i in range(TPG)], after=[t_T, t_vbn, bu.after])
            tw = k.mms([(bw[cs, i * P:(i + 1) * P], kb_nat[:, i * P + h * L3_D:i * P + (h + 1) * L3_D], invT[:, i * P:(i + 1) * P])
                        for i in range(TPG)], after=[t_T, t_kbn, bw.after])
            t_u.append(k.acopy(of_head(u[:, :]), bu[:, 0:TPG * L3_D].rearrange("p (i d) -> p i d", d=L3_D), after=[tu, u.after]))
            t_w.append(k.acopy(w[cs, :], bw[cs, :], after=[tw, w.after]))
            k.banks.put(bu, t_u[-1])
            k.banks.put(bw, t_w[-1])
            k.scratch.put(invT, [tu, tw])
            done.append([tu, tw])
            yield

        gram_read, done = [], []
        for pair in ((0, 1), (2, 3)):
            two = [inverse(h) for h in pair]
            live = list(two)
            while live:
                for gen in list(live):
                    if next(gen, "end") == "end":
                        live.remove(gen)
                yield
        k.scratch.put(kb, gram_read)
        k.scratch.put(kb_nat, done)
        k.scratch.put(vb_nat, done)
        prepared[g] = dict(q=(q, t_q), k=(kk, [t_k, gram_read]), k_nat=(k_nat, t_kn), u=(u, t_u), w=(w, t_w))
        yield

    def path_rows(g):
        b, pt = k.banks.take(), k.scratch.take()
        t = k.turn([(b[0:NP, i * P:(i + 1) * P], probs[:, (TPG * g + i) * NP:(TPG * g + i + 1) * NP]) for i in range(TPG)],
                   after=[b.after, t_probs])
        t_pt = k.acopy(pt[0:NP, :], b[0:NP, :], after=[t, pt.after])
        k.banks.put(b, t_pt)
        return pt, t_pt

    def filters_of(g):
        v, t_v = values.pop(g)
        pt, t_pt = path_rows(g)
        yield
        o = k.scratch.take()
        state = {"t": None}

        def add_path(p, value, t_value):
            b = k.banks.take()
            t = k.mm([(b[:, :], path[:, p, :], pt[0:NP, :])], after=[t_pt, b.after])
            dst = o if state["t"] is None else k.scratch.take()
            t = k.tt(batches(dst[:, :]), batches(b[:, :]), value, ALU.mult, after=[t, t_value, dst.after])
            k.banks.put(b, t)
            used = t
            if dst is not o:
                t = k.tt(o[:, :], o[:, :], dst[:, :], ALU.add, after=[t, state["t"]], on=k.G)
                k.scratch.put(dst, t)
            state["t"] = t
            return used

        add_path(4, v[:, :, VP:], t_v)
        yield
        for n, K in enumerate(L3_FIRS):
            s = k.scratch.take()
            on_pe = L3_PE_TAPS if n == 2 else 0
            t_f = None
            if on_pe:
                b = k.banks.take()
                for j0 in range(0, on_pe, 3):
                    j1 = min(on_pe, j0 + 3)
                    t_f = k.mm([(b[:, :], diag[:, j, :], v[:, :, VP - K + 1 + j:VP - K + 1 + j + SEQ]) for j in range(j0, j1)],
                               after=[t_v, b.after], start=(j0 == 0), stop=(j1 == on_pe))
                    yield
            t = None
            for j in range(on_pe, K):
                src = v[:, :, VP - K + 1 + j:VP - K + 1 + j + SEQ]
                if t is None and not on_pe:
                    t = k.ts(batches(s[:, :]), src, fir_w[n][:, j:j + 1], None, ALU.mult, after=[s.after, t_v])
                else:
                    prev = batches(b[:, :]) if t is None else batches(s[:, :])
                    t = k.stt(batches(s[:, :]), src, fir_w[n][:, j:j + 1], prev, ALU.mult, ALU.add,
                              after=[t, s.after, t_v, t_f])
                    if on_pe and j == on_pe:
                        k.banks.put(b, t)
                if j % 3 == 2:
                    yield
            t = add_path(n, batches(s[:, :]), t)
            k.scratch.put(s, t)
            yield
        vpads.put(v, t)
        k.scratch.put(pt, t)
        filtered[g] = (o, state["t"])

    values, filtered = {}, {}

    def recur(g):
        d = prepared.pop(g)
        (q, t_q), (kk, t_k), (k_nat, t_kn), (u, t_u), (w, t_w) = d["q"], d["k"], d["k_nat"], d["u"], d["w"]
        S = [k.scratch.take(), k.scratch.take()]
        t_S = k.fill(S[0][:, 0:BPG * P], 0.0, after=S[0].after)
        t_read = [[], S[1].after]
        s_bank, o_bank, w_bank = k.banks.take(), k.banks.take(), k.banks.take()
        t_o = []
        t_wread = w_bank.after
        for c in range(L3_CHUNKS):
            cur, nxt = S[c % 2], S[(c + 1) % 2]
            ci, tl = c % L3_CPT, c // L3_CPT
            r = slice(ci * L3_CHUNK, (ci + 1) * L3_CHUNK)
            at = lambda b: (TPG // BPG * b + tl) * P + ci * L3_CHUNK
            rd = []
            if c > 0:
                t = k.mms([(w_bank[r, b * P:(b + 1) * P], w[:, at(b):at(b) + L3_CHUNK], cur[:, b * P:(b + 1) * P])
                           for b in range(BPG)], after=[t_S, t_w, t_wread])
                rd.append(t)
                uu = tiles(u[:, :])[r, tl::TPG // BPG, :]
                t_u = [t_u, k.tt(uu, uu, w_bank[r, 0:BPG * P].rearrange("p (b n) -> p b n", b=BPG), ALU.subtract, after=[t, t_u])]
                t_wread = t_u[1]
            t = k.mms([(o_bank[:, at(b):at(b) + L3_CHUNK], cur[:, b * P:(b + 1) * P], q[:, at(b):at(b) + L3_CHUNK])
                       for b in range(BPG)], after=[t_S, t_q, o_bank.after])
            rd.append(t)
            t_o.append(t)
            t_read[c % 2] = rd
            yield
            if c < L3_CHUNKS - 1:
                for b in range(BPG):
                    col = (TPG // BPG * b + tl) * P
                    t = k.mm([(s_bank[:, b * P:(b + 1) * P], k_nat[r, col:col + P], u[r, col:col + P])],
                             after=[t_u, t_kn, s_bank.after], start=(c == 0 and b == 0), stop=(c == L3_CHUNKS - 2))
                t_S = k.tt(nxt[:, 0:BPG * P].rearrange("p (b n) -> p b n", b=BPG),
                           s_bank[:, 0:BPG * P].rearrange("p (b n) -> p b n", b=BPG),
                           head_block.unsqueeze(1).to_broadcast([P, BPG, P]), ALU.mult, after=[t, t_read[(c + 1) % 2]])
                k.T.wait(t_S)
                yield
        k.banks.put(s_bank, t_S)
        k.banks.put(w_bank, t_wread)
        for s in S:
            k.scratch.put(s, t_read)
        k.scratch.put(w, t_read)
        k.scratch.put(k_nat, t_S)
        b, dl = k.banks.take(), k.scratch.take()
        t_i = []

        def chunk_scores(h):
            r = slice(h["h"] * L3_D, (h["h"] + 1) * L3_D)
            bs, s = k.banks.take(), k.scratch.take()
            t = k.mms([(bs[:, i * P:(i + 1) * P], kk[r, i * P:(i + 1) * P], q[r, i * P:(i + 1) * P]) for i in range(TPG)],
                      after=[t_k, t_q, bs.after])
            h["read"] = t
            h["s"], h["t"] = s, k.tt(tiles(s[:, :]), tiles(bs[:, :]), four(causal), ALU.mult, after=[t, s.after])
            k.banks.put(bs, h["t"])

        def times_u(h):
            n, s = h["h"], h["s"]
            t_i.append(k.mms([(b[n * L3_D:(n + 1) * L3_D, i * P:(i + 1) * P], u[:, i * P + n * L3_D:i * P + (n + 1) * L3_D],
                               s[:, i * P:(i + 1) * P]) for i in range(TPG)], after=[t_u, h["t"], b.after]))
            k.scratch.put(s, t_i[-1])

        heads = [{"h": h} for h in range(L3_H)]
        yield from staged(heads, (0, chunk_scores), (1, times_u))
        k.scratch.put(q, [t_read, heads[-1]["read"]])
        k.scratch.put(kk, heads[-1]["read"])
        k.scratch.put(u, t_i)
        t = k.acopy(dl[:, :], o_bank[:, :], after=[t_o, dl.after])
        k.banks.put(o_bank, t)
        t_dl = k.tt(dl[:, :], dl[:, :], b[:, :], ALU.add, after=[t, t_i])
        k.banks.put(b, t_dl)
        yield
        pt, t_pt = path_rows(g)
        yield
        o, filtered_t = filtered.pop(g)
        b = k.banks.take()
        t = k.mm([(b[:, :], path[:, 3, :], pt[0:NP, :])], after=[t_pt, b.after])
        t = k.tt(dl[:, :], dl[:, :], b[:, :], ALU.mult, after=[t, t_dl])
        k.banks.put(b, t)
        k.scratch.put(pt, t)
        t = k.tt(o[:, :], o[:, :], dl[:, :], ALU.add, after=[t, filtered_t])
        k.scratch.put(dl, t)
        t = unit_rows(o, t, k.eps[:, 0:1], head_mean, norm_w)
        yield
        b, s = k.banks.take(), k.scratch.take()
        t = k.mm([(b[:, :], Wo, o[:, :])], after=[t, b.after])
        s.token = k.acopy(s[:, :], b[:, :], after=[t, s.after])
        k.scratch.put(o, t)
        k.banks.put(b, s.token)
        k.mixed[g] = s
        yield

    def ffn(g):
        k.T.wait(big)
        acc = k.banks.take()

        def hidden(e, f, x, gate):
            ba, bg, s = k.banks.take(), k.banks.take(), k.scratch.take()
            t = k.mm([(ba[:, :], W1[:, e, f * P:(f + 1) * P], x)], after=ba.after)
            t_g = k.mm([(bg[:, :], W1[:, e, (L3_FF + f) * P:(L3_FF + f + 1) * P], x)], after=bg.after)
            t = k.act(s[:, :], ba[:, :], ACT.Gelu, after=[t, s.after])
            k.banks.put(ba, t)
            t = k.tt(s[:, :], s[:, :], bg[:, :], ALU.mult, after=[t, t_g])
            k.banks.put(bg, t)
            return s, k.tt(s[:, :], s[:, :], gate[:, :], ALU.mult, after=[t, gate.token])

        yield from k.experts(g, gate_rows, acc, L3_FF, hidden, lambda e, f: W2[:, e, f, :], None, after=[])
        yield from k.gate_and_add(g, acc, k.t_acc[g], k.mixed[g])

    k.mixed = [None] * GROUPS
    mixed, passed = [], []

    def recur_and_count(g):
        yield from recur(g)
        mixed.append(g)

    def ffn_and_count(g):
        yield from ffn(g)
        passed.append(g)

    run_lanes(Lane(2, [(lambda g=g: len(mixed) >= g - 1 and len(passed) >= g - 2, lambda g=g: prepare(g)) for g in range(GROUPS)]),
              Lane(1, [(lambda g=g: g in values, lambda g=g: filters_of(g)) for g in range(GROUPS)]),
              Lane(1, [(lambda g=g: g in prepared and g in filtered, lambda g=g: recur_and_count(g)) for g in range(GROUPS)]),
              Lane(1, [(lambda g=g: k.mixed[g] is not None, lambda g=g: ffn_and_count(g)) for g in range(GROUPS)]))
    return k.x_ready


def layouts3(a):
    g = lambda n: a["L3_attn_" + n]
    return {"L3_Wqkv": np.concatenate([g("Wq").T, g("Wk").T, g("Wv").T], axis=1), "L3_Wo": g("Wo").T, "L3_Wb": g("Wb").T,
            "L3_taps": np.concatenate([g("conv_q"), g("conv_k"), g("conv_v")] +
                                      [g("fir_" + n).reshape(P, -1) for n in "sml"] +
                                      [np.tile(g("norm_w"), L3_H).reshape(P, 1)], axis=1),
            "L3_gate_w": g("gate_w").reshape(L3_H * L3_PATHS, P).T,
            "L3_row": np.concatenate([g(n).reshape(1, -1) for n in ("gate_b", "log_temp", "eps_param")], axis=1),
            "L3_consts": l3_constants(), "L3_Wg": a["L3_ffn_Wg"], "L3_W1": a["L3_ffn_W_in"], "L3_W2": a["L3_ffn_W_out"]}


def columns(v):
    return v.reshape(-1, P).T


def layouts(a):
    d = {"x": a["L0_attn_x"].reshape(TOKENS, P).T}
    if 0 in LAYERS:
        d.update({
            "L0_W1": a["L0_ffn_W1"], "L0_W2": a["L0_ffn_W2"], "L0_b1": columns(a["L0_ffn_b1"]), "L0_b2": a["L0_ffn_b2"],
            "L0_Wr": a["L0_ffn_Wr"], "L0_br": a["L0_ffn_br"].reshape(1, EXPERTS),
            "L0_Win": a["L0_attn_W_in"].T, "L0_Wout": a["L0_attn_W_out"].T})
    if 1 in LAYERS:
        d.update(layouts1(a))
    if 2 in LAYERS:
        d.update(layouts2(a))
    if 3 in LAYERS:
        d.update(layouts3(a))
    return d


def build(nc, ins, out, layers=LAYERS):
    k = Kernel(nc, ins, out)
    k.setup()
    words = REGION_WORDS
    regions = [k.sb("weights_even", [P, words[0]]), k.sb("weights_odd", [P, words[1]])]
    free = [[], []]
    for n in layers:
        k.first_layer, k.last_layer = n == layers[0], n == layers[-1]
        own, other = [Region(regions[m], words[m], free[m]) for m in (n % 2, 1 - n % 2)]
        done = layer3(k, own, other) if n == 3 else (layer0, layer1, layer2)[n](k, own)
        free[n % 2] = [done, k.banks_readers()]
    k.finish()


def kernel(**inputs):
    import concourse.bacc as bacc
    from concourse.bass_utils import run_bass_kernel_spmd

    arrays = {name: np.ascontiguousarray(a) for name, a in layouts({n: np.asarray(a) for n, a in inputs.items()}).items()}
    nc = bacc.Bacc("TRN2", target_bir_lowering=False, num_devices=1)
    ins = {name: nc.dram_tensor(f"in_{name}", a.shape, mybir.dt.from_np(a.dtype), kind="ExternalInput").ap()
           for name, a in arrays.items()}
    out = nc.dram_tensor("out_x", (P, TOKENS), F32, kind="ExternalOutput").ap()
    build(nc, ins, out)
    r = run_bass_kernel_spmd(nc, [{f"in_{name}": a for name, a in arrays.items()}], core_ids=[0])
    return np.ascontiguousarray(r.results[0]["out_x"].T).reshape(BATCH, SEQ, P)
```

```python
import numpy as np
import concourse.bass as bass
from concourse import mybir
from contextlib import ExitStack

F32 = mybir.dt.float32
ALU = mybir.AluOpType
ACT = mybir.ActivationFunctionType
AX = mybir.AxisListType

P = 128
BATCH, SEQ = 16, 256
TOKENS = BATCH * SEQ
GW = 512
GROUPS = TOKENS // GW
BPG = GW // SEQ
TPG = GW // P
TILES = TOKENS // P
EXPERTS = 8


HOP = 200.0
TABLES = {"Exp": 1, "Ln": 2, "Gelu": 3, "Silu": 4, "Sigmoid": 5}
expected = {}


def due(after):
    return max([expected.get((id(s), v), 0.0) for s, v in flat(after)], default=0.0)


def width(ap):
    return int(np.prod(ap.shape[1:]))


class Engine:

    latest = 0.0

    def __init__(self, name, ctx, nc):
        self.name, self.ctx, self.nc = name, ctx, nc
        self.queue, self.seen = [], {}
        self.sem, self.count = None, 0
        self.clock = 0.0

    def phase(self, label):
        self.sem = self.ctx.enter_context(self.nc.semaphore(f"{self.name}_{label}"))
        self.count = 0

    def wait(self, after):
        self.clock = max(self.clock, due(after) + HOP)
        for token in flat(after):
            sem, value = token
            if self.seen.get(id(sem), 0) < value:
                self.seen[id(sem)] = value
                self.queue.append(lambda eng, s=sem, v=value: eng.wait_ge(s, v))

    def run(self, emit, after=(), signal=True, cost=100.0):
        self.wait(after)
        self.clock += cost
        if not signal:
            self.queue.append(emit)
            return None
        self.count += 1
        sem = self.sem
        self.queue.append(lambda eng: emit(eng).then_inc(sem, 1))
        expected[(id(sem), self.count)] = self.clock
        Engine.latest = max(Engine.latest, self.clock)
        return (sem, self.count)

    def play(self, eng):
        for item in self.queue:
            item(eng)


def flat(after):
    if after is None:
        return []
    if isinstance(after, tuple) and len(after) == 2 and isinstance(after[1], int):
        return [after]
    return [t for a in after for t in flat(a)]


class Slot:
    def __init__(self, tensor, index):
        self.tensor, self.index, self.after = tensor, index, []

    def __getitem__(self, key):
        return self.tensor[key]


class Pool:

    def __init__(self, slots):
        self.free = list(slots)
        self.slots = len(self.free)

    def take(self):
        assert self.free, ("no buffer is free here", self.slots)
        best = min(range(len(self.free)), key=lambda n: due(self.free[n].after))
        return self.free.pop(best)

    def put(self, slot, readers):
        slot.after = flat(readers)
        self.free.append(slot)


class Lane:

    def __init__(self, pieces):
        self.pieces, self.current, self.ready = list(pieces), None, 0.0

    def may_step(self):
        return self.current is not None or (len(self.pieces) > 0 and self.pieces[0][0]())

    def step(self):
        if self.current is None:
            self.current = self.pieces.pop(0)[1]()
        Engine.latest = 0.0
        needs = next(self.current, "end")
        self.ready = due(needs) if needs not in (None, "end") else Engine.latest
        if needs == "end":
            self.current = None

    def over(self):
        return self.current is None and not self.pieces


def step_lanes(k, lanes, early):
    able = [lane for lane in lanes if lane.may_step()]
    assert able, "no lane may go on"
    room = [len(k.banks.free) > 3 and len(k.scratch.free) > (EARLY_ROOM if lane in early else ROOM) for lane in able]
    able = [lane for lane, r in zip(able, room) if r or lane.current is not None] or able
    ready = [lane for lane in able if lane.ready <= k.T.clock]
    (ready[0] if ready else min(able, key=lambda lane: lane.ready)).step()


def staged(units, *stages):
    last = max(lag for lag, _ in stages)
    for n in range(len(units) + last):
        for lag, f in reversed(stages):
            if 0 <= n - lag < len(units):
                f(units[n - lag])
        yield [units[n + 1 - lag]["t"] for lag, _ in stages if 0 <= n + 1 - lag < len(units) and "t" in units[n + 1 - lag]]


class Kernel:
    def __init__(self, nc, ins, out):
        self.nc, self.ins, self.out = nc, ins, out
        self.ctx = ExitStack()
        self.V = Engine("vector", self.ctx, nc)
        self.A = Engine("scalar", self.ctx, nc)
        self.G = Engine("gpsimd", self.ctx, nc)
        self.T = Engine("tensor", self.ctx, nc)
        self.D = Engine("sync", self.ctx, nc)
        self.stores = []
        self.table = 0

    def sb(self, name, shape, dt=F32):
        return self.ctx.enter_context(self.nc.sbuf_tensor(name, shape, dt))

    def phase(self, label):
        for e in (self.V, self.A, self.G, self.T):
            e.phase(label)

    def load(self, name, pairs, after=()):
        sem = self.ctx.enter_context(self.nc.semaphore(f"load_{name}"))
        self.D.wait(after)
        for dst, src in pairs:
            self.D.queue.append(lambda eng, d=dst, s=src: eng.dma_start(d, s).then_inc(sem, 16))
        return (sem, 16 * len(pairs))

    def mm(self, products, after=(), start=True, stop=True):
        self.T.wait(after)
        token = None
        n = len(products)
        for i, (o, l, r) in enumerate(products):
            token = self.T.run(lambda eng, o=o, l=l, r=r, a=(start and i == 0), z=(stop and i == n - 1):
                               eng.matmul(o, l, r, start=a, stop=z, skip_group_check=True),
                               signal=(i == n - 1), cost=width(o) * 4 / 2.4)
        return token

    def mms(self, products, after=()):
        self.T.wait(after)
        token = None
        for i, (o, l, r) in enumerate(products):
            token = self.T.run(lambda eng, o=o, l=l, r=r: eng.matmul(o, l, r, start=True, stop=True,
                                                                     skip_group_check=True),
                               signal=(i == len(products) - 1), cost=width(o) * 4 / 2.4)
        return token

    def turn(self, pairs, after=()):
        self.T.wait(after)
        token = None
        for i, (o, a) in enumerate(pairs):
            k = a.shape[0]
            token = self.T.run(lambda eng, o=o, a=a, k=k: eng.transpose(o, a, self.ident[0:k, 0:k]),
                               signal=(i == len(pairs) - 1), cost=width(o) * 2 / 2.4)
        return token

    def tt(self, out, a, b, op, after=(), on=None):
        return (on or self.V).run(lambda eng: eng.tensor_tensor(out, a, b, op), after,
                                  cost=(100 + 2.2 * width(out) if on is self.G else 70 + 1.05 * width(out)))

    def ts(self, out, a, s1, s2, op0, op1=None, after=(), on=None):
        if op1 is None:
            return (on or self.V).run(lambda eng: eng.tensor_scalar(out, a, s1, None, op0), after, cost=70 + 0.7 * width(out))
        return (on or self.V).run(lambda eng: eng.tensor_scalar(out, a, s1, s2, op0, op1), after, cost=70 + 0.7 * width(out))

    def recip(self, out, a, after=()):
        return self.V.run(lambda eng: eng.reciprocal(out, a), after, cost=70 + 6.3 * width(out))

    def stt(self, out, a, s, b, op0, op1, after=()):
        return self.V.run(lambda eng: eng.scalar_tensor_tensor(out=out, in0=a, scalar=s, in1=b, op0=op0, op1=op1), after, cost=70 + 1.05 * width(out))

    def red(self, out, a, op, after=(), negate=False):
        return self.V.run(lambda eng: eng.tensor_reduce(out, a, AX.X, op, negate=negate), after, cost=70 + 1.05 * width(a))

    def scan(self, out, decay, add, after=()):
        return self.V.run(lambda eng: eng.tensor_tensor_scan(out, decay, add, 0.0, ALU.mult, ALU.add), after, cost=70 + 2.1 * width(out))

    def act(self, out, a, func, bias=None, scale=1.0, accum=None, after=()):
        def emit(eng):
            kw = {"scale": scale}
            if bias is not None:
                kw["bias"] = bias
            if accum is not None:
                kw["accum_out"] = accum
            return eng.activation(out, a, func, **kw)
        table = TABLES.get(func.name, self.table)
        switch, self.table = (0.0 if table == self.table else 1300.0), table
        return self.A.run(emit, after, cost=switch + 180 + (100 if accum is not None else 0) + 0.83 * width(out))

    def vcopy(self, out, a, after=(), on=None):
        return (on or self.V).run(lambda eng: eng.tensor_copy(out, a), after, cost=70 + 1.05 * width(out))

    def acopy(self, out, a, after=(), scale=1.0):
        return self.act(out, a, ACT.Copy, scale=scale, after=after)

    def fill(self, out, value, after=(), on=None):
        return (on or self.G).run(lambda eng: eng.memset(out, value), after)

    def keep_where(self, ap, pattern, base, mult, op, fill, after=()):
        return self.G.run(lambda eng: eng.affine_select(out=ap, in_=ap, compare_op=op, fill=fill, base=base,
                                                        pattern=pattern, channel_multiplier=mult), after)

    def setup(self):
        self.xT = self.sb("x_channels", [P, TOKENS])
        self.xn = self.sb("normed_channels", [P, TOKENS])
        self.ident = self.sb("identity", [P, P])
        self.mean_w = self.sb("mean_weights", [P, P])
        self.eps = self.sb("eps_columns", [P, 4])
        self.scratch = Pool([Slot(self.sb(f"scratch{i}", [P, GW]), i) for i in range(SCRATCH)])
        self.banks = Pool([Slot(self.ctx.enter_context(self.nc.psum_tensor(f"bank{i}", [P, GW], F32)), i)
                           for i in range(8)])
        self.gate_slots = Pool([Slot(self.sb(f"gate_tile{i}", [P, GW]), i) for i in range(GATE_SLOTS)])
        for slot in self.gate_slots.free:
            slot.sem, slot.landed = self.ctx.enter_context(self.nc.semaphore(f"gate_tile{slot.index}")), 0
        self.stats = Pool([Slot(self.sb(f"stats{i}", [P, 16]), i) for i in range(12)])
        self.phase("setup")
        t = [self.fill(self.ident[:, :], 0.0),
             self.fill(self.mean_w[:, :], 1.0 / P)]
        for i, e in enumerate((1e-5, 1e-6, 0.0, 1.0)):
            t.append(self.fill(self.eps[:, i:i + 1], e))
        a = self.keep_where(self.ident[:, :], [[-1, P]], 0, 1, ALU.not_equal, 1.0, after=t)
        self.const = [a, t]
        for e in (self.V, self.A, self.T):
            e.wait(self.const)
        self.x_ready = [self.load(f"x{g}", [(self.cols(self.xT, g), self.ins["x"][:, g * GW:(g + 1) * GW])])
                        for g in range(GROUPS)]
        self.xn_ready = [None] * GROUPS
        self.normed = [0] * GROUPS
        self.t_acc = [None] * GROUPS
        self.xn_read = [[] for _ in range(GROUPS)]

    def cols(self, t, g):
        return t[:, g * GW:(g + 1) * GW]

    def layernorm(self, g):
        x, xn = self.cols(self.xT, g), self.cols(self.xn, g)
        mean, sq, var = self.banks.take(), self.scratch.take(), self.banks.take()
        t_mean = self.mm([(mean[:, :], self.mean_w[:, :], x)], after=[mean.after, self.x_ready[g]])
        yield
        t_d = self.tt(xn, x, mean[:, :], ALU.subtract, after=[t_mean, self.xn_read[g]])
        yield
        self.banks.put(mean, t_d)
        t_sq = self.act(sq[:, :], xn, ACT.Square, after=[t_d, sq.after])
        yield
        t_var = self.mm([(var[:, :], self.mean_w[:, :], sq[:, :])], after=[t_sq, var.after])
        yield
        t_r = self.inverse_root(sq[:, :], var, self.eps[:, 0:1], t_var)
        yield
        self.xn_ready[g] = self.tt(xn, xn, sq[:, :], ALU.mult, after=[t_r, t_d])
        self.scratch.put(sq, self.xn_ready[g])
        self.xn_read[g] = []
        self.normed[g] += 1
        yield

    def inverse_root(self, out, bank, eps, after):
        t = self.act(out, bank[:, :], ACT.Ln, bias=eps, after=after)
        self.banks.put(bank, t)
        return self.act(out, out, ACT.Exp, scale=-0.5, after=t)

    def normed_for(self, number):
        return lambda g: self.normed[g] >= number

    def first_layernorm(self):
        half = GROUPS // 2
        return [Lane([(lambda: True, lambda g=g: self.layernorm(g)) for g in range(m, GROUPS, half)]) for m in range(half)]

    def one_hot_first(self, mask, score, tmp, col, weight, n, w, after):
        v3 = lambda a: a.rearrange("p (n w) -> p n w", w=w)
        b = lambda c: c.unsqueeze(2).to_broadcast([P, n, w])
        t = self.red(col, v3(score), ALU.max, after=after)
        yield
        t = self.tt(v3(tmp), v3(score), b(col), ALU.is_equal, after=t)
        yield
        t = self.tt(tmp, tmp, weight, ALU.mult, after=t)
        yield
        t = self.red(col, v3(tmp), ALU.max, after=t)
        yield
        return self.tt(v3(mask), v3(tmp), b(col), ALU.is_equal, after=t)

    def softmax_experts(self, name, Wr, after, bias=None):
        N = TILES * EXPERTS
        bank = self.banks.take()
        for g in range(GROUPS):
            t = self.mms([(bank[:, i * EXPERTS:(i + 1) * EXPERTS], self.xn[:, i * P:(i + 1) * P], Wr)
                          for i in range(TPG * g, TPG * (g + 1))], after=[bank.after, after, self.xn_ready[g]])
            yield
        v3 = lambda a: a.rearrange("p (n w) -> p n w", w=EXPERTS)
        bc = lambda c: c.unsqueeze(2).to_broadcast([P, TILES, EXPERTS])
        lg, pr, col = self.scratch.take(), self.scratch.take(), self.scratch.take()
        l, p, c = lg[:, 0:N], pr[:, 0:N], col[:, 0:TILES]
        if bias is None:
            t = self.vcopy(l, bank[:, 0:N], after=[t, lg.after])
        else:
            t = self.tt(v3(l), v3(bank[:, 0:N]), bias.unsqueeze(1).to_broadcast([P, TILES, EXPERTS]), ALU.add,
                        after=[t, lg.after])
        self.banks.put(bank, t)
        yield
        t = self.red(c, v3(l), ALU.max, after=[t, col.after])
        yield
        t = self.tt(v3(l), v3(l), bc(c), ALU.subtract, after=t)
        yield
        t_e = self.act(p, l, ACT.Exp, after=[t, pr.after])
        yield
        t = self.red(c, v3(p), ALU.add, after=[t_e, t])
        yield
        t = self.recip(c, c, after=t)
        t = self.tt(v3(p), v3(p), bc(c), ALU.mult, after=t)
        self.scratch.put(col, t)
        return lg, pr, t

    def gates_to_rows(self, gates, label, after):
        rows = self.nc.dram_tensor(f"gate_rows_{label}", (EXPERTS, TOKENS), F32).ap()
        sem = self.ctx.enter_context(self.nc.semaphore(f"gate_rows_{label}"))
        stored = (sem, 16 * GROUPS)
        staging = []
        for g in range(GROUPS):
            bank, gt = self.banks.take(), self.scratch.take()
            t = self.turn([(bank[0:EXPERTS, i * P:(i + 1) * P],
                            gates[:, (TPG * g + i) * EXPERTS:(TPG * g + i + 1) * EXPERTS]) for i in range(TPG)],
                          after=[bank.after, after])
            yield
            t = self.vcopy(gt[0:EXPERTS, :], bank[0:EXPERTS, :], after=[t, gt.after])
            self.banks.put(bank, t)
            self.D.wait(t)
            self.D.queue.append(lambda eng, g=g, gt=gt: eng.dma_start(rows[:, g * GW:(g + 1) * GW], gt[0:EXPERTS, :])
                                .then_inc(sem, 16))
            staging.append(gt)
            yield
        for gt in staging:
            self.scratch.put(gt, stored)
        expected[(id(sem), stored[1])] = self.V.clock + 2500.0
        self.stores.append(stored)
        return rows, stored

    def gate_tile(self, rows, t_rows, e, g):
        slot = self.gate_slots.take()
        slot.landed += 16
        self.D.wait([t_rows, slot.after])
        src = rows[e:e + 1, g * GW:(g + 1) * GW].broadcast_to([P, GW])
        self.D.queue.append(lambda eng: eng.dma_start(slot[:, :], src).then_inc(slot.sem, 16))
        slot.token = (slot.sem, slot.landed)
        return slot

    def experts(self, g, rows, acc, nf, hidden, gated, W2, b2, after, ahead=4):
        x = self.cols(self.xn, g)
        units = [{"e": e, "f": f} for e in range(EXPERTS) for f in range(nf)]
        gates, used = {}, {e: [] for e in range(EXPERTS)}

        def fetch(u):
            if u["f"] == 0:
                gates[u["e"]] = self.gate_tile(*rows, u["e"], g)

        def up(u):
            u.update(hidden(u["e"], u["f"], x))

        def times_gate(u):
            e = u["e"]
            u["t"] = gated(u, gates[e])
            used[e].append(u["t"])
            if u["f"] == nf - 1:
                self.gate_slots.put(gates[e], used[e])

        def down(u):
            n = u["e"] * nf + u["f"]
            tok = self.mm([(acc[:, :], W2(u["e"], u["f"]), u["slot"][:, :])], after=[u["t"]] + ([acc.after] if n == 0 else []),
                          start=(n == 0), stop=(n == len(units) - 1 and b2 is None))
            self.scratch.put(u["slot"], tok)
            self.t_acc[g] = tok

        yield from staged(units, (0, fetch), (ahead, up), (ahead + 1, times_gate), (ahead + 4, down))
        if b2 is not None:
            gt = self.gate_slots.take()
            gt.landed += 16
            self.D.wait(gt.after)
            self.D.queue.append(lambda eng: eng.dma_start(gt[0:EXPERTS, :], rows[0][:, g * GW:(g + 1) * GW]).then_inc(gt.sem, 16))
            self.t_acc[g] = self.mm([(acc[:, :], b2, gt[0:EXPERTS, :])], after=[(gt.sem, gt.landed), after], start=False)
            self.gate_slots.put(gt, self.t_acc[g])

    def gate_and_add(self, g, acc, t_acc, s, silu=None):
        x = self.cols(self.xT, g)
        if silu is None:
            sl = self.scratch.take()
            t = self.act(sl[:, :], acc[:, :], ACT.Silu, after=[t_acc, sl.after])
            self.banks.put(acc, t)
        else:
            sl, t = silu, t_acc
        t = self.tt(sl[:, :], sl[:, :], s[:, :], ALU.mult, after=[t, s.token])
        self.scratch.put(s, t)
        self.x_ready[g] = self.tt(x, x, sl[:, :], ALU.add, after=t)
        self.scratch.put(sl, self.x_ready[g])
        self.xn_read[g] = [t_acc, s.token]
        if self.normed[g] == self.layers:
            self.D.wait(self.x_ready[g])
            sem = self.ctx.enter_context(self.nc.semaphore(f"store_group{g}"))
            self.D.queue.append(lambda eng: eng.dma_start(self.out[:, g * GW:(g + 1) * GW], x).then_inc(sem, 16))
            self.stores.append((sem, 16))
        else:
            yield
            yield from self.layernorm(g)

    def finish(self):
        self.D.wait(self.stores)
        with self.nc.Block() as block:
            block.sync(self.D.play)
            block.vector(self.V.play)
            block.scalar(self.A.play)
            block.gpsimd(self.G.play)
            block.tensor(self.T.play)
        self.ctx.close()

LAYERS = [0,1,2,3]
SCRATCH = 38
REGION_WORDS = (10300, 12200)
GATE_SLOTS = 4
ROOM = 12
EARLY_ROOM = 24


L0_HEADS = 16
L0_DH = P // L0_HEADS
L0_ORDERS = (1, 2, 3, 4, 5)
L0_FF = 4


def chebyshev_weights():
    order = 6
    alpha = (np.arange(order, dtype=np.float32) + 1.0) ** (-1.5)
    tail = np.flip(np.cumsum(np.flip(alpha)))
    beta = np.concatenate([np.zeros(1, np.float32), tail[1:].astype(np.float32), np.zeros(order - 1, np.float32)])
    return beta / beta.sum()


def layer0(k, region):
    nc, ins = k.nc, k.ins
    beta = chebyshev_weights()
    assert [i for i in range(len(beta)) if beta[i] != 0] == list(L0_ORDERS)
    take = region.take
    W1 = take("p (e f) -> p e f", e=EXPERTS, f=512)
    W2 = take("p (e c d) -> p e c d", e=EXPERTS, c=L0_FF, d=P)
    b1 = take("p (n) -> p n", n=EXPERTS * L0_FF)
    b2 = take("p (n) -> p n", n=P)[0:EXPERTS, :]
    Wr = take("p (n) -> p n", n=EXPERTS)
    br = take("p (n) -> p n", n=EXPERTS)
    Win = take("p (n) -> p n", n=3 * P)
    Wout = take("p (n) -> p n", n=P)
    NO = len(L0_ORDERS)
    rows = NO * L0_HEADS
    head_sum = take("p (o r) -> p o r", o=NO, r=rows)
    head_back = take("p (n) -> p n", n=P)[0:rows, :]
    ones = take("p (n) -> p n", n=SEQ)
    gates = take("p (n) -> p n", n=TILES * EXPERTS)
    weight = take("p (n w) -> p n w", n=TILES, w=EXPERTS)
    small = k.load("L0_small", [(Wr, ins["L0_Wr"][:, :]), (br, ins["L0_br"][:, :].broadcast_to([P, EXPERTS])),
                                (Win, ins["L0_Win"][:, :]), (Wout, ins["L0_Wout"][:, :]), (b1, ins["L0_b1"][:, :]),
                                (b2, ins["L0_b2"][:, :])], after=region.free_after)
    big = k.load("L0_experts", [(W1[:, e, :], ins["L0_W1"][e, :, :]) for e in range(EXPERTS)] +
                 [(W2[:, e, :, :], ins["L0_W2"][e, :, :].rearrange("(c p) d -> p c d", p=P)) for e in range(EXPERTS)])
    yield
    k.phase("L0")
    mixed, normed = [None] * GROUPS, k.normed_for(k.started)
    t = [k.fill(head_sum, 0.0, after=region.free_after), k.fill(ones, 1.0)]
    const = [t[1]]
    for o in range(NO):
        v = head_sum[:, o, o * L0_HEADS:(o + 1) * L0_HEADS]
        t1 = k.fill(v, 1.0, after=t)
        t2 = k.keep_where(v, [[-L0_DH, L0_HEADS]], 0, 1, ALU.is_ge, 0.0, after=t1)
        const.append(k.keep_where(v, [[L0_DH, L0_HEADS]], L0_DH - 1, -1, ALU.is_ge, 0.0, after=t2))
    hb = head_back.rearrange("p (h d) -> p h d", d=L0_DH)
    bank, buf = k.banks.take(), k.scratch.take()
    t0 = k.ts(buf[:, 0:rows], head_sum[:, 0, :], float(beta[L0_ORDERS[0]]), None, ALU.mult, after=[const, buf.after])
    for o in range(1, NO):
        t0 = k.stt(buf[:, 0:rows], head_sum[:, o, :], float(beta[L0_ORDERS[o]]), buf[:, 0:rows], ALU.mult, ALU.add, after=t0)
    t0 = k.turn([(bank[0:rows, 0:P], buf[:, 0:rows])], after=[bank.after, t0])
    t0 = k.vcopy(head_back, bank[0:rows, 0:P], after=t0)
    k.banks.put(bank, t0)
    k.scratch.put(buf, t0)
    for e in range(EXPERTS):
        const.append(k.fill(weight[:, :, e:e + 1], float(EXPERTS - e)))
    const.append(t0)
    k.T.wait(const)
    k.V.wait(const)


    def route():
        W = TILES * EXPERTS
        lg, pr, t_p = yield from k.softmax_experts("L0", Wr, small, bias=br)
        tmp, col = k.scratch.take(), k.scratch.take()
        t = yield from k.one_hot_first(gates, lg[:, 0:W], tmp[:, 0:W], col[:, 0:TILES],
                                       weight.rearrange("p n w -> p (n w)"), TILES, EXPERTS,
                                       after=[t_p, tmp.after, col.after])
        yield
        t_gates = k.tt(gates, gates, pr[:, 0:W], ALU.mult, after=[t, t_p])
        for s in (lg, pr, tmp, col):
            k.scratch.put(s, t_gates)
        yield
        return (yield from k.gates_to_rows(gates, "L0", t_gates))

    def attention(g):
        x = k.cols(k.xn, g)
        k.T.wait(small)
        xs = []
        for i in range(2):
            b, s = k.banks.take(), k.scratch.take()
            t = k.mm([(b[:, :], Win[:, i * P:(i + 1) * P], x)], after=[b.after, k.xn_ready[g]])
            yield
            t = k.act(s[:, :], b[:, :], ACT.Copy, scale=float(1.0 / np.sqrt(np.float32(L0_DH))), after=[t, s.after])
            yield
            k.banks.put(b, t)
            t = k.ts(s[:, :], s[:, :], -1.0 + 1e-6, 1.0 - 1e-6, ALU.max, ALU.min, after=t)
            xs.append((s, t))
            yield
        b, v = k.banks.take(), k.scratch.take()
        t = k.mm([(b[:, :], Win[:, 2 * P:3 * P], x)], after=b.after)
        yield
        t_v = k.acopy(v[:, :], b[:, :], after=[t, v.after])
        k.banks.put(b, t_v)
        yield
        prev, cur, dbl = [None, None], [xs[0], xs[1]], []
        for s, t in xs:
            d = k.scratch.take()
            dbl.append((d, k.ts(d[:, :], s[:, :], 2.0, None, ALU.mult, after=[t, d.after])))
        num = k.scratch.take()
        sums = [k.banks.take(), k.banks.take()]
        t_num = None
        t_sum = [None, None]
        for o in range(NO):
            if o > 0:
                for i in range(2):
                    n = k.scratch.take()
                    (cs, ct), (ds, dt) = cur[i], dbl[i]
                    t = k.tt(n[:, :], ds[:, :], cs[:, :], ALU.mult, after=[ct, dt, n.after])
                    if prev[i] is None:
                        t = k.ts(n[:, :], n[:, :], -1.0, None, ALU.add, after=t)
                    else:
                        ps, pt = prev[i]
                        t = k.tt(n[:, :], n[:, :], ps[:, :], ALU.subtract, after=[t, pt], on=k.G)
                        k.scratch.put(ps, [t, t_sum[i], t_num])
                    prev[i], cur[i] = cur[i], (n, t)
            for i in range(2):
                s, t = cur[i]
                t_sum[i] = k.mm([(sums[i][0:rows, :], head_sum[:, o, :], s[:, :])],
                                after=[t] + ([sums[i].after] if o == 0 else []), start=(o == 0), stop=(o == NO - 1))
            yield
            kv, cu = k.scratch.take(), k.scratch.take()
            t = k.tt(kv[:, :], cur[1][0][:, :], v[:, :], ALU.mult, after=[cur[1][1], t_v, kv.after])
            t_c = [k.scan(cu[:, j * SEQ:(j + 1) * SEQ], ones, kv[:, j * SEQ:(j + 1) * SEQ], after=[t, cu.after])
                   for j in range(BPG)]
            dst = num if o == 0 else kv
            t = k.stt(dst[:, :], cur[0][0][:, :], float(beta[L0_ORDERS[o]]), cu[:, :], ALU.mult, ALU.mult,
                      after=[t_c, cur[0][1]] + ([num.after] if o == 0 else []))
            t_q = t
            if o > 0:
                t = k.tt(num[:, :], num[:, :], kv[:, :], ALU.add, after=[t, t_num], on=k.G)
            k.scratch.put(kv, t)
            k.scratch.put(cu, t_q)
            t_num = t
            yield
        for i in range(2):
            for s in (prev[i][0], cur[i][0], dbl[i][0]):
                k.scratch.put(s, [t_num, t_sum[i]])
        k.scratch.put(v, t_num)
        kc, den = k.scratch.take(), k.banks.take()
        t_c = [k.scan(kc[0:rows, j * SEQ:(j + 1) * SEQ], ones[0:rows, :], sums[1][0:rows, j * SEQ:(j + 1) * SEQ],
                      after=[t_sum[1], kc.after]) for j in range(BPG)]
        t = k.tt(kc[0:rows, :], kc[0:rows, :], sums[0][0:rows, :], ALU.mult, after=[t_c, t_sum[0]])
        k.banks.put(sums[0], t)
        k.banks.put(sums[1], t)
        yield
        t = k.mm([(den[:, :], head_back, kc[0:rows, :])], after=[t, den.after])
        yield
        t = k.ts(kc[:, :], den[:, :], 1e-7, None, ALU.add, after=t)
        k.banks.put(den, t)
        t = k.recip(kc[:, :], kc[:, :], after=t)
        t = k.tt(num[:, :], num[:, :], kc[:, :], ALU.mult, after=[t, t_num])
        k.scratch.put(kc, t)
        yield
        b, s = k.banks.take(), k.scratch.take()
        t = k.mm([(b[:, :], Wout, num[:, :])], after=[t, b.after])
        yield
        s.token = k.acopy(s[:, :], b[:, :], after=[t, s.after])
        k.scratch.put(num, t)
        k.banks.put(b, s.token)
        mixed[g] = s
        yield

    def ffn(g, gate_rows):
        k.T.wait([big, small])
        acc = k.banks.take()

        def hidden(e, f, x):
            b, s = k.banks.take(), k.scratch.take()
            t = k.mm([(b[:, :], W1[:, e, f * P:(f + 1) * P], x)], after=b.after)
            n = e * L0_FF + f
            t = k.act(s[:, :], b[:, :], ACT.Gelu, bias=b1[:, n:n + 1], after=[t, s.after, small])
            k.banks.put(b, t)
            return {"slot": s, "t": t}

        def gated(u, gate):
            s = u["slot"]
            return k.tt(s[:, :], s[:, :], gate[:, :], ALU.mult, after=[u["t"], gate.token])

        yield from k.experts(g, gate_rows, acc, L0_FF, hidden, gated, lambda e, f: W2[:, e, f, :], b2, after=small)
        yield from k.gate_and_add(g, acc, k.t_acc[g], mixed[g])

    yield layer_lanes(route, attention, ffn, mixed, normed)


def layer_lanes(route, mix, ffn, mixed, normed):
    gate_rows = []
    passed = []

    def routing():
        gate_rows.append((yield from route()))

    def experts(g):
        yield from ffn(g, gate_rows[0])
        passed.append(g)

    return [Lane([(lambda: all(normed(g) for g in range(GROUPS)), routing)]),
            Lane([(lambda g=g: normed(g) and len(passed) >= g - 1, lambda g=g: mix(g)) for g in range(GROUPS)]),
            Lane([(lambda g=g: mixed[g] is not None and gate_rows, lambda g=g: experts(g)) for g in range(GROUPS)])], passed


class Region:

    def __init__(self, tensor, words, free_after, at=0):
        self.tensor, self.words, self.free_after, self.at = tensor, words, free_after, at

    def take(self, pattern, **sizes):
        n = int(np.prod(list(sizes.values())))
        n += -n % 8
        assert self.at + n <= self.words, ("region", self.at + n)
        ap = self.tensor[:, self.at:self.at + int(np.prod(list(sizes.values())))]
        self.at += n
        return ap if len(sizes) == 1 else ap.rearrange(pattern, **sizes)


L1_INNER = 2
L1_H, L1_E, L1_DH, L1_K = 8, 5, 64, 3
L1_ROW = L1_H * L1_DH


def top_mask(k, mask, score, tmp, pick, col, weight, n, w, count, after):
    t = after
    for r in range(count):
        t = yield from k.one_hot_first(pick, score, tmp, col, weight, n, w, after=t)
        yield
        if r == 0:
            t_m = k.vcopy(mask, pick, after=t)
        else:
            t_m = k.tt(mask, mask, pick, ALU.add, after=[t, t_m])
        if r < count - 1:
            t = k.stt(score, pick, -4.0, score, ALU.mult, ALU.add, after=t)
        t = [t, t_m]
        yield
    return t


def scores(k, u, q, kk, after):
    u["S"], u["max"] = k.banks.take(), k.stats.take()
    bank, mx = u["S"], u["max"]
    t = k.mms([(bank[:, i * SEQ:(i + 1) * SEQ], q[:, i * P:(i + 1) * P], kk) for i in range(2)],
              after=[bank.after, after])
    u["t"] = k.red(mx[:, 0:2], bank[:, :].rearrange("p (i j) -> p i j", j=SEQ), ALU.max, after=[t, mx.after], negate=True)


def exponentials(k, u, rsum, after):
    bank, mx, p = u["S"], u["max"], k.scratch.take()
    u["t"] = [k.act(p[:, i * SEQ:(i + 1) * SEQ], bank[:, i * SEQ:(i + 1) * SEQ], ACT.Exp, bias=mx[:, i:i + 1],
                    accum=rsum[:, i:i + 1], after=[u["t"], p.after, after]) for i in range(2)]
    k.banks.put(bank, u["t"])
    k.stats.put(mx, u["t"])
    u["p"] = p


def turned_scores(k, p, t_p, on_vector):
    bank, pt = k.banks.take(), k.scratch.take()
    t = k.turn([(bank[:, jc * SEQ + i * P:jc * SEQ + (i + 1) * P], p[:, i * SEQ + jc * P:i * SEQ + (jc + 1) * P])
                for jc in range(2) for i in range(2)], after=[bank.after, t_p])
    k.scratch.put(p, t)
    copy = k.vcopy if on_vector else k.acopy
    t = copy(pt[:, :], bank[:, :], after=[t, pt.after])
    k.banks.put(bank, t)
    return pt, t


def layer1(k, region):
    nc, ins = k.nc, k.ins
    take = region.take
    Iw = take("p (n) -> p n", n=256)
    Gw = take("p (n) -> p n", n=256)
    Bw, Cw, Dw = [take("p (c n) -> p c n", c=2, n=256) for _ in range(3)]
    Ow = take("p (c n) -> p c n", c=2, n=P)
    cols = take("p (n) -> p n", n=16)
    decay = take("p (c n) -> p c n", c=2, n=SEQ)
    one = take("p (n) -> p n", n=SEQ)
    Wsd = take("p (n) -> p n", n=2 * L1_H * L1_E)
    Wx = {kind: take("p (e n) -> p e n", e=L1_E, n=L1_ROW) for kind in ("q", "k", "v")}
    Wo = take("p (c n) -> p c n", c=3, n=P)
    NR = TPG * 2 * L1_H
    weight = take("p (n w) -> p n w", n=NR, w=L1_E)
    small = k.load("L1_small", [(Iw, ins["L1_Iw"][:, :]), (Gw, ins["L1_Gw"][:, :]), (cols, ins["L1_cols"][:, :])] +
                   [(w, ins[n][:, :].rearrange("(c p) n -> p c n", p=P))
                    for w, n in ((Bw, "L1_Bw"), (Cw, "L1_Cw"), (Dw, "L1_Dw"), (Ow, "L1_Ow"))], after=region.free_after)
    big = k.load("L1_ffn", [(Wsd, ins["L1_Wsd"][:, :])] +
                 [(Wx[n], ins[f"L1_W{n}"][:, :].rearrange("p (e n) -> p e n", e=L1_E)) for n in ("q", "k", "v")] +
                 [(Wo[:, 0:2, :], ins["L1_Wo"][0:2 * P, :].rearrange("(c p) n -> p c n", p=P)),
                  (Wo[0:64, 2, :], ins["L1_Wo"][2 * P:, :])])
    yield
    k.phase("L1")
    mixed, normed = [None] * GROUPS, k.normed_for(k.started)
    const = [k.fill(one, 1.0, after=region.free_after)]
    for e in range(L1_E):
        const.append(k.fill(weight[:, :, e:e + 1], float(L1_E - e), after=region.free_after))
    in_b, gate_b, b_b, c_b, d_b, a_log = [cols[:, 2 * i:2 * i + 2] for i in range(6)]
    out_b, norm_w = cols[:, 12:13], cols[:, 13:14]
    t_a = k.act(a_log, a_log, ACT.Sigmoid, scale=-1.0, after=small)
    t_decay = [k.ts(decay[:, c, :], one, a_log[:, c:c + 1], None, ALU.mult, after=[t_a, const]) for c in range(2)]
    k.V.wait([const, t_decay, small])

    def recurrence(g):
        x = k.cols(k.xn, g)
        sq, b = k.scratch.take(), k.banks.take()
        t = k.act(sq[:, :], x, ACT.Square, after=[k.xn_ready[g], sq.after])
        yield
        t = k.mm([(b[:, :], k.mean_w[:, :], sq[:, :])], after=[t, b.after])
        yield
        t = k.inverse_root(sq[:, :], b, k.eps[:, 1:2], t)
        yield
        t_r = k.stt(sq[:, :], x, norm_w, sq[:, :], ALU.mult, ALU.mult, after=[t, k.xn_ready[g]])
        yield
        xr = sq
        k.T.wait(small)
        u = []
        for c in range(2):
            s = k.scratch.take()
            bg, bu = k.banks.take(), k.banks.take()
            t_g = k.mm([(bg[:, :], Gw[:, c * P:(c + 1) * P], xr[:, :])], after=[t_r, bg.after])
            t_u = k.mm([(bu[:, :], Iw[:, c * P:(c + 1) * P], xr[:, :])], after=bu.after)
            yield
            t = k.act(s[:, :], bg[:, :], ACT.Sigmoid, bias=gate_b[:, c:c + 1], after=[t_g, s.after])
            yield
            k.banks.put(bg, t)
            t = k.stt(s[:, :], bu[:, :], in_b[:, c:c + 1], s[:, :], ALU.add, ALU.mult, after=[t_u, t])
            k.banks.put(bu, t)
            u.append((s, t))
            yield
        k.scratch.put(xr, t_u)
        ys = []
        for c in range(2):
            sl = slice(c * P, (c + 1) * P)
            bb, bc = k.banks.take(), k.banks.take()
            s, h = k.scratch.take(), k.scratch.take()
            t_b = k.mm([(bb[:, :], Bw[:, i, sl], u[i][0][:, :]) for i in range(2)], after=[u[0][1], u[1][1], bb.after])
            t_c = k.mm([(bc[:, :], Cw[:, i, sl], u[i][0][:, :]) for i in range(2)], after=bc.after)
            yield
            t = k.act(s[:, :], bb[:, :], ACT.Identity, bias=b_b[:, c:c + 1], after=[t_b, s.after])
            yield
            k.banks.put(bb, t)
            t = [k.scan(h[:, j * SEQ:(j + 1) * SEQ], decay[:, c, :], s[:, j * SEQ:(j + 1) * SEQ], after=[t, h.after])
                 for j in range(BPG)]
            t = k.stt(h[:, :], bc[:, :], c_b[:, c:c + 1], h[:, :], ALU.add, ALU.mult, after=[t, t_c])
            k.banks.put(bc, t)
            k.scratch.put(s, t)
            yield
            bd = k.banks.take()
            t_d = k.mm([(bd[:, :], Dw[:, i, sl], u[i][0][:, :]) for i in range(2)], after=bd.after)
            yield
            t = k.stt(h[:, :], bd[:, :], d_b[:, c:c + 1], h[:, :], ALU.add, ALU.add, after=[t, t_d])
            k.banks.put(bd, t)
            ys.append((h, t))
            yield
        for s, _ in u:
            k.scratch.put(s, t_d)
        b, s = k.banks.take(), k.scratch.take()
        t = k.mm([(b[:, :], Ow[:, i, :], ys[i][0][:, :]) for i in range(2)], after=[ys[0][1], ys[1][1], b.after])
        yield
        for y, _ in ys:
            k.scratch.put(y, t)
        s.token = k.stt(s[:, :], b[:, :], out_b, x, ALU.add, ALU.add, after=[t, s.after])
        k.banks.put(b, s.token)
        mixed[g] = s
        yield

    W = 2 * L1_H * L1_E
    NW = TPG * W
    heads = lambda a: a.rearrange("p (h d) -> p h d", d=L1_DH)
    routed, projected, outputs, gated_out, passed = {}, {}, {}, {}, []

    def per_head(s, i, which, e):
        v = s[:, 0:NW].rearrange("p (n w h e) -> p n w h e", n=TPG, w=2, h=L1_H, e=L1_E)
        return v[:, i, which, :, e].unsqueeze(2).to_broadcast([P, L1_H, L1_DH])

    def route(g):
        k.T.wait(big)
        x = k.cols(k.xn, g)
        bank, sg, mk, sc, tmp, pick, col = [k.banks.take()] + [k.scratch.take() for _ in range(6)]
        t = k.mms([(bank[:, i * W:(i + 1) * W], x[:, i * P:(i + 1) * P], Wsd) for i in range(TPG)],
                  after=[bank.after, k.xn_ready[g]])
        yield
        t_s = k.act(sg[:, 0:NW], bank[:, 0:NW], ACT.Sigmoid, after=[t, sg.after])
        k.banks.put(bank, t_s)
        yield
        t = k.vcopy(sc[:, 0:NW], sg[:, 0:NW], after=[t_s, sc.after, tmp.after, pick.after, col.after, mk.after])
        t = yield from top_mask(k, mk[:, 0:NW], sc[:, 0:NW], tmp[:, 0:NW], pick[:, 0:NW], col[:, 0:NR],
                                weight.rearrange("p n w -> p (n w)"), NR, L1_E, L1_K, after=t)
        t_g = k.tt(sg[:, 0:NW], sg[:, 0:NW], mk[:, 0:NW], ALU.mult, after=t)
        for s in (sc, tmp, pick, col):
            k.scratch.put(s, t_g)
        routed[g] = (sg, mk, t_g)

    def project(bt):
        g, b = bt // BPG, bt % BPG
        sg, mk, t_g = routed[g]
        x = k.cols(k.xn, g)
        turned = {"q": [k.scratch.take(), k.scratch.take()], "k": [k.scratch.take(), k.scratch.take()]}
        t_turned = {"q": [], "k": []}
        vs = []

        def product(u):
            i, kind, which, e = u["i"], u["kind"], u["which"], u["e"]
            bank, dst = k.banks.take(), k.scratch.take()
            t = k.mm([(bank[:, :], x[:, i * P:(i + 1) * P], Wx[kind][:, e, :])], after=bank.after)
            t = k.tt(heads(dst[:, :]), heads(bank[:, :]), per_head(sg, i, which, e), ALU.mult, after=[t, t_g, dst.after])
            k.banks.put(bank, t)
            u["dst"], u["t"] = dst, t

        def add(u):
            i, kind, e, dst, t = u["i"], u["kind"], u["e"], u["dst"], u["t"]
            if e == 0:
                u["all"]["sum"] = (dst, t)
            else:
                acc, t_acc = u["all"]["sum"]
                t = k.tt(acc[:, :], acc[:, :], dst[:, :], ALU.add, after=[t, t_acc], on=(k.V if e == 2 else k.G))
                k.scratch.put(dst, t)
                u["all"]["sum"] = (acc, t)
            if kind == "v" and e == L1_E - 1:
                vs.append(u["all"]["sum"])

        def turn_sum(u):
            i, kind = u["i"], u["kind"]
            if kind == "v" or u["e"] < L1_E - 1:
                return
            acc, t = u["all"]["sum"]
            bank = k.banks.take()
            t = k.turn([(bank[:, m * P:(m + 1) * P], acc[:, m * P:(m + 1) * P]) for m in range(4)], after=[t, bank.after])
            k.scratch.put(acc, t)
            t2 = []
            for s in range(2):
                o = turned[kind][s]
                t2.append(k.acopy(o[:, :].rearrange("p (m t) -> p m t", t=SEQ)[:, :, (i % 2) * P:(i % 2 + 1) * P],
                                  bank[:, s * SEQ:(s + 1) * SEQ].rearrange("p (m t) -> p m t", t=P),
                                  scale=(L1_DH ** -0.5 if kind == "q" else 1.0), after=[t, o.after]))
            t_turned[kind] += t2
            k.banks.put(bank, t2)

        units = []
        for i in (2 * b, 2 * b + 1):
            for kind, which in (("q", 1), ("k", 0), ("v", 0)):
                shared = {}
                units += [{"i": i, "kind": kind, "which": which, "e": e, "all": shared} for e in range(L1_E)]
        yield from staged(units, (0, product), (2, add), (8, turn_sum))
        projected[bt] = (turned, t_turned, vs)

    def attend(bt):
        g, b = bt // BPG, bt % BPG
        sg, mk, t_g = routed[g]
        turned, t_turned, vs = projected.pop(bt)
        O = [k.banks.take(), k.banks.take()]
        rs = k.stats.take()
        rsv = rs[:, 0:2 * L1_H].rearrange("p (h i) -> p h i", i=2)
        done = []

        def query_key(u):
            h = u["h"]
            m, r = h // 2, (h % 2) * L1_DH
            q, kk = [turned[n][m // 2][r:r + L1_DH, (m % 2) * SEQ:(m % 2 + 1) * SEQ] for n in ("q", "k")]
            scores(k, u, q, kk, [t_turned["q"], t_turned["k"]])

        def exps(u):
            exponentials(k, u, rsv[:, u["h"], :], rs.after)
            u["sums"] = u["t"]

        def turn(u):
            u["pt"], u["t"] = turned_scores(k, u["p"], u["t"], u["h"] % 4 == 0)

        def times_v(u):
            h, pt = u["h"], u["pt"]
            for i in range(2):
                t = k.mm([(O[i][:, h * L1_DH:(h + 1) * L1_DH], pt[:, jc * SEQ + i * P:jc * SEQ + (i + 1) * P],
                           vs[jc][0][:, h * L1_DH:(h + 1) * L1_DH]) for jc in range(2)],
                         after=[u["t"], vs[0][1], vs[1][1], O[i].after])
            k.scratch.put(pt, t)
            done.append(t)

        units = [{"h": h} for h in range(L1_H)]
        yield from staged(units, (0, query_key), (1, exps), (3, turn), (5, times_v))
        t_pv = done[-1]
        for s in turned["q"] + turned["k"] + [v for v, _ in vs]:
            k.scratch.put(s, t_pv)
        yield
        t_r = k.recip(rs[:, 0:2 * L1_H], rs[:, 0:2 * L1_H], after=[u["sums"] for u in units])
        out = []
        for i in range(2):
            o = k.scratch.take()
            t = k.tt(heads(o[:, :]), heads(O[i][:, :]), rsv[:, :, i].unsqueeze(2).to_broadcast([P, L1_H, L1_DH]),
                     ALU.mult, after=[t_pv, t_r, o.after])
            k.banks.put(O[i], t)
            out.append((o, t))
        k.stats.put(rs, t)
        outputs[bt] = out
        yield

    def combine(bt):
        g, b = bt // BPG, bt % BPG
        sg, mk, t_g = routed[g]
        if b == 0:
            gated_out[g] = [k.scratch.take(), []]
        fo, fo_tokens = gated_out[g]
        tiles_out = [{"n": TPG // BPG * b + i, "o": o, "mixd": k.scratch.take(), "ts": []}
                     for i, (o, _) in enumerate(outputs[bt])]
        t_out = [t for _, t in outputs.pop(bt)]

        def kept_heads(u):
            a = u["tile"]
            u["tmp"] = k.scratch.take()
            u["t"] = k.tt(heads(u["tmp"][:, :]), heads(a["o"][:, :]), per_head(mk, a["n"], 1, u["e"]), ALU.mult,
                          after=[t_out, u["tmp"].after], on=k.G)
            if u["e"] == L1_E - 1:
                k.scratch.put(a["o"], u["t"])

        def over_heads(u):
            a, e = u["tile"], u["e"]
            u["t"] = k.red(a["mixd"][:, e * L1_DH:(e + 1) * L1_DH], u["tmp"][:, :].rearrange("p (h d) -> p d h", d=L1_DH),
                           ALU.add, after=[u["t"], a["mixd"].after])
            k.scratch.put(u["tmp"], u["t"])
            a["ts"].append(u["t"])

        pieces = ((0, P), (1, P), (2, L1_E * L1_DH - 2 * P))

        def turn(u):
            if u["e"] < L1_E - 1:
                return
            a = u["tile"]
            a["bank"], mixd = k.banks.take(), a["mixd"]
            u["t"] = k.turn([(a["bank"][0:w, c * P:(c + 1) * P], mixd[:, c * P:c * P + w]) for c, w in pieces],
                            after=[a["ts"], a["bank"].after])
            k.scratch.put(mixd, u["t"])

        def copy(u):
            if u["e"] < L1_E - 1:
                return
            bank, at = u["tile"]["bank"], k.scratch.take()
            u["t"] = [k.acopy(at[:, 0:2 * P], bank[:, 0:2 * P], after=[u["t"], at.after]),
                      k.acopy(at[0:64, 2 * P:3 * P], bank[0:64, 2 * P:3 * P], after=u["t"])]
            k.banks.put(bank, u["t"])
            u["at"] = at

        def project_out(u):
            if u["e"] < L1_E - 1:
                return
            n, at, bank = u["tile"]["n"], u["at"], k.banks.take()
            t = k.mm([(bank[:, 0:P], Wo[0:w, c, :], at[0:w, c * P:(c + 1) * P]) for c, w in pieces],
                     after=[u["t"], bank.after])
            k.scratch.put(at, t)
            t = k.acopy(fo[:, n * P:(n + 1) * P], bank[:, 0:P], after=[t, fo.after])
            k.banks.put(bank, t)
            fo_tokens.append(t)

        units = [{"tile": a, "e": e} for a in tiles_out for e in range(L1_E)]
        yield from staged(units, (0, kept_heads), (1, over_heads), (2, turn), (3, copy), (4, project_out))
        if b == BPG - 1:
            routed.pop(g)
            for s in (sg, mk):
                k.scratch.put(s, [t_g, [a["ts"] for a in tiles_out], t_out])
            t = k.act(fo[:, :], fo[:, :], ACT.Silu, after=fo_tokens)
            yield from k.gate_and_add(g, None, t, mixed[g], silu=fo)
            passed.append(g)

    attended = []

    def attend_and_count(bt):
        yield from attend(bt)
        attended.append(bt)

    lane = lambda n, may_start, part: Lane([(lambda m=m: may_start(m), lambda m=m: part(m)) for m in range(n)])
    yield [lane(BATCH, lambda bt: bt in outputs and mixed[bt // BPG] is not None, combine),
           lane(GROUPS, lambda g: normed(g) and len(passed) >= g - 1, recurrence),
           lane(BATCH, lambda bt: bt in projected, attend_and_count),
           lane(GROUPS, lambda g: normed(g) and len(attended) >= BPG * (g - 1), route),
           lane(BATCH, lambda bt: bt // BPG in routed and len(attended) >= bt - 1, project)], passed


def layouts1(a):
    T = lambda n: a[n].T
    cols = np.concatenate([columns(a["L1_attn_" + n]) for n in
                           ("in_b", "gate_b", "b_b", "c_b", "d_b", "a_log", "out_b", "norm_w")] +
                          [np.zeros((P, 2), np.float32)], axis=1)
    H, E, DH = L1_H, L1_E, L1_DH
    by_expert = lambda w: w.reshape(P, H, E, DH).transpose(0, 2, 1, 3).reshape(P, E * H * DH)
    kv = a["L1_ffn_Wkv"].reshape(P, 2, H * E * DH)
    return {"L1_Iw": T("L1_attn_in_w"), "L1_Gw": T("L1_attn_gate_w"), "L1_Bw": T("L1_attn_b_w"),
            "L1_Cw": T("L1_attn_c_w"), "L1_Dw": T("L1_attn_d_w"), "L1_Ow": T("L1_attn_out_w"), "L1_cols": cols,
            "L1_Wsd": np.concatenate([a["L1_ffn_Ws"], a["L1_ffn_Wd"]], axis=1),
            "L1_Wq": by_expert(a["L1_ffn_Wq"]), "L1_Wk": by_expert(kv[:, 0]), "L1_Wv": by_expert(kv[:, 1]),
            "L1_Wo": a["L1_ffn_Wo"].reshape(DH, E, P).transpose(1, 0, 2).reshape(E * DH, P)}


L2_HEADS, L2_DH = 16, 64
L2_PAIRS = L2_HEADS // 2
L2_FF = 2


def top2_gates(k, gates, pr, t_p, weight, spare, both=None):
    W = TILES * EXPERTS
    v3 = lambda s: s[:, 0:W].rearrange("p (n w) -> p n w", w=EXPERTS)
    sc, tmp, m1, m2, col = spare
    t = k.vcopy(sc[:, 0:W], pr[:, 0:W], after=[t_p, [s.after for s in spare]])
    yield
    t1 = yield from k.one_hot_first(m1[:, 0:W], sc[:, 0:W], tmp[:, 0:W], col[:, 0:TILES], weight, TILES, EXPERTS, after=t)
    yield
    t = k.stt(sc[:, 0:W], m1[:, 0:W], -4.0, sc[:, 0:W], ALU.mult, ALU.add, after=t1)
    yield
    t2 = yield from k.one_hot_first(m2[:, 0:W], sc[:, 0:W], tmp[:, 0:W], col[:, 0:TILES], weight, TILES, EXPERTS, after=t)
    yield
    if both is not None:
        return [t1, t2]
    t = k.tt(tmp[:, 0:W], m1[:, 0:W], m2[:, 0:W], ALU.add, after=[t1, t2])
    yield
    t = k.tt(gates, tmp[:, 0:W], pr[:, 0:W], ALU.mult, after=t)
    g3 = gates.rearrange("p (n w) -> p n w", w=EXPERTS)
    t = k.red(col[:, 0:TILES], g3, ALU.add, after=t)
    yield
    t = k.recip(col[:, 0:TILES], col[:, 0:TILES], after=t)
    return k.tt(g3, g3, col[:, 0:TILES].unsqueeze(2).to_broadcast([P, TILES, EXPERTS]), ALU.mult, after=t)


def layer2(k, region):
    nc, ins = k.nc, k.ins
    take = region.take
    Wqk = take("p (n) -> p n", n=P)
    Wv = take("p (n) -> p n", n=L2_DH)
    Fqk = take("p (n) -> p n", n=L2_HEADS * L2_DH)
    Fv = take("p (n) -> p n", n=L2_HEADS * L2_DH)
    Fv_b = take("p (n) -> p n", n=L2_HEADS * L2_DH)
    Fo = take("p (c n) -> p c n", c=L2_PAIRS, n=P)
    cols = take("p (n) -> p n", n=2 * L2_PAIRS + 1)
    W1 = take("p (e f) -> p e f", e=EXPERTS, f=L2_FF * P)
    W2 = take("p (e c d) -> p e c d", e=EXPERTS, c=L2_FF, d=P)
    b1 = take("p (n) -> p n", n=EXPERTS * L2_FF)
    b2 = take("p (n) -> p n", n=P)[0:EXPERTS, :]
    Wg = take("p (n) -> p n", n=EXPERTS)
    gates = take("p (n) -> p n", n=TILES * EXPERTS)
    weight = take("p (n w) -> p n w", n=TILES, w=EXPERTS)
    loaded = k.load("L2", [(Wg, ins["L2_Wg"][:, :]), (Wqk, ins["L2_Wqk"][:, :]), (Wv, ins["L2_Wv"][:, :]),
                           (cols, ins["L2_cols"][:, :]), (Fqk, ins["L2_Fqk"][:, :]), (Fv[0:L2_DH, :], ins["L2_Fv"][:, :]),
                           (Fv_b, ins["L2_Fv_b"][:, :].broadcast_to([P, L2_HEADS * L2_DH])),
                           (Fo, ins["L2_Fo"][:, :].rearrange("(c p) n -> p c n", p=P))], after=region.free_after)
    big = k.load("L2_experts", [(b1, ins["L2_b1"][:, :]), (b2, ins["L2_b2"][:, :]),
                                (W1, ins["L2_W1"].rearrange("e d f -> d e f"))] +
                 [(W2[:, e, :, :], ins["L2_W2"][e, :, :].rearrange("(c p) d -> p c d", p=P)) for e in range(EXPERTS)])
    yield
    k.phase("L2")
    mixed, normed = [None] * GROUPS, k.normed_for(k.started)
    fq_b, fk_b, fo_b = cols[:, 0:8], cols[:, 8:16], cols[:, 16:17]
    const = [k.fill(weight[:, :, e:e + 1], float(EXPERTS - e), after=region.free_after) for e in range(EXPERTS)]
    k.V.wait([const, loaded])
    k.A.wait(loaded)
    k.T.wait(loaded)

    def route():
        lg, pr, t_p = yield from k.softmax_experts("L2", Wg, loaded)
        k.scratch.put(lg, t_p)
        spare = [k.scratch.take() for _ in range(5)]
        t_gates = yield from top2_gates(k, gates, pr, t_p, weight.rearrange("p n w -> p (n w)"), spare)
        for s in spare + [pr]:
            k.scratch.put(s, t_gates)
        yield
        return (yield from k.gates_to_rows(gates, "L2", t_gates))

    def attention(g):
        x = k.cols(k.xn, g)
        bz, bv, zqk, zv = k.banks.take(), k.banks.take(), k.scratch.take(), k.scratch.take()
        t = k.mm([(bz[:, :], Wqk, x)], after=[bz.after, k.xn_ready[g]])
        t_z = k.acopy(zqk[:, :], bz[:, :], after=[t, zqk.after])
        t = k.mm([(bv[0:L2_DH, :], Wv, x)], after=bv.after)
        t_zv = k.acopy(zv[0:L2_DH, :], bv[0:L2_DH, :], after=[t, zv.after])
        k.banks.put(bz, t_z)
        k.banks.put(bv, t_zv)
        yield
        v = [[None, None] for _ in range(TPG)]
        for i in range(TPG):
            for c in range(2):
                b, s = k.banks.take(), k.scratch.take()
                t_fv = k.mm([(b[:, :], zv[0:L2_DH, i * P:(i + 1) * P], Fv[0:L2_DH, c * GW:(c + 1) * GW])], after=[b.after, t_zv])
                t = k.tt(s[:, :], b[:, :], Fv_b[:, c * GW:(c + 1) * GW], ALU.add, after=[t_fv, s.after])
                k.banks.put(b, t)
                v[i][c] = (s, t)
                yield
        k.scratch.put(zv, t_fv)
        acc = k.banks.take()
        pairs, state = {}, {}

        def query_key(u):
            m, b, half = u["m"], u["b"], u["half"]
            if b == 0 and half == 0:
                qk = []
                for r, bias, scale in ((0, fq_b, L2_DH ** -0.5), (L2_DH, fk_b, 1.0)):
                    bk, s = k.banks.take(), k.scratch.take()
                    t = k.mm([(bk[:, :], Fqk[r:r + L2_DH, m * P:(m + 1) * P], zqk[r:r + L2_DH, :])], after=[bk.after, t_z])
                    t = k.ts(s[:, :], bk[:, :], bias[:, m:m + 1], scale, ALU.add, ALU.mult, after=[t, s.after])
                    k.banks.put(bk, t)
                    qk.append((s, t))
                pairs[m] = {"qk": qk}
            qk = pairs[m]["qk"]
            r, sl = half * L2_DH, slice(b * SEQ, (b + 1) * SEQ)
            scores(k, u, qk[0][0][r:r + L2_DH, sl], qk[1][0][r:r + L2_DH, sl], [qk[0][1], qk[1][1]])

        def exps(u):
            u["sums"] = k.stats.take()
            exponentials(k, u, u["sums"][:, 0:2], u["sums"].after)

        def normalise(u):
            rs, p, t_e = u["sums"], u["p"], u["t"]
            t_r = k.recip(rs[:, 0:2], rs[:, 0:2], after=t_e)
            u["t"] = [k.ts(p[:, i * SEQ:(i + 1) * SEQ], p[:, i * SEQ:(i + 1) * SEQ], rs[:, i:i + 1], None, ALU.mult,
                           after=[t_r, t_e]) for i in range(2)]
            k.stats.put(rs, u["t"])

        def turn(u):
            u["pt"], u["t"] = turned_scores(k, u["p"], u["t"], (2 * u["m"] + u["half"]) % 2 == 0)

        def times_v(u):
            m, b, half = u["m"], u["b"], u["half"]
            if b == 0 and half == 0:
                pairs[m]["O"] = k.banks.take()
            O = pairs[m]["O"]
            h = 2 * m + half
            cs = slice((h % 8) * L2_DH, (h % 8 + 1) * L2_DH)
            r = half * L2_DH
            vv = [v[2 * b + jc][h // 8] for jc in range(2)]
            t = k.mm([(O[r:r + L2_DH, b * SEQ:(b + 1) * SEQ], vv[jc][0][:, cs], u["pt"][:, jc * SEQ:(jc + 1) * SEQ])
                      for jc in range(2)], after=[u["t"], vv[0][1], vv[1][1], O.after])
            k.scratch.put(u["pt"], t)
            if b == BPG - 1 and half == 1:
                s = k.scratch.take()
                pairs[m]["s"], pairs[m]["t"] = s, k.acopy(s[:, :], O[:, :], after=[t, s.after])
                k.banks.put(O, pairs[m]["t"])
                for q, _ in pairs[m]["qk"]:
                    k.scratch.put(q, t)

        def fold(u):
            m = u["m"]
            if u["b"] == BPG - 1 and u["half"] == 1:
                state["t"] = k.mm([(acc[:, :], Fo[:, m, :], pairs[m]["s"][:, :])],
                                  after=[pairs[m]["t"]] + ([acc.after] if m == 0 else []),
                                  start=(m == 0), stop=(m == L2_PAIRS - 1))
                k.scratch.put(pairs[m]["s"], state["t"])

        units = [{"m": m, "b": b, "half": half} for m in range(L2_PAIRS) for b in range(BPG) for half in range(2)]
        yield from staged(units, (0, query_key), (1, exps), (2, normalise), (4, turn), (6, times_v), (8, fold))
        k.scratch.put(zqk, state["t"])
        for i in range(TPG):
            for s, _ in v[i]:
                k.scratch.put(s, state["t"])
        s = k.scratch.take()
        s.token = k.act(s[:, :], acc[:, :], ACT.Identity, bias=fo_b, after=[state["t"], s.after])
        k.banks.put(acc, s.token)
        mixed[g] = s
        yield

    def ffn(g, gate_rows):
        k.T.wait(big)
        acc = k.banks.take()

        def hidden(e, f, x):
            b, s = k.banks.take(), k.scratch.take()
            t = k.mm([(b[:, :], W1[:, e, f * P:(f + 1) * P], x)], after=b.after)
            n = e * L2_FF + f
            t = k.act(s[:, :], b[:, :], ACT.Relu, bias=b1[:, n:n + 1], after=[t, s.after, big])
            k.banks.put(b, t)
            return {"slot": s, "t": t}

        def gated(u, gate):
            s = u["slot"]
            return k.tt(s[:, :], s[:, :], gate[:, :], ALU.mult, after=[u["t"], gate.token])

        yield from k.experts(g, gate_rows, acc, L2_FF, hidden, gated, lambda e, f: W2[:, e, f, :], b2, after=big)
        yield from k.gate_and_add(g, acc, k.t_acc[g], mixed[g])

    yield layer_lanes(route, attention, ffn, mixed, normed)


def layouts2(a):
    return {"L2_Wqk": np.concatenate([a["L2_attn_wq"], a["L2_attn_wk"]], axis=1), "L2_Wv": a["L2_attn_wv"],
            "L2_Fqk": np.concatenate([a["L2_attn_fcq_w"], a["L2_attn_fck_w"]], axis=0), "L2_Fv": a["L2_attn_fcv_w"],
            "L2_Fv_b": a["L2_attn_fcv_b"].reshape(1, -1), "L2_Fo": a["L2_attn_fco_w"],
            "L2_cols": np.concatenate([columns(a["L2_attn_" + n]) for n in ("fcq_b", "fck_b", "fco_b")], axis=1),
            "L2_Wg": a["L2_ffn_Wg"], "L2_W1": a["L2_ffn_W1"], "L2_W2": a["L2_ffn_W2"],
            "L2_b1": columns(a["L2_ffn_b1"]), "L2_b2": a["L2_ffn_b2"]}


L3_H, L3_D = 4, 32
L3_CONV = 4
L3_FIRS = (3, 15, 63)
L3_LMAX = max(L3_FIRS)
L3_CHUNK = 32
L3_CPT = P // L3_CHUNK
L3_CHUNKS = SEQ // L3_CHUNK
L3_PATHS = 5
L3_LEVELS = 5
L3_FF = 2
L3_CAPACITY = -(-2 * TOKENS * 5 // (EXPERTS * 4))
L3_PE_TAPS = 12


def l3_constants():
    r, c = np.arange(P)[:, None], np.arange(P)[None, :]
    same = r // L3_CHUNK == c // L3_CHUNK
    masks = [(r >> (n + 1) == c >> (n + 1)) & ((r >> n) % 2 == 0) & ((c >> n) % 2 == 1) for n in range(L3_LEVELS)]
    masks.append(same & (r <= c))
    masks.append(same)
    masks.append(r < c)
    path = np.zeros((P, L3_PATHS, P), np.float32)
    for h in range(L3_H):
        for p in range(L3_PATHS):
            path[h * L3_PATHS + p, p, h * L3_D:(h + 1) * L3_D] = 1.0
    return np.concatenate([np.concatenate(masks, axis=1).astype(np.float32), path.reshape(P, -1)], axis=1)


def layer3(k, region, spare_words, other):
    nc, ins = k.nc, k.ins
    take = region.take
    Wqkv = take("p (n) -> p n", n=3 * P)
    Wo = take("p (n) -> p n", n=P)
    Wb = take("p (n) -> p n", n=L3_H)
    taps = take("p (n) -> p n", n=3 * L3_CONV + sum(L3_FIRS) + 1)
    GW_ = take("p (n) -> p n", n=L3_H * L3_PATHS)
    row = take("p (n) -> p n", n=L3_H * (L3_PATHS + 2))
    consts = take("p (n) -> p n", n=8 * P + L3_PATHS * P)
    mask = [consts[:, i * P:(i + 1) * P] for i in range(8)]
    path = consts[:, 8 * P:].rearrange("p (q n) -> p q n", q=L3_PATHS)[0:L3_H * L3_PATHS]
    causal, head_block, earlier = mask[5], mask[6], mask[7]
    Wbx = take("p (h d) -> p h d", h=L3_H, d=L3_D)
    head_mean = take("p (n) -> p n", n=P)
    all_ones = take("p (n) -> p n", n=P)
    W1 = take("p (e f) -> p e f", e=EXPERTS, f=2 * L3_FF * P)
    W2 = take("p (e c d) -> p e c d", e=EXPERTS, c=L3_FF, d=P)
    Wg = take("p (n) -> p n", n=EXPERTS)
    gates = take("p (n) -> p n", n=TILES * EXPERTS)
    weight = take("p (n w) -> p n w", n=TILES, w=EXPERTS)
    NP = L3_H * L3_PATHS
    probs = take("p (n) -> p n", n=TILES * NP)
    loaded = k.load("L3", [(Wqkv, ins["L3_Wqkv"][:, :]), (Wo, ins["L3_Wo"][:, :]), (Wb, ins["L3_Wb"][:, :]),
                           (taps, ins["L3_taps"][:, :]), (GW_, ins["L3_gate_w"][:, :]), (consts, ins["L3_consts"][:, :]),
                           (row, ins["L3_row"][:, :].broadcast_to([P, L3_H * (L3_PATHS + 2)])), (Wg, ins["L3_Wg"][:, :])],
                    after=region.free_after)
    big = k.load("L3_experts", [(W1, ins["L3_W1"].rearrange("e d f -> d e f"))] +
                 [(W2[:, e, :, :], ins["L3_W2"][e, :, :].rearrange("(c p) d -> p c d", p=P)) for e in range(EXPERTS)])
    yield
    k.phase("L3")
    mixed, normed = [None] * GROUPS, k.normed_for(k.started)
    free = region.free_after
    const = [k.fill(weight[:, :, e:e + 1], float(EXPERTS - e), after=free) for e in range(EXPERTS)]
    const.append(k.fill(all_ones, 1.0, after=free))
    const.append(k.ts(head_mean, head_block, 1.0 / L3_D, None, ALU.mult, after=[loaded, free]))
    const.append(k.vcopy(Wbx, Wb.unsqueeze(2).to_broadcast([P, L3_H, L3_D]), after=[loaded, free]))
    conv_w = [taps[:, i * L3_CONV:(i + 1) * L3_CONV] for i in range(3)]
    fir_at = [3 * L3_CONV + sum(L3_FIRS[:i]) for i in range(3)]
    fir_w = [taps[:, a:a + n] for a, n in zip(fir_at, L3_FIRS)]
    norm_w = taps[:, fir_at[2] + L3_FIRS[2]:fir_at[2] + L3_FIRS[2] + 1]
    CP, VP = L3_CONV - 1, L3_LMAX - 1
    pads = Pool([Slot(spare_words.take("p (b t) -> p b t", b=BPG, t=CP + SEQ), i) for i in range(2)])
    vpads = Pool([Slot(region.take("p (b t) -> p b t", b=BPG, t=VP + SEQ), i) for i in range(3)])
    for s in pads.free:
        s.after = flat([k.fill(s[:, :, 0:CP], 0.0, after=free), free])
    for s in vpads.free:
        s.after = flat([k.fill(s[:, :, 0:VP], 0.0, after=free), free])
    gate_b, log_t, eps = row[:, 0:NP], row[:, NP:NP + L3_H], row[:, NP + L3_H:NP + 2 * L3_H]
    rs = k.scratch.take()
    inv_t, keep = rs[:, 0:L3_H], rs[:, L3_H:2 * L3_H]
    t1 = k.act(inv_t, log_t, ACT.Exp, scale=-1.0, after=[loaded, rs.after])
    t = k.ts(eps, eps, 0.0, 0.2, ALU.max, ALU.min, after=loaded)
    t2 = k.ts(keep, eps, -5.0, 1.0, ALU.mult, ALU.add, after=[t, rs.after])
    k.V.wait([const, loaded, t1, t2])
    k.T.wait([const, loaded])

    diag, t_diag = other.take("p (j n) -> p j n", j=L3_PE_TAPS, n=P), []
    done_before = {}

    def path_gates():
        for j in range(L3_PE_TAPS):
            t_diag.append(k.ts(diag[:, j, :], k.ident[:, :], fir_w[2][:, j:j + 1], None, ALU.mult,
                               after=[loaded, list(k.x_ready)]))
            yield
        HT = 16
        for half in range(TILES // HT):
            bank, cl = k.banks.take(), k.scratch.take()
            n = HT * NP
            t = k.mms([(bank[:, i * NP:(i + 1) * NP], k.xn[:, (half * HT + i) * P:(half * HT + i + 1) * P], GW_)
                       for i in range(HT)], after=[bank.after, k.xn_ready])
            yield
            pr = probs[:, half * n:(half + 1) * n]
            rows = pr.rearrange("p (n w) -> p n w", w=L3_PATHS)
            c = cl[:, 0:HT * L3_H]
            bc = c.unsqueeze(2).to_broadcast([P, HT * L3_H, L3_PATHS])
            by_tile = pr.rearrange("p (i n) -> p i n", i=HT)
            t = k.tt(by_tile, bank[:, 0:n].rearrange("p (i n) -> p i n", i=HT), gate_b.unsqueeze(1).to_broadcast([P, HT, NP]),
                     ALU.add, after=[t, free])
            k.banks.put(bank, t)

            def per_head(v, op, t):
                toks = []
                for h in range(L3_H):
                    a = by_tile[:, :, h * L3_PATHS:(h + 1) * L3_PATHS]
                    toks.append(k.ts(a, a, v[:, h:h + 1], None, op, after=t))
                return toks
            yield
            t = per_head(inv_t, ALU.mult, t)
            yield
            t = k.red(c, rows, ALU.max, after=[t, cl.after])
            yield
            t = k.tt(rows, rows, bc, ALU.subtract, after=t)
            yield
            t_e = k.act(pr, pr, ACT.Exp, after=t)
            yield
            t = k.red(c, rows, ALU.add, after=[t_e, t])
            yield
            t = k.recip(c, c, after=t)
            yield
            t = k.tt(rows, rows, bc, ALU.mult, after=t)
            k.scratch.put(cl, t)
            yield
            t = per_head(keep, ALU.mult, t)
            yield
            t_probs = per_head(eps, ALU.add, t)
        k.scratch.put(rs, t_probs)
        done_before["probs"] = t_probs

    def expert_gates():
        W = TILES * EXPERTS
        v3 = lambda a: a.rearrange("p (n w) -> p n w", w=EXPERTS)
        lg, pr, t_p = yield from k.softmax_experts("L3", Wg, loaded)
        k.scratch.put(lg, t_p)
        spare = [k.scratch.take() for _ in range(5)]
        sc, tmp, m1, m2, col = spare
        t = yield from top2_gates(k, None, pr, t_p, weight.rearrange("p n w -> p (n w)"), spare, both=True)
        total = k.scratch.take()
        base = None
        kept = []
        for which, m in enumerate((m1, m2)):
            loc, tot = k.banks.take(), k.banks.take()
            t_l = k.mm([(loc[:, 0:W], earlier, m[:, 0:W])], after=[t, loc.after])
            t_t = k.mm([(tot[:, 0:W], all_ones, m[:, 0:W])], after=[t, tot.after])
            yield
            t_c = k.vcopy(sc[:, 0:W], tot[:, 0:W], after=[t_t, kept])
            yield
            t_s = [k.scan(tmp[:, e:W:EXPERTS], all_ones[:, 0:TILES], sc[:, e:W:EXPERTS], after=[t_c, kept])
                   for e in range(EXPERTS)]
            yield
            t_x = k.tt(sc[:, 0:W], tmp[:, 0:W], sc[:, 0:W], ALU.subtract, after=t_s)
            t_x = k.tt(sc[:, 0:W], sc[:, 0:W], loc[:, 0:W], ALU.add, after=[t_x, t_l])
            if which == 1:
                t_x = k.tt(v3(sc[:, 0:W]), v3(sc[:, 0:W]), total[:, 0:EXPERTS].unsqueeze(1).to_broadcast([P, TILES, EXPERTS]),
                           ALU.add, after=[t_x, base])
            else:
                base = k.vcopy(total[:, 0:EXPERTS], tmp[:, W - EXPERTS:W], after=[t_s, total.after])
            k.banks.put(loc, t_x)
            k.banks.put(tot, t_c)
            yield
            t_k = k.stt(m[:, 0:W], sc[:, 0:W], float(L3_CAPACITY), m[:, 0:W], ALU.is_lt, ALU.mult, after=[t_x, t_l, t_t])
            kept = [kept, t_k, base]
        yield
        t = k.tt(sc[:, 0:W], m1[:, 0:W], m2[:, 0:W], ALU.add, after=kept)
        yield
        t = k.tt(gates, sc[:, 0:W], pr[:, 0:W], ALU.mult, after=[t, free])
        yield
        t = k.red(col[:, 0:TILES], v3(gates), ALU.add, after=t)
        yield
        t = k.ts(col[:, 0:TILES], col[:, 0:TILES], 1e-9, None, ALU.max, after=t)
        yield
        t = k.recip(col[:, 0:TILES], col[:, 0:TILES], after=t)
        yield
        t_gates = k.tt(v3(gates), v3(gates), col[:, 0:TILES].unsqueeze(2).to_broadcast([P, TILES, EXPERTS]), ALU.mult, after=t)
        for s in spare + [pr, total]:
            k.scratch.put(s, t_gates)
        done_before["rows"] = yield from k.gates_to_rows(gates, "L3", t_gates)

    four = lambda m: m.unsqueeze(1).to_broadcast([P, TPG, P])
    tiles = lambda a: a.rearrange("p (i n) -> p i n", n=P)
    batches = lambda a: a.rearrange("p (b t) -> p b t", b=BPG)

    def unit_rows(s, t, eps_col, weights, scale_col=None):
        sq, b = k.scratch.take(), k.banks.take()
        t1 = k.act(sq[:, :], s[:, :], ACT.Square, after=[t, sq.after])
        yield
        t1 = k.mm([(b[:, :], weights, sq[:, :])], after=[t1, b.after])
        yield
        t1 = k.inverse_root(sq[:, :], b, eps_col, t1)
        yield
        if scale_col is None:
            t1 = k.tt(s[:, :], s[:, :], sq[:, :], ALU.mult, after=[t1, t])
        else:
            t1 = k.stt(s[:, :], s[:, :], scale_col, sq[:, :], ALU.mult, ALU.mult, after=[t1, t])
        k.scratch.put(sq, t1)
        return t1

    prepared = {}

    def front(g):
        x = k.cols(k.xn, g)
        def project(u):
            u["b"] = k.banks.take()
            w = Wbx.rearrange("p h d -> p (h d)") if u["n"] == 3 else Wqkv[:, u["n"] * P:(u["n"] + 1) * P]
            u["t"] = k.mm([(u["b"][:, :], w, x)], after=[u["b"].after, k.xn_ready[g]])

        def copy(u):
            if u["n"] == 3:
                u["s"] = k.scratch.take()
                u["t"] = k.act(u["s"][:, :], u["b"][:, :], ACT.Sigmoid, after=[u["t"], u["s"].after])
            else:
                u["pad"] = pads.take()
                u["t"] = k.acopy(u["pad"][:, :, CP:], batches(u["b"][:, :]), after=[u["t"], u["pad"].after])
            k.banks.put(u["b"], u["t"])

        def convolve(u):
            if u["n"] == 3:
                return
            n, pad, s = u["n"], u["pad"], k.scratch.take()
            t = k.ts(batches(s[:, :]), pad[:, :, 0:SEQ], conv_w[n][:, 0:1], None, ALU.mult, after=[u["t"], s.after])
            for j in range(1, L3_CONV):
                t = k.stt(batches(s[:, :]), pad[:, :, j:j + SEQ], conv_w[n][:, j:j + 1], batches(s[:, :]), ALU.mult, ALU.add,
                          after=t)
            pads.put(pad, t)
            u["s"], u["t"] = s, t

        def silu(u):
            s = u.get("s")
            if u["n"] < 2:
                u["t"] = k.act(s[:, :], s[:, :], ACT.Silu, after=u["t"])
            elif u["n"] == 2:
                u["v"] = vpads.take()
                u["t"] = k.act(u["v"][:, :, VP:], batches(s[:, :]), ACT.Silu, after=[u["t"], u["v"].after])
                k.scratch.put(s, u["t"])
                values[g] = (u["v"], u["t"])

        def square(u):
            if u["n"] < 2:
                u["sq"] = k.scratch.take()
                u["t"] = k.act(u["sq"][:, :], u["s"][:, :], ACT.Square, after=[u["t"], u["sq"].after])

        def norm(u):
            if u["n"] < 2:
                u["b"] = k.banks.take()
                u["t"] = k.mm([(u["b"][:, :], head_block, u["sq"][:, :])], after=[u["t"], u["b"].after])

        def root(u):
            if u["n"] < 2:
                u["t"] = k.inverse_root(u["sq"][:, :], u["b"], k.eps[:, 1:2], u["t"])

        def scale(u):
            if u["n"] < 2:
                u["t"] = k.tt(u["s"][:, :], u["s"][:, :], u["sq"][:, :], ALU.mult, after=u["t"])
                k.scratch.put(u["sq"], u["t"])

        units = [{"n": n} for n in (0, 1, 2, 3)]
        yield from staged(units, (0, project), (1, copy), (2, convolve), (3, silu), (4, square), (5, norm), (6, root), (7, scale))
        q, kk, v, beta = units[0]["s"], units[1]["s"], units[2]["v"], units[3]["s"]
        t_q, t_k, t_v, t = [u["t"] for u in units]
        kb, vb = k.scratch.take(), k.scratch.take()
        t_kb = k.tt(kb[:, :], kk[:, :], beta[:, :], ALU.mult, after=[t, t_k, kb.after])
        t_vb = k.tt(batches(vb[:, :]), v[:, :, VP:], batches(beta[:, :]), ALU.mult, after=[t, t_v, vb.after])
        k.scratch.put(beta, [t_kb, t_vb])
        yield

        def turn(u):
            u["b"] = k.banks.take()
            u["t"] = k.turn([(u["b"][:, i * P:(i + 1) * P], u["s"][:, i * P:(i + 1) * P]) for i in range(TPG)],
                            after=[u["t"], u["b"].after])

        def copy_turned(u):
            u["o"] = k.scratch.take()
            t = k.acopy(u["o"][:, :], u["b"][:, :], after=[u["t"], u["o"].after])
            k.banks.put(u["b"], t)
            u["turned"], u["t"] = u["t"], t

        units = [{"s": s, "t": t} for s, t in ((kk, t_k), (kb, t_kb), (vb, t_vb))]
        yield from staged(units, (0, turn), (1, copy_turned))
        k.scratch.put(vb, units[2]["turned"])
        nat = [(u["o"], u["t"]) for u in units]
        fronts[g] = (q, t_q), (kk, t_k), (kb, t_kb), nat

    def invert(g):
        (q, t_q), (kk, t_k), (kb, t_kb), nat = fronts.pop(g)
        (k_nat, t_kn), (kb_nat, t_kbn), (vb_nat, t_vbn) = nat
        u, w = k.scratch.take(), k.scratch.take()
        t_u, t_w = [], []

        def inverse(h):
            r = slice(h * L3_D, (h + 1) * L3_D)
            b, gram, inv, invT, lm = k.banks.take(), *[k.scratch.take() for _ in range(4)]
            t = k.mms([(b[:, i * P:(i + 1) * P], kk[r, i * P:(i + 1) * P], kb[r, i * P:(i + 1) * P]) for i in range(TPG)],
                      after=[t_k, t_kb, b.after])
            yield
            gram_read.append(t)
            t_g = k.acopy(gram[:, :], b[:, :], after=[t, gram.after])
            k.banks.put(b, t_g)
            yield
            t = k.tt(tiles(lm[:, :]), tiles(gram[:, :]), four(mask[0]), ALU.mult, after=[t_g, lm.after], on=k.G)
            t_lm = k.G.run(lambda eng: eng.tensor_tensor(tiles(invT[:, :]), four(k.ident[:, :]), tiles(lm[:, :]), ALU.subtract),
                           [t, invT.after])
            t_T = t_lm
            t_i = k.V.run(lambda eng: eng.transpose(inv[:, :], invT[:, :]), [t_T, inv.after])
            t_read = t_lm
            yield
            for n in range(1, L3_LEVELS):
                t_lm = k.tt(tiles(lm[:, :]), tiles(gram[:, :]), four(mask[n]), ALU.mult, after=t_read, on=k.G)
                yield
                bx, xs = k.banks.take(), k.scratch.take()
                t = k.mms([(bx[:, i * P:(i + 1) * P], lm[:, i * P:(i + 1) * P], inv[:, i * P:(i + 1) * P]) for i in range(TPG)],
                          after=[t_lm, t_i, bx.after])
                yield
                t_read = t
                t = k.acopy(xs[:, :], bx[:, :], after=[t, xs.after])
                k.banks.put(bx, t)
                yield
                by = k.banks.take()
                t_y = k.mms([(by[:, i * P:(i + 1) * P], invT[:, i * P:(i + 1) * P], xs[:, i * P:(i + 1) * P]) for i in range(TPG)],
                            after=[t, t_T, by.after])
                yield
                k.scratch.put(xs, t_y)
                t_i = k.tt(inv[:, :], inv[:, :], by[:, :], ALU.subtract, after=[t_y, t_i, t_read])
                k.banks.put(by, t_i)
                t_T = k.V.run(lambda eng: eng.transpose(invT[:, :], inv[:, :]), [t_i, t_y])
                yield
            k.scratch.put(gram, t_lm)
            k.scratch.put(lm, t_read)
            k.scratch.put(inv, t_T)
            cs = slice(h * L3_D, (h + 1) * L3_D)
            bu, bw = k.banks.take(), k.banks.take()
            of_head = lambda a: tiles(a)[:, :, cs]
            tu = k.mms([(bu[:, i * L3_D:(i + 1) * L3_D], invT[:, i * P:(i + 1) * P], vb_nat[:, i * P + h * L3_D:i * P + (h + 1) * L3_D])
                        for i in range(TPG)], after=[t_T, t_vbn, bu.after])
            tw = k.mms([(bw[cs, i * P:(i + 1) * P], kb_nat[:, i * P + h * L3_D:i * P + (h + 1) * L3_D], invT[:, i * P:(i + 1) * P])
                        for i in range(TPG)], after=[t_T, t_kbn, bw.after])
            yield
            t_u.append(k.acopy(of_head(u[:, :]), bu[:, 0:TPG * L3_D].rearrange("p (i d) -> p i d", d=L3_D), after=[tu, u.after]))
            t_w.append(k.acopy(w[cs, :], bw[cs, :], after=[tw, w.after]))
            k.banks.put(bu, t_u[-1])
            k.banks.put(bw, t_w[-1])
            k.scratch.put(invT, [tu, tw])
            done.append([tu, tw])
            yield

        gram_read, done = [], []
        for pair in ((0, 1), (2, 3)):
            two = [inverse(h) for h in pair]
            live = list(two)
            while live:
                for gen in list(live):
                    if next(gen, "end") == "end":
                        live.remove(gen)
                yield
        k.scratch.put(kb, gram_read)
        k.scratch.put(kb_nat, done)
        k.scratch.put(vb_nat, done)
        prepared[g] = dict(q=(q, t_q), k=(kk, [t_k, gram_read]), k_nat=(k_nat, t_kn), u=(u, t_u), w=(w, t_w))
        yield

    def path_rows(g):
        b, pt = k.banks.take(), k.scratch.take()
        t = k.turn([(b[0:NP, i * P:(i + 1) * P], probs[:, (TPG * g + i) * NP:(TPG * g + i + 1) * NP]) for i in range(TPG)],
                   after=[b.after, done_before["probs"]])
        t_pt = k.acopy(pt[0:NP, :], b[0:NP, :], after=[t, pt.after])
        k.banks.put(b, t_pt)
        return pt, t_pt

    def taken(v, n, j):
        at = VP - L3_FIRS[n] + 1 + j
        return v[:, :, at:at + SEQ], fir_w[n][:, j:j + 1]

    def filters_of(g):
        v, t_v = values.pop(g)
        sums = {}

        def product(u):
            src, tap = taken(v, u["n"], u["j"])
            s = k.scratch.take()
            u["s"], u["t"] = s, k.act(batches(s[:, :]), src, ACT.Identity, scale=tap, after=[s.after, t_v])

        def add(u):
            if u["j"] == 0:
                sums[u["n"]] = (u["s"], u["t"])
            else:
                s, t = sums[u["n"]]
                t = k.tt(s[:, :], s[:, :], u["s"][:, :], ALU.add, after=[t, u["t"]], on=k.G)
                k.scratch.put(u["s"], t)
                sums[u["n"]] = (s, t)

        short = staged([{"n": n, "j": j} for n in (0, 1) for j in range(L3_FIRS[n])], (0, product), (1, add))
        n, s, t = 2, k.scratch.take(), None
        for j in range(L3_PE_TAPS, L3_FIRS[2]):
            src, tap = taken(v, n, j)
            if t is None:
                t = k.ts(batches(s[:, :]), src, tap, None, ALU.mult, after=[s.after, t_v])
            else:
                t = k.stt(batches(s[:, :]), src, tap, batches(s[:, :]), ALU.mult, ALU.add, after=t)
            if j % 3 == 2:
                next(short, None)
                yield
        for _ in short:
            yield
        sums[2] = (s, t)
        tapped[g] = (v, t_v, sums)
        yield

    def gate_paths(g):
        v, t_v, sums = tapped.pop(g)
        pt, t_pt = path_rows(g)
        b = k.banks.take()
        for j0 in range(0, L3_PE_TAPS, 3):
            j1 = min(L3_PE_TAPS, j0 + 3)
            t = k.mm([(b[:, :], diag[:, j, :], taken(v, 2, j)[0]) for j in range(j0, j1)],
                     after=[t_v, t_diag, b.after], start=(j0 == 0), stop=(j1 == L3_PE_TAPS))
            yield
        s, t_s = sums[2]
        t_s = k.tt(s[:, :], s[:, :], b[:, :], ALU.add, after=[t, t_s])
        k.banks.put(b, t_s)
        sums[2] = (s, t_s)
        o = k.scratch.take()
        state = {"t": None}

        def gate_row(u):
            u["b"] = k.banks.take()
            u["t"] = k.mm([(u["b"][:, :], path[:, u["p"], :], pt[0:NP, :])], after=[t_pt, u["b"].after])

        def times_gate(u):
            dst = u["dst"] = o if state["t"] is None else k.scratch.take()
            state["t"] = state["t"] or [u["t"]]
            u["t"] = k.tt(batches(dst[:, :]), batches(u["b"][:, :]), u["value"], ALU.mult, after=[u["t"], u["t_value"], dst.after])
            u["gated"] = u["t"]
            k.banks.put(u["b"], u["t"])

        def add_path(u):
            if u["dst"] is not o:
                u["t"] = k.tt(o[:, :], o[:, :], u["dst"][:, :], ALU.add, after=[u["t"], state["t"]], on=k.G)
                k.scratch.put(u["dst"], u["t"])
            state["t"] = u["t"]

        units = [{"p": 4, "value": v[:, :, VP:], "t_value": t_v}] + \
                [{"p": n, "value": batches(sums[n][0][:, :]), "t_value": sums[n][1]} for n in (0, 1, 2)]
        yield from staged(units, (0, gate_row), (1, times_gate), (2, add_path))
        for n, u in zip((0, 1, 2), units[1:]):
            k.scratch.put(sums[n][0], u["gated"])
        vpads.put(v, [units[0]["gated"], [t_s for _, t_s in sums.values()], t])
        k.scratch.put(pt, units[-1]["t"])
        filtered[g] = (o, state["t"])

    values, fronts, tapped, filtered, deltas = {}, {}, {}, {}, {}

    def recur(g):
        d = prepared.pop(g)
        (q, t_q), (kk, t_k), (k_nat, t_kn), (u, t_u), (w, t_w) = d["q"], d["k"], d["k_nat"], d["u"], d["w"]
        S = [k.scratch.take(), k.scratch.take()]
        t_S = k.fill(S[0][:, 0:BPG * P], 0.0, after=S[0].after)
        t_read = [[], S[1].after]
        s_bank, o_bank, w_bank = k.banks.take(), k.banks.take(), k.banks.take()
        t_o = []
        t_wread = w_bank.after
        for c in range(L3_CHUNKS):
            cur, nxt = S[c % 2], S[(c + 1) % 2]
            ci, tl = c % L3_CPT, c // L3_CPT
            r = slice(ci * L3_CHUNK, (ci + 1) * L3_CHUNK)
            at = lambda b: (TPG // BPG * b + tl) * P + ci * L3_CHUNK
            rd = []
            if c > 0:
                t = k.mms([(w_bank[r, b * P:(b + 1) * P], w[:, at(b):at(b) + L3_CHUNK], cur[:, b * P:(b + 1) * P])
                           for b in range(BPG)], after=[t_S, t_w, t_wread])
                yield
                rd.append(t)
                uu = tiles(u[:, :])[r, tl::TPG // BPG, :]
                t_u = [t_u, k.tt(uu, uu, w_bank[r, 0:BPG * P].rearrange("p (b n) -> p b n", b=BPG), ALU.subtract, after=[t, t_u])]
                t_wread = t_u[1]
            t = k.mms([(o_bank[:, at(b):at(b) + L3_CHUNK], cur[:, b * P:(b + 1) * P], q[:, at(b):at(b) + L3_CHUNK])
                       for b in range(BPG)], after=[t_S, t_q, o_bank.after])
            rd.append(t)
            t_o.append(t)
            t_read[c % 2] = rd
            yield
            if c < L3_CHUNKS - 1:
                for b in range(BPG):
                    col = (TPG // BPG * b + tl) * P
                    t = k.mm([(s_bank[:, b * P:(b + 1) * P], k_nat[r, col:col + P], u[r, col:col + P])],
                             after=[t_u, t_kn, s_bank.after], start=(c == 0 and b == 0), stop=(c == L3_CHUNKS - 2))
                t_S = k.tt(nxt[:, 0:BPG * P].rearrange("p (b n) -> p b n", b=BPG),
                           s_bank[:, 0:BPG * P].rearrange("p (b n) -> p b n", b=BPG),
                           head_block.unsqueeze(1).to_broadcast([P, BPG, P]), ALU.mult, after=[t, t_read[(c + 1) % 2]])
                k.T.wait(t_S)
                yield
        k.banks.put(s_bank, t_S)
        k.banks.put(w_bank, t_wread)
        for s in S:
            k.scratch.put(s, t_read)
        k.scratch.put(w, t_read)
        k.scratch.put(k_nat, t_S)
        b, dl = k.banks.take(), k.scratch.take()
        t_i = []

        def chunk_scores(h):
            r = slice(h["h"] * L3_D, (h["h"] + 1) * L3_D)
            bs, s = k.banks.take(), k.scratch.take()
            t = k.mms([(bs[:, i * P:(i + 1) * P], kk[r, i * P:(i + 1) * P], q[r, i * P:(i + 1) * P]) for i in range(TPG)],
                      after=[t_k, t_q, bs.after])
            h["read"] = t
            h["s"], h["t"] = s, k.tt(tiles(s[:, :]), tiles(bs[:, :]), four(causal), ALU.mult, after=[t, s.after])
            k.banks.put(bs, h["t"])

        def times_u(h):
            n, s = h["h"], h["s"]
            t_i.append(k.mms([(b[n * L3_D:(n + 1) * L3_D, i * P:(i + 1) * P], u[:, i * P + n * L3_D:i * P + (n + 1) * L3_D],
                               s[:, i * P:(i + 1) * P]) for i in range(TPG)], after=[t_u, h["t"], b.after]))
            k.scratch.put(s, t_i[-1])

        heads = [{"h": h} for h in range(L3_H)]
        yield from staged(heads, (0, chunk_scores), (1, times_u))
        k.scratch.put(q, [t_read, heads[-1]["read"]])
        k.scratch.put(kk, heads[-1]["read"])
        k.scratch.put(u, t_i)
        t = k.acopy(dl[:, :], o_bank[:, :], after=[t_o, dl.after])
        yield
        k.banks.put(o_bank, t)
        t_dl = k.tt(dl[:, :], dl[:, :], b[:, :], ALU.add, after=[t, t_i])
        k.banks.put(b, t_dl)
        deltas[g] = (dl, t_dl)
        yield

    def blend(g):
        dl, t_dl = deltas.pop(g)
        pt, t_pt = path_rows(g)
        yield
        o, filtered_t = filtered.pop(g)
        b = k.banks.take()
        t = k.mm([(b[:, :], path[:, 3, :], pt[0:NP, :])], after=[t_pt, b.after])
        yield
        t = k.tt(dl[:, :], dl[:, :], b[:, :], ALU.mult, after=[t, t_dl])
        k.banks.put(b, t)
        k.scratch.put(pt, t)
        t = k.tt(o[:, :], o[:, :], dl[:, :], ALU.add, after=[t, filtered_t])
        k.scratch.put(dl, t)
        t = yield from unit_rows(o, t, k.eps[:, 0:1], head_mean, norm_w)
        yield
        b, s = k.banks.take(), k.scratch.take()
        t = k.mm([(b[:, :], Wo, o[:, :])], after=[t, b.after])
        yield
        s.token = k.acopy(s[:, :], b[:, :], after=[t, s.after])
        k.scratch.put(o, t)
        k.banks.put(b, s.token)
        mixed[g] = s
        yield

    def ffn(g):
        k.T.wait(big)
        acc = k.banks.take()

        def hidden(e, f, x):
            ba, bg, s = k.banks.take(), k.banks.take(), k.scratch.take()
            t = k.mm([(ba[:, :], W1[:, e, f * P:(f + 1) * P], x)], after=ba.after)
            t_g = k.mm([(bg[:, :], W1[:, e, (L3_FF + f) * P:(L3_FF + f + 1) * P], x)], after=bg.after)
            t = k.act(s[:, :], ba[:, :], ACT.Gelu, after=[t, s.after])
            k.banks.put(ba, t)
            return {"slot": s, "t": [t, t_g], "bg": bg}

        def gated(u, gate):
            s, bg = u["slot"], u["bg"]
            t = k.tt(s[:, :], s[:, :], bg[:, :], ALU.mult, after=u["t"])
            k.banks.put(bg, t)
            return k.tt(s[:, :], s[:, :], gate[:, :], ALU.mult, after=[t, gate.token], on=k.G)

        yield from k.experts(g, done_before["rows"], acc, L3_FF, hidden, gated, lambda e, f: W2[:, e, f, :], None, after=[])
        yield from k.gate_and_add(g, acc, k.t_acc[g], mixed[g])

    recurred, passed = [], []

    def counted(part, into):
        def run(g):
            yield from part(g)
            into.append(g)
        return run

    def lane(may_start, part):
        return Lane([(lambda g=g: may_start(g), lambda g=g: part(g)) for g in range(GROUPS)])

    all_normed = lambda: all(normed(g) for g in range(GROUPS))
    yield [Lane([(all_normed, path_gates), (all_normed, expert_gates)]),
           lane(lambda g: g in deltas and g in filtered, blend),
           lane(lambda g: g in prepared, counted(recur, recurred)),
           lane(lambda g: g in fronts, invert),
           lane(lambda g: normed(g) and len(recurred) >= g - 2 and len(passed) >= g - 3 and not fronts and len(vpads.free) > 0, front),
           lane(lambda g: g in tapped and "probs" in done_before, gate_paths),
           lane(lambda g: g in values, filters_of),
           lane(lambda g: mixed[g] is not None and "rows" in done_before, counted(ffn, passed))], passed


def layouts3(a):
    g = lambda n: a["L3_attn_" + n]
    return {"L3_Wqkv": np.concatenate([g("Wq").T, g("Wk").T, g("Wv").T], axis=1), "L3_Wo": g("Wo").T, "L3_Wb": g("Wb").T,
            "L3_taps": np.concatenate([g("conv_q"), g("conv_k"), g("conv_v")] +
                                      [g("fir_" + n).reshape(P, -1) for n in "sml"] +
                                      [np.tile(g("norm_w"), L3_H).reshape(P, 1)], axis=1),
            "L3_gate_w": g("gate_w").reshape(L3_H * L3_PATHS, P).T,
            "L3_row": np.concatenate([g(n).reshape(1, -1) for n in ("gate_b", "log_temp", "eps_param")], axis=1),
            "L3_consts": l3_constants(), "L3_Wg": a["L3_ffn_Wg"], "L3_W1": a["L3_ffn_W_in"], "L3_W2": a["L3_ffn_W_out"]}


def columns(v):
    return v.reshape(-1, P).T


def layouts(a):
    d = {"x": a["L0_attn_x"].reshape(TOKENS, P).T}
    if 0 in LAYERS:
        d.update({
            "L0_W1": a["L0_ffn_W1"], "L0_W2": a["L0_ffn_W2"], "L0_b1": columns(a["L0_ffn_b1"]), "L0_b2": a["L0_ffn_b2"],
            "L0_Wr": a["L0_ffn_Wr"], "L0_br": a["L0_ffn_br"].reshape(1, EXPERTS),
            "L0_Win": a["L0_attn_W_in"].T, "L0_Wout": a["L0_attn_W_out"].T})
    if 1 in LAYERS:
        d.update(layouts1(a))
    if 2 in LAYERS:
        d.update(layouts2(a))
    if 3 in LAYERS:
        d.update(layouts3(a))
    return d


def build(nc, ins, out, layers=LAYERS):
    k = Kernel(nc, ins, out)
    k.setup()
    words = REGION_WORDS
    regions = [k.sb("weights_even", [P, words[0]]), k.sb("weights_odd", [P, words[1]])]
    free_after = []
    used = [0, 0]

    def queue_loads(n):
        m = n % 2
        own = Region(regions[m], words[m], free_after)
        if n == 3:
            spare_words, other = [Region(regions[0], words[0], free_after, at) for at in (max(used[0], L3_PE_TAPS * P), 0)]
            steps = layer3(k, own, spare_words, other)
        else:
            steps = (layer0, layer1, layer2)[n](k, own)
        next(steps)
        used[m] = own.at
        return steps

    k.layers = len(layers)
    queued = [queue_loads(n) for n in layers[:2]]
    lanes, passed, k.started = [k.first_layernorm()], [[0] * GROUPS], 0
    while k.started < len(layers) or not all(lane.over() for lane in sum(lanes, [])):
        beside = 1 if k.started < len(layers) and layers[k.started] != 3 else 0
        if k.started < len(queued) and len(passed[-1]) >= GROUPS - beside:
            k.started += 1
            own, through = next(queued[k.started - 1])
            lanes.append(own)
            passed.append(through)
            continue
        over = sum(all(lane.over() for lane in own) for own in lanes[1:])
        if len(queued) < min(over + 2, len(layers)):
            free_after = list(k.x_ready)
            queued.append(queue_loads(layers[len(queued)]))
        step_lanes(k, [lane for own in lanes for lane in own if not lane.over()],
                   lanes[-1] if over < k.started - 1 else [])
    k.finish()


def kernel(**inputs):
    import concourse.bacc as bacc
    from concourse.bass_utils import run_bass_kernel_spmd

    arrays = {name: np.ascontiguousarray(a) for name, a in layouts({n: np.asarray(a) for n, a in inputs.items()}).items()}
    nc = bacc.Bacc("TRN2", target_bir_lowering=False, num_devices=1)
    ins = {name: nc.dram_tensor(f"in_{name}", a.shape, mybir.dt.from_np(a.dtype), kind="ExternalInput").ap()
           for name, a in arrays.items()}
    out = nc.dram_tensor("out_x", (P, TOKENS), F32, kind="ExternalOutput").ap()
    build(nc, ins, out)
    r = run_bass_kernel_spmd(nc, [{f"in_{name}": a for name, a in arrays.items()}], core_ids=[0])
    return np.ascontiguousarray(r.results[0]["out_x"].T).reshape(BATCH, SEQ, P)
```
